# Optimizing a Trainium2 kernel written in Bass

```python
import numpy as np
import jax
import jax.numpy as jnp

def _softmax(x, axis=-1):
    return jax.nn.softmax(x, axis=axis)

def _gelu(x):
    return jax.nn.gelu(x, approximate=True)

def _silu(x):
    return jax.nn.silu(x)

def _sigmoid(x):
    return jax.nn.sigmoid(x)

def _layernorm(x, axis=-1, eps=1e-05):
    m = jnp.mean(x, axis=axis, keepdims=True)
    v = jnp.var(x, axis=axis, keepdims=True)
    return (x - m) / jnp.sqrt(v + eps)

def _scatter_add(tgt, idx, src, axis=0):
    return tgt.at[idx].add(src)

def _segment_sum(src, seg, n):
    return jax.ops.segment_sum(src, seg, n)
kernel_name = 'mk_recurrent_d2_jaxref_r8_6437e5'

def setup_inputs(seed: int=0):
    np.random.seed(seed)
    _w = jnp.asarray

    def _L0_attn_setup():
        import math
        import jax, jax.numpy as jnp
        import numpy as np
        HID = 256
        H = 16
        HKV = 8
        D = HID // H
        F = D
        SEQ = 256
        BATCH = 2
        THETA = 10000.0

        def _rotate_half(x):
            x1, x2 = (x[..., :x.shape[-1] // 2], x[..., x.shape[-1] // 2:])
            return jnp.concatenate((-x2, x1), axis=-1)

        def _softmax_kernel(x, R):
            n = jnp.sqrt(jnp.sum(x * x, axis=-1, keepdims=True))
            x = x / jnp.maximum(n, 1e-06)
            p = jnp.einsum('...d,ed->...e', x, R)
            feats = jnp.concatenate([jnp.sin(p), jnp.cos(p)], axis=-1)
            return feats / math.sqrt(F)
        key = jax.random.key(seed)
        ks = jax.random.split(key, 10)
        s = lambda k, shape, scale=0.02: jax.random.normal(k, shape, dtype=jnp.float32) * scale
        return {'hidden_states': jax.random.normal(ks[0], (BATCH, SEQ, HID), dtype=jnp.float32), 'Wq': s(ks[1], (HID, HID)), 'bq': s(ks[2], (HID,)), 'Wk': s(ks[3], (HKV * D, HID)), 'bk': s(ks[4], (HKV * D,)), 'Wv': s(ks[5], (HKV * D, HID)), 'bv': s(ks[6], (HKV * D,)), 'Wo': s(ks[7], (HID, HID)), 'bo': s(ks[8], (HID,)), 'rand_matrix': jax.random.normal(ks[9], (F // 2, D), dtype=jnp.float32)}
    _L0_attn_in = _L0_attn_setup()

    def _L0_ffn_setup():
        import jax, jax.numpy as jnp
        import numpy as np
        from functools import partial
        SEQ, BATCH, HIDDEN = (256, 4, 256)
        FFN = 176
        N_EXPERTS = 8
        TOP_K = 2
        EPS = 1e-20
        key = jax.random.key(seed)
        k0, k1, k2, k3 = jax.random.split(key, 4)
        x = jax.random.normal(k0, (SEQ, BATCH, HIDDEN), dtype=jnp.float32)
        wg = jax.random.normal(k1, (N_EXPERTS, HIDDEN), dtype=jnp.float32) * 0.02
        w1 = jax.random.normal(k2, (N_EXPERTS, HIDDEN, 2 * FFN), dtype=jnp.float32) * 0.02
        w2 = jax.random.normal(k3, (N_EXPERTS, FFN, HIDDEN), dtype=jnp.float32) * 0.02
        return {'x': x, 'wg': wg, 'w1': w1, 'w2': w2}
    _L0_ffn_in = _L0_ffn_setup()

    def _L1_attn_setup():
        import jax, jax.numpy as jnp
        import numpy as np
        N_HEADS = 16
        key = jax.random.key(seed)
        ks = jax.random.split(key, 9)
        B, S, D = (2, 256, 256)
        s = 0.02
        return {'X': jax.random.normal(ks[0], (B, S, D), jnp.float32), 'Wq': jax.random.normal(ks[1], (D, D), jnp.float32) * s, 'bq': jax.random.normal(ks[2], (D,), jnp.float32) * s, 'Wk': jax.random.normal(ks[3], (D, D), jnp.float32) * s, 'bk': jax.random.normal(ks[4], (D,), jnp.float32) * s, 'Wv': jax.random.normal(ks[5], (D, D), jnp.float32) * s, 'bv': jax.random.normal(ks[6], (D,), jnp.float32) * s, 'Wo': jax.random.normal(ks[7], (D, D), jnp.float32) * s, 'bo': jax.random.normal(ks[8], (D,), jnp.float32) * s}
    _L1_attn_in = _L1_attn_setup()

    def _L1_ffn_setup():
        import jax, jax.numpy as jnp
        import numpy as np
        B, S, H = (4, 128, 256)
        E, K, I, SI = (16, 4, 176, 704)

        def _silu_mul(gu, inter):
            return jax.nn.silu(gu[:, :inter]) * gu[:, inter:]
        key = jax.random.key(seed)
        ks = jax.random.split(key, 7)
        s = 0.02
        return {'hidden_states': jax.random.normal(ks[0], (B, S, H), jnp.float32), 'gate_w': jax.random.normal(ks[1], (E, H), jnp.float32) * s, 'expert_gate_up': jax.random.normal(ks[2], (E, 2 * I, H), jnp.float32) * s, 'expert_down': jax.random.normal(ks[3], (E, H, I), jnp.float32) * s, 'shared_gate_up': jax.random.normal(ks[4], (2 * SI, H), jnp.float32) * s, 'shared_down': jax.random.normal(ks[5], (H, SI), jnp.float32) * s, 'shared_gate_vec': jax.random.normal(ks[6], (1, H), jnp.float32) * s}
    _L1_ffn_in = _L1_ffn_setup()
    _d = {'L0_attn_hidden_states': _L0_attn_in['hidden_states'], 'L0_attn_Wq': _L0_attn_in['Wq'], 'L0_attn_bq': _L0_attn_in['bq'], 'L0_attn_Wk': _L0_attn_in['Wk'], 'L0_attn_bk': _L0_attn_in['bk'], 'L0_attn_Wv': _L0_attn_in['Wv'], 'L0_attn_bv': _L0_attn_in['bv'], 'L0_attn_Wo': _L0_attn_in['Wo'], 'L0_attn_bo': _L0_attn_in['bo'], 'L0_attn_rand_matrix': _L0_attn_in['rand_matrix'], 'L0_ffn_wg': _L0_ffn_in['wg'], 'L0_ffn_w1': _L0_ffn_in['w1'], 'L0_ffn_w2': _L0_ffn_in['w2'], 'L1_attn_Wq': _L1_attn_in['Wq'], 'L1_attn_bq': _L1_attn_in['bq'], 'L1_attn_Wk': _L1_attn_in['Wk'], 'L1_attn_bk': _L1_attn_in['bk'], 'L1_attn_Wv': _L1_attn_in['Wv'], 'L1_attn_bv': _L1_attn_in['bv'], 'L1_attn_Wo': _L1_attn_in['Wo'], 'L1_attn_bo': _L1_attn_in['bo'], 'L1_ffn_gate_w': _L1_ffn_in['gate_w'], 'L1_ffn_expert_gate_up': _L1_ffn_in['expert_gate_up'], 'L1_ffn_expert_down': _L1_ffn_in['expert_down'], 'L1_ffn_shared_gate_up': _L1_ffn_in['shared_gate_up'], 'L1_ffn_shared_down': _L1_ffn_in['shared_down'], 'L1_ffn_shared_gate_vec': _L1_ffn_in['shared_gate_vec']}
    _x0 = _d['L0_attn_hidden_states']
    _d['L0_attn_hidden_states'] = jax.random.normal(jax.random.fold_in(jax.random.key(seed), 1), (4, 1024, 256), dtype=_x0.dtype)
    del _x0
    return _d

def reference(L0_attn_hidden_states, L0_attn_Wq, L0_attn_bq, L0_attn_Wk, L0_attn_bk, L0_attn_Wv, L0_attn_bv, L0_attn_Wo, L0_attn_bo, L0_attn_rand_matrix, L0_ffn_wg, L0_ffn_w1, L0_ffn_w2, L1_attn_Wq, L1_attn_bq, L1_attn_Wk, L1_attn_bk, L1_attn_Wv, L1_attn_bv, L1_attn_Wo, L1_attn_bo, L1_ffn_gate_w, L1_ffn_expert_gate_up, L1_ffn_expert_down, L1_ffn_shared_gate_up, L1_ffn_shared_down, L1_ffn_shared_gate_vec):

    def _L0_attn_ref(hidden_states, Wq, bq, Wk, bk, Wv, bv, Wo, bo, rand_matrix):
        import math
        import jax, jax.numpy as jnp
        import numpy as np
        HID = 256
        H = 16
        HKV = 8
        D = HID // H
        F = D
        SEQ = 256
        BATCH = 2
        THETA = 10000.0

        def _rotate_half(x):
            x1, x2 = (x[..., :x.shape[-1] // 2], x[..., x.shape[-1] // 2:])
            return jnp.concatenate((-x2, x1), axis=-1)

        def _softmax_kernel(x, R):
            n = jnp.sqrt(jnp.sum(x * x, axis=-1, keepdims=True))
            x = x / jnp.maximum(n, 1e-06)
            p = jnp.einsum('...d,ed->...e', x, R)
            feats = jnp.concatenate([jnp.sin(p), jnp.cos(p)], axis=-1)
            return feats / math.sqrt(F)
        b, s, _ = hidden_states.shape
        q = (hidden_states @ Wq.T + bq).reshape(b, s, H, D).transpose(0, 2, 1, 3)
        k = (hidden_states @ Wk.T + bk).reshape(b, s, HKV, D).transpose(0, 2, 1, 3)
        v = (hidden_states @ Wv.T + bv).reshape(b, s, HKV, D).transpose(0, 2, 1, 3)
        inv_freq = 1.0 / THETA ** (jnp.arange(0, D, 2, dtype=jnp.float32) / D)
        freqs = jnp.arange(s, dtype=jnp.float32)[:, None] * inv_freq[None, :]
        emb = jnp.concatenate((freqs, freqs), axis=-1)
        cos = jnp.cos(emb)[None, None, :, :]
        sin = jnp.sin(emb)[None, None, :, :]
        q = q * cos + _rotate_half(q) * sin
        k = k * cos + _rotate_half(k) * sin
        rep = H // HKV
        k = jnp.repeat(k, rep, axis=1)
        v = jnp.repeat(v, rep, axis=1)
        qp = _softmax_kernel(q, rand_matrix)
        kp = _softmax_kernel(k, rand_matrix)
        kv = jnp.einsum('bhsf,bhsd->bsfd', kp, v)
        out = jnp.einsum('bhsf,bsfd->bhsd', qp, kv)
        out = out.reshape(b, s, HID)
        return out @ Wo.T + bo

    def _L0_ffn_ref(x, wg, w1, w2):
        import jax, jax.numpy as jnp
        import numpy as np
        from functools import partial
        SEQ, BATCH, HIDDEN = (256, 4, 256)
        FFN = 176
        N_EXPERTS = 8
        TOP_K = 2
        EPS = 1e-20
        S, B, H = x.shape
        T = B * S
        xt = jnp.transpose(x, (1, 0, 2)).reshape(T, H)
        logits = xt @ wg.T
        scores = jax.nn.softmax(logits, axis=-1)
        topk_w, topk_i = jax.lax.top_k(scores, TOP_K)
        topk_w = topk_w / (jnp.sum(topk_w, axis=-1, keepdims=True) + EPS)
        C = jnp.zeros((T, N_EXPERTS), dtype=xt.dtype)
        C = C.at[jnp.arange(T)[:, None], topk_i].add(topk_w)

        def step(acc, inputs):
            w1e, w2e, ce = inputs
            h = xt @ w1e
            a, b = jnp.split(h, 2, axis=-1)
            y = jax.nn.silu(a) * b @ w2e
            return (acc + ce[:, None] * y, None)
        out0 = jnp.zeros((T, H), dtype=xt.dtype)
        out, _ = jax.lax.scan(step, out0, (w1, w2, C.T))
        return jnp.transpose(out.reshape(B, S, H), (1, 0, 2))

    def _L1_attn_ref(X, Wq, bq, Wk, bk, Wv, bv, Wo, bo):
        import jax, jax.numpy as jnp
        import numpy as np
        N_HEADS = 16
        B, S, D = X.shape
        H = N_HEADS
        d_head = D // H
        scale = jnp.asarray(1.0 / np.sqrt(np.sqrt(d_head)), X.dtype)
        Q = (X @ Wq.T + bq).reshape(B, S, H, d_head) * scale
        K = (X @ Wk.T + bk).reshape(B, S, H, d_head) * scale
        V = (X @ Wv.T + bv).reshape(B, S, H, d_head)
        scores = jnp.einsum('bqhd,bkhd->bhqk', Q, K)
        causal = jnp.tril(jnp.ones((S, S), bool))
        scores = jnp.where(causal[None, None], scores, -jnp.inf)
        attn = jax.nn.softmax(scores.astype(jnp.float32), axis=-1).astype(X.dtype)
        out = jnp.einsum('bhqk,bkhd->bqhd', attn, V).reshape(B, S, D)
        return out @ Wo.T + bo

    def _L1_ffn_ref(hidden_states, gate_w, expert_gate_up, expert_down, shared_gate_up, shared_down, shared_gate_vec):
        import jax, jax.numpy as jnp
        import numpy as np
        B, S, H = (4, 128, 256)
        E, K, I, SI = (16, 4, 176, 704)

        def _silu_mul(gu, inter):
            return jax.nn.silu(gu[:, :inter]) * gu[:, inter:]
        orig_shape = hidden_states.shape
        x = hidden_states.reshape(-1, H)
        router_logits = x @ gate_w.T
        routing_probs = jax.nn.softmax(router_logits.astype(jnp.float32), axis=-1)
        topk_w, topk_idx = jax.lax.top_k(routing_probs, K)
        topk_w = topk_w / topk_w.sum(axis=-1, keepdims=True)
        topk_w = topk_w.astype(x.dtype)
        combine = (jax.nn.one_hot(topk_idx, E, dtype=x.dtype) * topk_w[..., None]).sum(1)
        shared = _silu_mul(x @ shared_gate_up.T, SI) @ shared_down.T
        shared = shared * jax.nn.sigmoid(x @ shared_gate_vec.T)

        def step(acc, ew):
            w_gu, w_d, cw = ew
            h = _silu_mul(x @ w_gu.T, I)
            return (acc + h @ w_d.T * cw[:, None], None)
        acc0 = jnp.zeros_like(x)
        sparse, _ = jax.lax.scan(step, acc0, (expert_gate_up, expert_down, combine.T))
        return (shared + sparse).reshape(orig_shape)
    x = L0_attn_hidden_states
    xn = _layernorm(x, axis=-1)
    s = _L0_attn_ref(xn, L0_attn_Wq, L0_attn_bq, L0_attn_Wk, L0_attn_bk, L0_attn_Wv, L0_attn_bv, L0_attn_Wo, L0_attn_bo, L0_attn_rand_matrix)
    g = _silu(_L0_ffn_ref(xn, L0_ffn_wg, L0_ffn_w1, L0_ffn_w2))
    x = x + s * g
    xn = _layernorm(x, axis=-1)
    s = _L1_attn_ref(xn, L1_attn_Wq, L1_attn_bq, L1_attn_Wk, L1_attn_bk, L1_attn_Wv, L1_attn_bv, L1_attn_Wo, L1_attn_bo)
    g = _silu(_L1_ffn_ref(xn, L1_ffn_gate_w, L1_ffn_expert_gate_up, L1_ffn_expert_down, L1_ffn_shared_gate_up, L1_ffn_shared_down, L1_ffn_shared_gate_vec))
    x = x + s * g
    return x

_drawn_inputs = setup_inputs


def setup_inputs(seed=0):
    import zlib

    import numpy as np

    out = dict(_drawn_inputs(seed))
    spreads = {}
    factors = {'L0_attn_Wq': 8.0,
     'L0_attn_bq': 8.0,
     'L0_attn_Wk': 8.0,
     'L0_attn_bk': 8.0,
     'L0_attn_Wv': 8.0,
     'L0_attn_bv': 8.0,
     'L0_attn_Wo': 8.0,
     'L0_attn_bo': 8.0,
     'L0_attn_rand_matrix': 8.0,
     'L0_ffn_wg': 8.0,
     'L0_ffn_w1': 8.0,
     'L0_ffn_w2': 8.0,
     'L1_attn_Wq': 8.0,
     'L1_attn_bq': 8.0,
     'L1_attn_Wk': 8.0,
     'L1_attn_Wv': 8.0,
     'L1_attn_bv': 8.0,
     'L1_attn_Wo': 8.0,
     'L1_attn_bo': 8.0,
     'L1_ffn_gate_w': 8.0,
     'L1_ffn_expert_gate_up': 8.0,
     'L1_ffn_expert_down': 8.0,
     'L1_ffn_shared_gate_up': 8.0,
     'L1_ffn_shared_down': 8.0,
     'L1_ffn_shared_gate_vec': 8.0}
    for name, (base, spread) in spreads.items():
        noise = np.random.default_rng([zlib.crc32(name.encode()), seed]).standard_normal(out[name].shape)
        drawn = base * np.exp(spread * noise) if base else spread * noise
        out[name] = jnp.asarray(drawn.astype(out[name].dtype))
    for name, factor in factors.items():
        out[name] = (out[name] * factor).astype(out[name].dtype)
    return out
```

```python
from contextlib import ExitStack

import concourse.bass as bass
from concourse import mybir

F32 = mybir.dt.float32
F32R = mybir.dt.float32r
BF16 = mybir.dt.bfloat16
ALU = mybir.AluOpType
ACT = mybir.ActivationFunctionType
AX = mybir.AxisListType

P = 128
BATCH, SEQ, HID = 4, 1024, 256
TOKENS = BATCH * SEQ
TILES = TOKENS // P
KT = HID // P
CHUNK = 512
CHUNKS = TOKENS // CHUNK
TPC = CHUNK // P
HEADS, D = 16, 16
KV_HEADS = 8
QK_HEADS = HEADS + KV_HEADS
SHARE = (HEADS // KV_HEADS) / D
RF = D // 2
POS_TILES = SEQ // P
EPS = 1e-5
NEG = -1e30
ROUND = 1.5 * 2.0 ** 23
TWO_PI = 6.283185005187988
MID = 176
E0, TOP0 = 8, 2
E1, TOP1 = 16, 4
RW1 = E1 + 2
SHARED = 704
NT0 = E0 * MID // P
NT1 = -(-(E1 * MID + SHARED) // P)
G0, G1 = 11, 7
WT = 2 * KT * P + HID
WTS = WT + P
GH = 4
GROUPS = HEADS // GH
AW = 3 * KT * P
SPAN = SEQ // CHUNK


def new_semaphore(nc, ctx, name):
    handle = ctx.enter_context(nc.semaphore(name))
    ctx.callback(lambda: nc.gpsimd.sem_clear(handle))
    return handle


class Steps:

    def __init__(self, eng, sem):
        self.eng, self.sem, self.n, self.base = eng, sem, 0, 0

    def link(self, ins):
        self.n += 1
        ins.then_inc(self.sem, 1)
        self.eng.wait_ge(self.sem, self.base + self.n)


def three_passes(pe, out, w_hi, w_lo, x_hi, x_lo, kt, first=True, last=True, check=False):
    n = 0
    for k in range(kt):
        for w, x in ((w_hi, x_hi), (w_hi, x_lo), (w_lo, x_hi)):
            ins = pe.matmul(out, w(k), x(k), start=first and n == 0, stop=last and n == 3 * kt - 1,
                            skip_group_check=check)
            n += 1
    return ins


def standardise(nc, x_sb, mean_rstd, load, tag):
    LOADS = TILES // 4
    with ExitStack() as ctx:
        ctx.callback(nc.all_engine_barrier)
        def sem(name):
            return new_semaphore(nc, ctx, f"{tag}_{name}")
        stats = ctx.enter_context(nc.sbuf_tensor(f"{tag}_stats", [P, 2, 6], F32))
        x_in = [sem(f"x_in{c}") for c in range(LOADS)]
        stats_step, aggr_step = sem("stats_step"), sem("aggr_step")
        stats_done, root_done, mr_done = sem("stats_done"), sem("root_done"), sem("mr_done")
        block = ctx.enter_context(nc.Block())

        @block.sync
        def _(sp):
            for c in range(LOADS):
                load(sp, c).then_inc(x_in[c], 16)

        @block.vector
        def _(dve):
            for t in range(TILES):
                dve.wait_ge(x_in[t // 4], 16)
                dve.bn_stats(stats[:, t % 2, :], x_sb[:, t, :]).then_inc(stats_step, 1)
                dve.wait_ge(stats_step, t + 1)
                dve.bn_aggr(mean_rstd[:, t, :], stats[:, t % 2, :]).then_inc(aggr_step, 1)
            dve.wait_ge(aggr_step, TILES)
            ins = dve.tensor_scalar(mean_rstd[:, :, 1], mean_rstd[:, :, 1], EPS, None, ALU.add)
            ins.then_inc(stats_done, 1)
            dve.wait_ge(root_done, 1)
            dve.reciprocal(mean_rstd[:, :, 1], mean_rstd[:, :, 1]).then_inc(mr_done, 1)
            dve.wait_ge(mr_done, 1)

        @block.scalar
        def _(act):
            act.wait_ge(stats_done, 1)
            act.activation(mean_rstd[:, :, 1], mean_rstd[:, :, 1], ACT.Sqrt).then_inc(root_done, 1)


def split_weights(nc, tag, pairs, loads):
    with ExitStack() as ctx:
        ctx.callback(nc.all_engine_barrier)
        w_in = new_semaphore(nc, ctx, f"{tag}_w_in")
        hi_done = new_semaphore(nc, ctx, f"{tag}_hi_done")
        lo_done = new_semaphore(nc, ctx, f"{tag}_lo_done")
        block = ctx.enter_context(nc.Block())

        @block.sync
        def _(sp):
            for dst, src in loads:
                sp.dma_start(dst, src).then_inc(w_in, 16)

        @block.vector
        def _(dve):
            dve.wait_ge(w_in, 16 * len(loads))
            for raw, hi, lo in pairs:
                dve.tensor_copy(hi, raw).then_inc(hi_done, 1)
            for n, (raw, hi, lo) in enumerate(pairs):
                dve.wait_ge(hi_done, n + 1)
                dve.tensor_tensor(lo, raw, hi.bitcast(F32), ALU.subtract).then_inc(lo_done, 1)
            if pairs:
                dve.wait_ge(lo_done, len(pairs))


def normalise_and_transpose(nc, tag, x_sb, mean_rstd, XT_hi, XT_lo, logits, wr_hi, wr_lo, NE, ident,
                            extra=None):
    with ExitStack() as ctx:
        ctx.callback(nc.all_engine_barrier)
        def sem(name):
            return new_semaphore(nc, ctx, f"{tag}_{name}")

        def sb(name, shape, dt=F32):
            return ctx.enter_context(nc.sbuf_tensor(f"{tag}_{name}", shape, dt))

        def ps(name, shape):
            return [ctx.enter_context(nc.psum_tensor(f"{tag}_{name}{i}", shape, F32)) for i in range(2)]
        xn = sb("xn", [P, 2, HID])
        st_hi, st_lo = sb("st_hi", [P, 2, HID], F32R), sb("st_lo", [P, 2, HID], F32R)
        psT, psL = ps("psT", [P, HID]), ps("psL", [P, CHUNK])
        xn_done, xT_done, hi_done, lo_done = (sem(x) for x in ("xn_done", "xT_done", "hi_done", "lo_done"))
        stored = [sem("stored0"), sem("stored1")]
        logits_done, logits_out = sem("logits_done"), sem("logits_out")
        if extra:
            e = extra
            psQ, psR = ps("psQ", [P, 512]), ps("psR", [P, QK_HEADS * D])
            qk = sb("qk", [P, 2, QK_HEADS * D])
            rot_a, rot_b, rot = (sb(x, [P, 2, QK_HEADS * D]) for x in ("rot_a", "rot_b", "rot"))
            sq = sb("sq", [P, 2, QK_HEADS * D])
            rotT = sb("rotT", [P, 2, QK_HEADS * D])
            n2 = sb("n2", [P, 2, QK_HEADS])
            qkv_done, qk_out, v_out, rot_parts, rot_done = (sem(x) for x in ("qkv_done", "qk_out", "v_out", "rot_parts", "rot_done"))
            sq_done, n2_done, n2_out, rotT_done, rotT_out, p_done, p_out = (
                sem(x) for x in ("sq_done", "n2_done", "n2_out", "rotT_done", "rotT_out", "p_done", "p_out"))
        block = ctx.enter_context(nc.Block())

        def tiles(front, back):
            def loop(eng):
                front(0, 0)
                front(1, 1)
                back(0, 0)
                front(2, 0)
                back(1, 1)
                with eng.Fori(1, TILES // 2 - 1) as i:
                    front(i * 2 + 1, 1)
                    back(i * 2, 0)
                    front(i * 2 + 2, 0)
                    back(i * 2 + 1, 1)
                front(TILES - 1, 1)
                back(TILES - 2, 0)
                back(TILES - 1, 1)
            return loop

        def nothing(t, b):
            pass

        @block.sync
        def _(sp):
            def store(t, b):
                t0 = sp.snap(t * P) if not isinstance(t, int) else t * P
                sp.wait_ge(lo_done, t + 1)
                for st, XT in ((st_hi, XT_hi), (st_lo, XT_lo)):
                    sp.dma_start(XT[:, :, bass.ds(t0, P)].bitcast(F32),
                                 st[:, b, :].rearrange("p (k n) -> p k n", k=KT).bitcast(F32)).then_inc(stored[b], 16)
            tiles(nothing, store)(sp)
            for b in range(2):
                sp.wait_ge(stored[b], 16 * TILES)

        @block.vector
        def _(dve):
            def front(t, b):
                if isinstance(t, int) and t < 2:
                    pass
                else:
                    dve.wait_ge(xT_done, t - 1)
                dve.tensor_scalar(xn[:, b, :], x_sb[:, bass.ds(t, 1), :].rearrange("p a n -> p (a n)"),
                                  mean_rstd[:, bass.ds(t, 1), 0], mean_rstd[:, bass.ds(t, 1), 1],
                                  ALU.subtract, ALU.mult).then_inc(xn_done, 1)
                dve.wait_ge(hi_done, t + 1)
                dve.tensor_tensor(st_lo[:, b, :], psT[b][:], st_hi[:, b, :].bitcast(F32), ALU.subtract)\
                   .then_inc(lo_done, 1)

            def back(t, b):
                if not extra:
                    return
                dve.wait_ge(qkv_done, t + 1)
                if not (isinstance(t, int) and t < 2):
                    dve.wait_ge(rot_done, t - 1)
                nq = QK_HEADS * D
                dve.tensor_tensor(qk[:, b, :], psQ[b][:, 0:nq], e["bias"][:, 0:nq], ALU.add).then_inc(qk_out, 1)
                dve.tensor_tensor(e["v"][:, bass.ds(t, 1), :].rearrange("p a n -> p (a n)"), psQ[b][:, nq:512],
                                  e["bias"][:, nq:512], ALU.add).then_inc(v_out, 1)
                dve.wait_ge(rot_done, t + 1)
                dve.tensor_tensor(sq[:, b, :], rot[:, b, :], rot[:, b, :], ALU.mult).then_inc(sq_done, 1)
                dve.wait_ge(sq_done, t + 1)
                dve.tensor_reduce(n2[:, b, :], sq[:, b, :].rearrange("p (h d) -> p h d", d=D), AX.X, ALU.add)\
                   .then_inc(n2_done, 1)
                dve.wait_ge(n2_done, t + 1)
                dve.tensor_copy(e["n2"][:, bass.ds(t, 1), :].rearrange("p a n -> p (a n)"), n2[:, b, :])\
                   .then_inc(n2_out, 1)
            tiles(front, back)(dve)
            if extra:
                dve.wait_ge(v_out, TILES)
                dve.wait_ge(n2_out, TILES)

        @block.scalar
        def _(act):
            def front(t, b):
                act.wait_ge(xT_done, t + 1)
                if not (isinstance(t, int) and t < 2):
                    act.wait_ge(stored[b], (t - b) * 16)
                act.activation(st_hi[:, b, :], psT[b][:], ACT.Copy).then_inc(hi_done, 1)
                act.wait_ge(logits_done, t + 1)
                act.activation(logits[:, bass.ds(t, 1), :].rearrange("p a n -> p (a n)"), psL[b][:, 0:NE], ACT.Copy)\
                   .then_inc(logits_out, 1)

            def back(t, b):
                if not extra:
                    return
                act.wait_ge(rotT_done, t + 1)
                act.activation(rotT[:, b, :], psR[b][:], ACT.Copy).then_inc(rotT_out, 1)
                act.wait_ge(p_done, t + 1)
                act.activation(e["proj"][:, bass.ds(t, 1), :].rearrange("p a n -> p (a n)"),
                               psL[b][:, 64:64 + QK_HEADS * RF], ACT.Copy).then_inc(p_out, 1)
            tiles(front, back)(act)

        if extra:
            @block.gpsimd
            def _(pool):
                def rotate(t, b, pos):
                    pool.wait_ge(qk_out, t + 1)
                    if not (isinstance(t, int) and t < 2):
                        pool.wait_ge(rotT_done, t - 1)
                        pool.wait_ge(sq_done, t - 1)
                    cos = e["cos"][:, pos, :].unsqueeze(1).broadcast_to([P, QK_HEADS, D])
                    q3 = qk[:, b, :].rearrange("p (h d) -> p h d", d=D)
                    a3 = rot_a[:, b, :].rearrange("p (h d) -> p h d", d=D)
                    b3 = rot_b[:, b, :].rearrange("p (h d) -> p h d", d=D)
                    pool.tensor_tensor(a3, q3, cos, ALU.mult).then_inc(rot_parts, 1)
                    for half in range(2):
                        sin = e["sin"][:, pos, half * RF:half * RF + RF].unsqueeze(1).broadcast_to([P, QK_HEADS, RF])
                        other = (1 - half) * RF
                        pool.tensor_tensor(b3[:, :, half * RF:half * RF + RF], q3[:, :, other:other + RF], sin, ALU.mult)\
                            .then_inc(rot_parts, 1)
                    pool.wait_ge(rot_parts, t * 3 + 3)
                    pool.tensor_tensor(rot[:, b, :], rot_a[:, b, :], rot_b[:, b, :], ALU.add).then_inc(rot_done, 1)
                for pos in range(POS_TILES):
                    rotate(pos, pos % 2, pos)
                with pool.Fori(1, BATCH) as i:
                    for pos in range(POS_TILES):
                        rotate(i * POS_TILES + pos, pos % 2, pos)

        @block.tensor
        def _(pe):
            def front(t, b):
                pe.wait_ge(xn_done, t + 1)
                if not (isinstance(t, int) and t < 2):
                    pe.wait_ge(lo_done, t - 1)
                for k in range(KT):
                    ins = pe.transpose(psT[b][:, k * P:(k + 1) * P], xn[:, b, k * P:(k + 1) * P], ident[:])
                ins.then_inc(xT_done, 1)
                pe.wait_ge(lo_done, t + 1)
                x_hi = lambda k: st_hi[:, b, k * P:(k + 1) * P]
                x_lo = lambda k: st_lo[:, b, k * P:(k + 1) * P]
                if not (isinstance(t, int) and t < 2):
                    pe.wait_ge(p_out if extra else logits_out, t - 1)
                three_passes(pe, psL[b][:, 0:NE], x_hi, x_lo, lambda k: wr_hi[:, k, :], lambda k: wr_lo[:, k, :], KT)\
                    .then_inc(logits_done, 1)
                if extra:
                    if not (isinstance(t, int) and t < 2):
                        pe.wait_ge(v_out, t - 1)
                    three_passes(pe, psQ[b][:], x_hi, x_lo, lambda k: e["w_hi"][:, k, :], lambda k: e["w_lo"][:, k, :], KT)\
                        .then_inc(qkv_done, 1)

            def back(t, b):
                if not extra:
                    return
                pe.wait_ge(rot_done, t + 1)
                for k in range(3):
                    ins = pe.transpose(psR[b][:, k * P:(k + 1) * P], rot[:, b, k * P:(k + 1) * P], ident[:])
                ins.then_inc(rotT_done, 1)
                pe.wait_ge(rotT_out, t + 1)
                pe.wait_ge(logits_out, t + 1)
                for k in range(3):
                    ins = pe.matmul(psL[b][:, 64 + k * 64:128 + k * 64], rotT[:, b, k * P:(k + 1) * P], e["rblk"][:],
                                    start=k == 0, stop=True, skip_group_check=True)
                ins.then_inc(p_done, 1)
            tiles(front, back)(pe)


def linear_attention(nc, e, o_dram):
    NQ = HEADS * D
    with ExitStack() as ctx:
        ctx.callback(nc.all_engine_barrier)
        def sem(name):
            return new_semaphore(nc, ctx, f"la_{name}")

        def sb(name, shape, dt=F32):
            return ctx.enter_context(nc.sbuf_tensor(f"la_{name}", shape, dt))
        arg, whole, feat = (sb(x, [P, 2, QK_HEADS, D]) for x in ("arg", "whole", "feat"))
        qk_prod = sb("qk_prod", [P, 2, HEADS * KV_HEADS * D])
        av_prod = sb("av_prod", [P, HEADS * D * KV_HEADS])
        A = sb("A", [P, HEADS, KV_HEADS])
        out = sb("out", [P, 2, NQ])
        (steps, root_done, arg_done, feat_done, prod_done, A_done, av_done, out_done) = (
            sem(x) for x in ("steps", "root_done", "arg_done", "feat_done", "prod_done", "A_done", "av_done", "out_done"))
        stored = [sem("stored0"), sem("stored1")]
        block = ctx.enter_context(nc.Block())
        inv = e["n2"]

        def tiles(front, back):
            def loop(eng):
                front(0, 0)
                front(1, 1)
                back(0, 0)
                front(2, 0)
                back(1, 1)
                with eng.Fori(1, TILES // 2 - 1) as i:
                    front(i * 2 + 1, 1)
                    back(i * 2, 0)
                    front(i * 2 + 2, 0)
                    back(i * 2 + 1, 1)
                front(TILES - 1, 1)
                back(TILES - 2, 0)
                back(TILES - 1, 1)
            return loop

        def nothing(t, b):
            pass

        def late(t):
            return not (isinstance(t, int) and t < 2)

        @block.scalar
        def _(act):
            act.activation(inv[:, :, :], inv[:, :, :], ACT.Sqrt).then_inc(root_done, 1)

            def front(t, b):
                act.wait_ge(arg_done, t + 1)
                if late(t):
                    act.wait_ge(prod_done, t - 1)
                act.activation(feat[:, b, :, :], arg[:, b, :, :], ACT.Sin, scale=TWO_PI).then_inc(feat_done, 1)
            tiles(front, nothing)(act)

        @block.gpsimd
        def _(pool):
            def front(t, b):
                pool.wait_ge(feat_done, t + 1)
                if late(t):
                    pool.wait_ge(A_done, t - 1)
                q4 = feat[:, b, 0:HEADS, :].unsqueeze(2).broadcast_to([P, HEADS, KV_HEADS, D])
                k4 = feat[:, b, HEADS:QK_HEADS, :].unsqueeze(1).broadcast_to([P, HEADS, KV_HEADS, D])
                pool.tensor_tensor(qk_prod[:, b, :].rearrange("p (h g d) -> p h g d", g=KV_HEADS, d=D), q4, k4, ALU.mult)\
                    .then_inc(prod_done, 1)
            tiles(front, nothing)(pool)

        @block.vector
        def _(dve):
            s = Steps(dve, steps)
            dve.wait_ge(root_done, 1)
            s.link(dve.tensor_scalar(inv[:, :, :], inv[:, :, :], 1e-6, None, ALU.max))
            s.link(dve.reciprocal(inv[:, :, :], inv[:, :, :]))
            s.link(dve.tensor_scalar(inv[:, :, :], inv[:, :, :], 0.15915494309189535, None, ALU.mult))
            done = 3
            per_front = 3

            def front(t, b):
                s.base, s.n = done + t * per_front, 0
                if late(t):
                    dve.wait_ge(feat_done, t - 1)
                p3 = e["proj"][:, bass.ds(t, 1), :].rearrange("p a (h f) -> p (a h) f", f=RF)
                i3 = inv[:, bass.ds(t, 1), :].rearrange("p a h -> p (a h)").unsqueeze(2).broadcast_to([P, QK_HEADS, RF])
                s.link(dve.tensor_tensor(arg[:, b, :, 0:RF], p3, i3, ALU.mult))
                s.link(dve.tensor_scalar(arg[:, b, :, RF:D], arg[:, b, :, 0:RF], 0.25, None, ALU.add))
                s.link(dve.tensor_scalar(whole[:, b, :, :], arg[:, b, :, :], ROUND, ROUND, ALU.add, ALU.subtract))
                dve.tensor_tensor(arg[:, b, :, :], arg[:, b, :, :], whole[:, b, :, :], ALU.subtract).then_inc(arg_done, 1)

            def back(t, b):
                dve.wait_ge(prod_done, t + 1)
                dve.tensor_reduce(A[:, :, :], qk_prod[:, b, :].rearrange("p (h g d) -> p h g d", g=KV_HEADS, d=D),
                                  AX.X, ALU.add).then_inc(A_done, 1)
                dve.wait_ge(A_done, t + 1)
                v4 = e["v"][:, bass.ds(t, 1), :].rearrange("p a (g d) -> p a d g", d=D).broadcast_to([P, HEADS, D, KV_HEADS])
                a4 = A[:, :, :].unsqueeze(2).broadcast_to([P, HEADS, D, KV_HEADS])
                prod = av_prod[:, :].rearrange("p (h d g) -> p h d g", d=D, g=KV_HEADS)
                dve.tensor_tensor(prod, a4, v4, ALU.mult).then_inc(av_done, 1)
                dve.wait_ge(av_done, t + 1)
                if late(t):
                    dve.wait_ge(stored[b], (t - b) * 8)
                dve.tensor_reduce(out[:, b, :].rearrange("p (h d) -> p h d", d=D), prod, AX.X, ALU.add)\
                   .then_inc(out_done, 1)
            tiles(front, back)(dve)

        @block.sync
        def _(sp):
            with sp.Fori(0, BATCH) as i:
                for pos in range(POS_TILES):
                    t = i * POS_TILES + pos
                    seq = sp.snap(i)
                    sp.wait_ge(out_done, t + 1)
                    sp.dma_start(o_dram[bass.ds(seq, 1), :, pos * P:(pos + 1) * P, :].rearrange("b h s d -> s (b h) d"),
                                 out[:, pos % 2, :].rearrange("p (h d) -> p h d", d=D)).then_inc(stored[pos % 2], 16)
            for b in range(2):
                sp.wait_ge(stored[b], 8 * TILES)


def route(nc, tag, logits, NE, E, TOP, guard, CT, ident):
    T = TILES
    with ExitStack() as ctx:
        ctx.callback(nc.all_engine_barrier)
        def sem(name):
            return new_semaphore(nc, ctx, f"{tag}_{name}")

        def sb(name, shape, dt=F32):
            return ctx.enter_context(nc.sbuf_tensor(f"{tag}_{name}", shape, dt))
        prob, left, same, comb = (sb(x, [P, T, E]) for x in ("prob", "left", "same", "comb"))
        rank = sb("rank", [P, E])
        top, one = sb("top", [P, T]), sb("one", [P, T])
        total = sb("total", [P, T])
        split = sb("split", [P, T, 2 * NE])
        rounded = sb("rounded", [P, T, NE], F32R)
        psC = [ctx.enter_context(nc.psum_tensor(f"{tag}_psC{i}", [2 * NE, CHUNK], F32)) for i in range(2)]
        steps, shifted, exp_done, gate_done, split_done, cT_done, cT_out, rank_done = (
            sem(x) for x in ("steps", "shifted", "exp_done", "gate_done", "split_done", "cT_done", "cT_out", "rank_done"))
        block = ctx.enter_context(nc.Block())

        def over(x):
            return x[:, :].unsqueeze(2).broadcast_to([P, T, E])

        @block.gpsimd
        def _(pool):
            for j in range(E):
                pool.memset(rank[:, j:j + 1], float(E - j)).then_inc(rank_done, 1)

        @block.vector
        def _(dve):
            s = Steps(dve, steps)
            s.link(dve.tensor_reduce(top[:, :], logits[:, :, 0:E], AX.X, ALU.max))
            dve.tensor_tensor(prob[:, :, :], logits[:, :, 0:E], over(top), ALU.subtract).then_inc(shifted, 1)
            dve.wait_ge(exp_done, 1)
            s.link(dve.tensor_reduce(total[:, :], prob[:, :, :], AX.X, ALU.add))
            s.link(dve.reciprocal(total[:, :], total[:, :]))
            s.link(dve.tensor_tensor(prob[:, :, :], prob[:, :, :], over(total), ALU.mult))
            s.link(dve.tensor_copy(left[:, :, :], prob[:, :, :]))
            s.link(dve.memset(comb[:, :, :], 0.0))
            dve.wait_ge(rank_done, E)
            r3 = rank[:, :].unsqueeze(1).broadcast_to([P, T, E])
            for _k in range(TOP):
                s.link(dve.tensor_reduce(top[:, :], left[:, :, :], AX.X, ALU.max))
                s.link(dve.tensor_tensor(same[:, :, :], left[:, :, :], over(top), ALU.is_equal))
                s.link(dve.tensor_tensor(same[:, :, :], same[:, :, :], r3, ALU.mult))
                s.link(dve.tensor_reduce(one[:, :], same[:, :, :], AX.X, ALU.max))
                s.link(dve.tensor_tensor(same[:, :, :], over(one), r3, ALU.is_equal))
                s.link(dve.tensor_tensor(comb[:, :, :], comb[:, :, :], same[:, :, :], ALU.add))
                s.link(dve.scalar_tensor_tensor(left[:, :, :], same[:, :, :], -4.0, left[:, :, :], ALU.mult, ALU.add))
            s.link(dve.tensor_tensor(comb[:, :, :], comb[:, :, :], prob[:, :, :], ALU.mult))
            s.link(dve.tensor_reduce(total[:, :], comb[:, :, :], AX.X, ALU.add))
            if guard:
                s.link(dve.tensor_scalar(total[:, :], total[:, :], guard, None, ALU.add))
            s.link(dve.reciprocal(total[:, :], total[:, :]))
            s.link(dve.tensor_tensor(split[:, :, 0:E], comb[:, :, :], over(total), ALU.mult))
            if NE > E:
                dve.wait_ge(gate_done, 1)
            s.link(dve.tensor_copy(rounded[:, :, :], split[:, :, 0:NE]))
            s.link(dve.tensor_tensor(split[:, :, NE:2 * NE], split[:, :, 0:NE], rounded[:, :, :].bitcast(F32), ALU.subtract))
            dve.tensor_copy(split[:, :, 0:NE], rounded[:, :, :].bitcast(F32)).then_inc(split_done, 1)

        @block.scalar
        def _(act):
            act.wait_ge(shifted, 1)
            act.activation(prob[:, :, :], prob[:, :, :], ACT.Exp).then_inc(exp_done, 1)
            if NE > E:
                act.activation(split[:, :, E:NE], logits[:, :, E:NE], ACT.Sigmoid).then_inc(gate_done, 1)
            for c in range(CHUNKS):
                act.wait_ge(cT_done, c + 1)
                act.activation(CT[:, c * CHUNK:(c + 1) * CHUNK], psC[c % 2][:, :], ACT.Copy).then_inc(cT_out, 1)

        @block.tensor
        def _(pe):
            pe.wait_ge(split_done, 1)
            for c in range(CHUNKS):
                if c >= 2:
                    pe.wait_ge(cT_out, c - 1)
                for j in range(TPC):
                    ins = pe.transpose(psC[c % 2][:, j * P:(j + 1) * P], split[:, c * TPC + j, :], ident[:])
                ins.then_inc(cT_done, 1)


def experts(nc, tag, w_dram, NT, G, NE, XT_hi, XT_lo, CT, acc):
    NG = NT // G
    with ExitStack() as ctx:
        ctx.callback(nc.all_engine_barrier)
        def sem(name):
            return new_semaphore(nc, ctx, f"{tag}_{name}")

        def sb(name, shape, dt=F32):
            return ctx.enter_context(nc.sbuf_tensor(f"{tag}_{name}", shape, dt))
        RAW = 2
        raw = sb("raw", [P, RAW, WTS])
        w_hi, w_lo = sb("w_hi", [P, G, WTS], F32R), sb("w_lo", [P, G, WT], F32R)
        h = sb("h", [P, 2, CHUNK])
        h_hi, h_lo = sb("h_hi", [P, 2, CHUNK], F32R), sb("h_lo", [P, 2, CHUNK], F32R)
        psG, psU, psC = ([ctx.enter_context(nc.psum_tensor(f"{tag}_{n}{i}", [P, CHUNK], F32)) for i in range(2)]
                         for n in ("psG", "psU", "psC"))
        psY = ctx.enter_context(nc.psum_tensor(f"{tag}_psY", [P, TPC, HID], F32))
        raw_in = [sem(f"raw_in{i}") for i in range(RAW)]
        (hiw_done, low_done, up_done, silu_done, gu_done, h_done, hi_done, lo_done, down_done, y_done, y_out, zeroed) = (
            sem(x) for x in ("hiw_done", "low_done", "up_done", "silu_done", "gu_done", "h_done", "hi_done", "lo_done",
                             "down_done", "y_done", "y_out", "zeroed"))
        block = ctx.enter_context(nc.Block())

        @block.sync
        def _(sp):
            for w in range(NT):
                if w >= RAW:
                    sp.wait_ge(low_done, w - RAW + 1)
                sp.dma_start(raw[:, w % RAW, :], w_dram[w]).then_inc(raw_in[w % RAW], 16)

        @block.gpsimd
        def _(pool):
            pool.memset(acc[:, :, :], 0.0).then_inc(zeroed, 1)

        def groups(eng, first, chunk, tail):
            for g in range(NG):
                first(g)
                chunk(g, 1)
                with eng.Fori(1, CHUNKS // 2) as i:
                    chunk(g, i * 2, 0)
                    chunk(g, i * 2 + 1, 1)
                tail(g)

        def step(g, c, j):
            return (g * CHUNKS + c) * G + j

        def b_of(g, cpar, j):
            return (g * CHUNKS * G + cpar * G + j) % 2

        @block.vector
        def _(dve):
            def weights(g, j):
                w = g * G + j
                dve.wait_ge(raw_in[w % RAW], 16 * (w // RAW + 1))
                dve.wait_ge(hiw_done, w + 1)
                dve.tensor_tensor(w_lo[:, j, :], raw[:, w % RAW, 0:WT], w_hi[:, j, 0:WT].bitcast(F32), ALU.subtract)\
                   .then_inc(low_done, 1)

            def tile(g, c, j, b):
                n = step(g, c, j)
                dve.wait_ge(silu_done, n + 1)
                dve.tensor_tensor(h[:, b, :], h[:, b, :], psU[b][:, :], ALU.mult).then_inc(gu_done, 1)
                dve.wait_ge(gu_done, n + 1)
                dve.tensor_tensor(h[:, b, :], h[:, b, :], psC[b][:, :], ALU.mult).then_inc(h_done, 1)
                dve.wait_ge(hi_done, n + 1)
                dve.tensor_tensor(h_lo[:, b, :], h[:, b, :], h_hi[:, b, :].bitcast(F32), ALU.subtract).then_inc(lo_done, 1)

            def collect(g, c):
                m = g * CHUNKS + c
                dve.wait_ge(y_done, m + 1)
                for half in range(2):
                    a = acc[:, bass.ds(c * TPC + 2 * half, 2), :]
                    dve.tensor_tensor(a, a, psY[:, 2 * half:2 * half + 2, :], ALU.add).then_inc(y_out, 1)

            def first(g):
                if g:
                    dve.wait_ge(down_done, step(g, 0, 0))
                for j in range(G):
                    weights(g, j)
                    tile(g, 0, j, b_of(g, 0, j))

            def chunk(g, c, cpar=1):
                for j in range(G):
                    tile(g, c, j, b_of(g, cpar, j))
                    if j == 0:
                        collect(g, c - 1)
            dve.wait_ge(zeroed, 1)
            groups(dve, first, chunk, lambda g: collect(g, CHUNKS - 1))
            dve.wait_ge(y_out, 2 * NG * CHUNKS)

        @block.scalar
        def _(act):
            def weights(g, j):
                w = g * G + j
                act.wait_ge(raw_in[w % RAW], 16 * (w // RAW + 1))
                act.activation(w_hi[:, j, :], raw[:, w % RAW, :], ACT.Copy).then_inc(hiw_done, 1)

            def tile(g, c, j, b):
                n = step(g, c, j)
                act.wait_ge(up_done, n + 1)
                if not (isinstance(n, int) and n < 2):
                    act.wait_ge(lo_done, n - 1)
                act.activation(h[:, b, :], psG[b][:, :], ACT.Silu).then_inc(silu_done, 1)
                act.wait_ge(h_done, n + 1)
                if not (isinstance(n, int) and n < 2):
                    act.wait_ge(down_done, n - 1)
                act.activation(h_hi[:, b, :], h[:, b, :], ACT.Copy).then_inc(hi_done, 1)

            def first(g):
                if g:
                    act.wait_ge(down_done, step(g, 0, 0))
                for j in range(G):
                    weights(g, j)
                    tile(g, 0, j, b_of(g, 0, j))

            def chunk(g, c, cpar=1):
                for j in range(G):
                    tile(g, c, j, b_of(g, cpar, j))
            groups(act, first, chunk, lambda g: None)

        @block.tensor
        def _(pe):
            def up(g, c, j, b):
                n = step(g, c, j)
                if not (isinstance(n, int) and n < 2):
                    pe.wait_ge(h_done, n - 1)
                x_hi = lambda k: XT_hi[:, k, bass.ds(c * CHUNK, CHUNK)]
                x_lo = lambda k: XT_lo[:, k, bass.ds(c * CHUNK, CHUNK)]
                for half, out in ((0, psG[b]), (1, psU[b])):
                    col = lambda k: (half * KT + k) * P
                    three_passes(pe, out[:, :], lambda k: w_hi[:, j, col(k):col(k) + P],
                                 lambda k: w_lo[:, j, col(k):col(k) + P], x_hi, x_lo, KT)
                pe.matmul(psC[b][:, :], w_hi[0:2 * NE, j, WT:WTS], CT[:, bass.ds(c * CHUNK, CHUNK)], start=True, stop=True)\
                    .then_inc(up_done, 1)

            def down(g, c, j, b):
                n = step(g, c, j)
                pe.wait_ge(lo_done, n + 1)
                if j == 0 and not (isinstance(c, int) and g * CHUNKS + c == 0):
                    pe.wait_ge(y_out, (g * CHUNKS + c) * 2)
                for m in range(TPC):
                    ins = three_passes(pe, psY[:, m, :], lambda k: h_hi[:, b, m * P:(m + 1) * P],
                                       lambda k: h_lo[:, b, m * P:(m + 1) * P],
                                       lambda k: w_hi[:, j, 2 * KT * P:WT], lambda k: w_lo[:, j, 2 * KT * P:WT], 1,
                                       first=j == 0 and m % 2 == 0, last=j == G - 1, check=True)
                ins.then_inc(down_done, 1)
                if j == G - 1:
                    pe.wait_ge(down_done, n + 1)
                    pe.sem_inc(y_done, 1)

            def first(g):
                for j in range(G):
                    pe.wait_ge(low_done, g * G + j + 1)
                    up(g, 0, j, b_of(g, 0, j))
                    if j:
                        down(g, 0, j - 1, b_of(g, 0, j - 1))

            def chunk(g, c, cpar=1):
                for j in range(G):
                    up(g, c, j, b_of(g, cpar, j))
                    if j:
                        down(g, c, j - 1, b_of(g, cpar, j - 1))
                    else:
                        down(g, c - 1, G - 1, b_of(g, 1 - cpar, G - 1))
            groups(pe, first, chunk, lambda g: down(g, CHUNKS - 1, G - 1, b_of(g, 1, G - 1)))


def gate_and_add(nc, tag, x_dram, s_dram, acc, out_dram):
    with ExitStack() as ctx:
        ctx.callback(nc.all_engine_barrier)
        def sem(name):
            return new_semaphore(nc, ctx, f"{tag}_{name}")
        STEP = 4
        xt = ctx.enter_context(nc.sbuf_tensor(f"{tag}_xt", [P, 2, STEP, HID], F32))
        stt = ctx.enter_context(nc.sbuf_tensor(f"{tag}_stt", [P, 2, STEP, HID], F32))
        gate = ctx.enter_context(nc.sbuf_tensor(f"{tag}_gate", [P, 2, STEP, HID], F32))
        x_in, s_in = [sem("x_in0"), sem("x_in1")], [sem("s_in0"), sem("s_in1")]
        gate_done, mul_done, sum_done, stored = (sem(x) for x in ("gate_done", "mul_done", "sum_done", "stored"))
        block = ctx.enter_context(nc.Block())
        N = TILES // STEP

        @block.sync
        def _(sp):
            for t in range(N):
                if t >= 2:
                    sp.wait_ge(sum_done, t - 1)
                for src, dst, sems in ((x_dram, xt, x_in), (s_dram, stt, s_in)):
                    sp.dma_start(dst[:, t % 2, :, :], src[t * STEP:(t + 1) * STEP].rearrange("t p n -> p t n"))\
                        .then_inc(sems[t % 2], 16)

        @block.gpsimd
        def _(pool):
            for t in range(N):
                pool.wait_ge(sum_done, t + 1)
                pool.dma_start(out_dram[t * STEP:(t + 1) * STEP].rearrange("t p n -> p t n"),
                               acc[:, t * STEP:(t + 1) * STEP, :]).then_inc(stored, 16)
            pool.wait_ge(stored, 16 * N)

        @block.scalar
        def _(act):
            for t in range(N):
                if t >= 2:
                    act.wait_ge(mul_done, t - 1)
                act.activation(gate[:, t % 2, :, :], acc[:, t * STEP:(t + 1) * STEP, :], ACT.Silu).then_inc(gate_done, 1)

        @block.vector
        def _(dve):
            for t in range(N):
                b = t % 2
                dve.wait_ge(gate_done, t + 1)
                dve.wait_ge(s_in[b], 16 * (t // 2 + 1))
                dve.tensor_tensor(stt[:, b, :, :], stt[:, b, :, :], gate[:, b, :, :], ALU.mult).then_inc(mul_done, 1)
                dve.wait_ge(mul_done, t + 1)
                dve.wait_ge(x_in[b], 16 * (t // 2 + 1))
                dve.tensor_tensor(acc[:, t * STEP:(t + 1) * STEP, :], stt[:, b, :, :], xt[:, b, :, :], ALU.add)\
                   .then_inc(sum_done, 1)


def steps_of(pairs):
    return pairs


def causal_attention(nc, w_dram, XT_hi, XT_lo, ident, mask_qk, mask_kq, ident_b, ao):
    with ExitStack() as ctx:
        ctx.callback(nc.all_engine_barrier)
        def sem(name):
            return new_semaphore(nc, ctx, f"ca_{name}")

        def sb(name, shape, dt=F32):
            return ctx.enter_context(nc.sbuf_tensor(f"ca_{name}", shape, dt))
        raw = sb("raw", [P, AW + 4])
        w_hi, w_lo = sb("w_hi", [P, AW], F32R), sb("w_lo", [P, AW], F32R)
        QKV = sb("QKV", [P, 3, SEQ])
        QT, KTT, VT = (QKV[:, i, :] for i in range(3))
        VA = sb("VA", [P, POS_TILES, P])
        Mst = sb("Mst", [P, POS_TILES, P])
        max_steps = [(qt, k0, min(CHUNK, (qt + 1) * P - k0)) for qt in range(POS_TILES)
                     for k0 in range(0, (qt + 1) * P, CHUNK)]
        mpart = sb("mpart", [P, len(max_steps), GH])
        mwhole = sb("mwhole", [P, POS_TILES, GH])
        OT = sb("OT", [P, CHUNK])
        rsum = sb("rsum", [P, TPC, GH])
        keys = [[(kt, max(kt * P - c * CHUNK, 0)) for kt in range((c + 1) * TPC)] for c in range(SPAN)]
        sizes = [sum(CHUNK - off for _, off in ks) for ks in keys]
        PT = [sb(f"PT{c}", [P, GH * sizes[c]]) for c in range(SPAN)]
        bank = ctx.enter_context(nc.psum_tensor("ca_bank", [P, 8, CHUNK], F32))
        (w_in, hiw_done, low_done, proj_done, proj_out, vT_done, v_out, max_done, max_out, m_done, mT_done, q_ready,
         s_done, exp_done, pv_done, ot_out, oT_done, sum_done, o_out, zeroed, steps) = (sem(x) for x in (
             "w_in", "hiw_done", "low_done", "proj_done", "proj_out", "vT_done", "v_out", "max_done", "max_out", "m_done",
             "mT_done", "q_ready", "s_done", "exp_done", "pv_done", "ot_out", "oT_done", "sum_done", "o_out", "zeroed", "steps"))
        block = ctx.enter_context(nc.Block())

        NM = len(max_steps)
        NS = sum(len(k) for k in keys)
        S_STEPS = [(c, kt, off) for c in range(SPAN) for kt, off in keys[c]]

        def pt(c, kt, h0, h1):
            base = GH * sum(CHUNK - off for k, off in keys[c] if k < kt)
            w = CHUNK - keys[c][kt][1]
            return PT[c][:, base:base + GH * w].rearrange("p (h n) -> p h n", h=GH)[:, h0:h1, :]

        def s_set(s):
            return 4 * (1 - s % 2) if s < NS // 3 + 1 else 4 * (1 - s % 2)

        def every(eng, body, group=None):
            with eng.Fori(0, GROUPS) as g:
                if group:
                    group(g)
                with eng.Fori(0, BATCH) as b:
                    body(g, b, g * BATCH + b)

        @block.sync
        def _(sp):
            sp.dma_start(raw[:, :], w_dram[0]).then_inc(w_in, 16)
            for g in range(1, GROUPS):
                sp.wait_ge(low_done, g)
                sp.wait_ge(proj_out, g * (BATCH * 6))
                sp.dma_start(raw[:, :], w_dram[g]).then_inc(w_in, 16)

        @block.gpsimd
        def _(pool):
            pool.memset(Mst[:, :, :], 0.0).then_inc(zeroed, 1)

        @block.vector
        def _(dve):
            dve.wait_ge(zeroed, 1)

            def group(g):
                dve.wait_ge(w_in, g * 16 + 16)
                dve.tensor_copy(w_hi[:, :], raw[:, 0:AW]).then_inc(hiw_done, 1)
                dve.wait_ge(hiw_done, g + 1)
                dve.tensor_tensor(w_lo[:, :], raw[:, 0:AW], w_hi[:, :].bitcast(F32), ALU.subtract).then_inc(low_done, 1)

            def body(g, b, i):
                for u in range(6):
                    which, c = u // 2, u % 2
                    dve.wait_ge(proj_done, i * 6 + u + 1)
                    dve.tensor_scalar(QKV[:, which, c * CHUNK:(c + 1) * CHUNK], bank[:, u, :], raw[:, AW + which:AW + which + 1],
                                      0.25 if which == 0 else 1.0, ALU.add, ALU.mult).then_inc(proj_out, 1)
                for s, (qt, k0, w) in enumerate(max_steps):
                    dve.wait_ge(max_done, i * NM + s + 1)
                    set0 = 4 * (s % 2)
                    part = 0 if k0 == 0 else 1
                    dve.tensor_reduce(mpart[:, s, :], bank[:, set0:set0 + GH, 0:w], AX.X, ALU.max).then_inc(max_out, 1)
                    if k0 + w == (qt + 1) * P:
                        dve.wait_ge(max_out, i * NM + s + 1)
                        m_col = Mst[:, qt, :].rearrange("p (h c) -> p h c", h=GH)[:, :, D]
                        if part:
                            dve.tensor_tensor(mwhole[:, qt, :], mpart[:, s - 1, :], mpart[:, s, :], ALU.max).then_inc(steps, 1)
                            dve.wait_ge(steps, i * (POS_TILES - TPC) + (qt - TPC) + 1)
                        dve.tensor_scalar(m_col, mwhole[:, qt, :] if part else mpart[:, s, :], -1.0, None, ALU.mult).then_inc(m_done, 1)
                for c in range(SPAN):
                    dve.wait_ge(mT_done, i * SPAN + c + 1)
                    q = QT[:, c * CHUNK:(c + 1) * CHUNK]
                    dve.tensor_tensor(q, q, bank[:, c, :], ALU.add).then_inc(q_ready, 1)
                for c in range(SPAN):
                    dve.wait_ge(pv_done, i * SPAN + c + 1)
                    dve.tensor_copy(OT[:, :], bank[:, 4 * c, :]).then_inc(ot_out, 1)
                    dve.wait_ge(oT_done, i * SPAN + c + 1)
                    o4 = bank[:, 4 * c + 1, :].rearrange("p (q h d) -> p q h d", q=TPC, h=GH)
                    dve.reciprocal(rsum[:, :, :], o4[:, :, :, D]).then_inc(sum_done, 1)
                    dve.wait_ge(sum_done, i * SPAN + c + 1)
                    for hh in range(GH):
                        dst = ao[:, bass.ds(b * POS_TILES + c * TPC, TPC), bass.ds(g * (GH * D) + hh * D, D)]
                        ins = dve.tensor_tensor(dst, o4[:, :, hh, 0:D], rsum[:, :, hh].unsqueeze(2).broadcast_to([P, TPC, D]),
                                                ALU.mult)
                        ins.then_inc(o_out, 1)
            every(dve, body, group)
            dve.wait_ge(o_out, GROUPS * BATCH * SPAN * GH)

        @block.scalar
        def _(act):
            def body(g, b, i):
                for v in range(2):
                    act.wait_ge(vT_done, i * 2 + v + 1)
                    act.activation(VA[:, v * TPC:(v + 1) * TPC, :].rearrange("p a n -> p (a n)"), bank[:, 6 + v, :], ACT.Copy)\
                       .then_inc(v_out, 1)
                for s, (c, kt, off) in enumerate(S_STEPS):
                    act.wait_ge(s_done, i * NS + s + 1)
                    set0 = 4 * (1 - s % 2)
                    act.activation(pt(c, kt, 0, GH), bank[:, set0:set0 + GH, off:CHUNK], ACT.Exp).then_inc(exp_done, 1)
            every(act, body)

        @block.tensor
        def _(pe):
            def scores(lhs, l0, rhs, r0, w, set0, off, mask, diag):
                for h in range(GH):
                    rows = slice(32 * h, 32 * h + 32)
                    ins = pe.matmul(bank[:, set0 + h, off:off + w], lhs[rows, l0:l0 + P], rhs[rows, r0:r0 + w],
                                    start=True, stop=diag is None, tile_position=(32 * h, 0), skip_group_check=True)
                if diag is not None:
                    for h in range(GH):
                        ins = pe.matmul(bank[:, set0 + h, diag:diag + P], ident_b[:, :], mask[:, :], start=False, stop=True,
                                        skip_group_check=True)
                return ins

            def values(i, c):
                n = len(keys[c])
                for j, (kt, off) in enumerate(keys[c]):
                    for h in range(GH):
                        rows = slice(32 * h, 32 * h + 32)
                        ins = pe.matmul(bank[rows, 4 * c, off:CHUNK], VA[:, kt, 32 * h:32 * h + 32],
                                        pt(c, kt, h, h + 1).rearrange("p a n -> p (a n)"),
                                        start=j == 0, stop=j == n - 1, tile_position=(0, 32 * h), skip_group_check=True)
                ins.then_inc(pv_done, 1)
                pe.wait_ge(ot_out, i * SPAN + c + 1)
                for q in range(TPC):
                    ins = pe.transpose(bank[:, 4 * c + 1, q * P:(q + 1) * P], OT[:, q * P:(q + 1) * P], ident[:, :])
                ins.then_inc(oT_done, 1)
                pe.wait_ge(o_out, i * (SPAN * GH) + (c + 1) * GH)

            def body(g, b, i):
                pe.wait_ge(low_done, g + 1)
                for u in range(6):
                    which, c = u // 2, u % 2
                    x = bass.ds(b * SEQ + c * CHUNK, CHUNK)
                    col = lambda k: (which * KT + k) * P
                    three_passes(pe, bank[:, u, :], lambda k: w_hi[:, col(k):col(k) + P], lambda k: w_lo[:, col(k):col(k) + P],
                                 lambda k: XT_hi[:, k, x], lambda k: XT_lo[:, k, x], KT).then_inc(proj_done, 1)
                pe.wait_ge(proj_out, i * 6 + 6)
                for v in range(2):
                    for q in range(TPC):
                        kt = v * TPC + q
                        ins = pe.transpose(bank[:, 6 + v, q * P:(q + 1) * P], VT[:, kt * P:(kt + 1) * P], ident[:, :])
                    ins.then_inc(vT_done, 1)
                for s, (qt, k0, w) in enumerate(max_steps):
                    if s == 1:
                        pe.wait_ge(v_out, i * 2 + 2)
                    if s >= 2:
                        pe.wait_ge(max_out, i * NM + s - 1)
                    diag = w - P if k0 + w == (qt + 1) * P else None
                    scores(QT, qt * P, KTT, k0, w, 4 * (s % 2), 0, mask_qk, diag).then_inc(max_done, 1)
                pe.wait_ge(m_done, i * POS_TILES + POS_TILES)
                for c in range(SPAN):
                    for q in range(TPC):
                        ins = pe.transpose(bank[:, c, q * P:(q + 1) * P], Mst[:, c * TPC + q, :], ident[:, :])
                    ins.then_inc(mT_done, 1)
                pe.wait_ge(q_ready, i * SPAN + SPAN)
                for s, (c, kt, off) in enumerate(S_STEPS):
                    if s >= 2:
                        pe.wait_ge(exp_done, i * NS + s - 1)
                    diag = off if kt * P >= c * CHUNK else None
                    scores(KTT, kt * P, QT, c * CHUNK + off, CHUNK - off, 4 * (1 - s % 2), off, mask_kq, diag)\
                        .then_inc(s_done, 1)
                    if s == TPC:
                        pe.wait_ge(exp_done, i * NS + TPC)
                        values(i, 0)
                pe.wait_ge(exp_done, i * NS + NS)
                values(i, 1)
            every(pe, body)


def project_out(nc, tag, o_tile, s_dram, ident, wo, bo, scale):
    with ExitStack() as ctx:
        ctx.callback(nc.all_engine_barrier)
        def sem(name):
            return new_semaphore(nc, ctx, f"{tag}_{name}")
        o_st = ctx.enter_context(nc.sbuf_tensor(f"{tag}_o_st", [P, 2, HID], F32))
        oT = ctx.enter_context(nc.sbuf_tensor(f"{tag}_oT", [P, 2, HID], F32))
        s_sb = ctx.enter_context(nc.sbuf_tensor(f"{tag}_s_sb", [P, 2, HID], F32))
        psT = [ctx.enter_context(nc.psum_tensor(f"{tag}_psT{i}", [P, HID], F32)) for i in range(2)]
        psS = [ctx.enter_context(nc.psum_tensor(f"{tag}_psS{i}", [P, HID], F32)) for i in range(2)]
        oT_done, oT_out, s_done, s_out = (sem(x) for x in ("oT_done", "oT_out", "s_done", "s_out"))
        staged = [sem("staged0"), sem("staged1")]
        stored = [sem("stored0"), sem("stored1")]
        block = ctx.enter_context(nc.Block())

        def tiles(eng, body):
            body(0, 0)
            body(1, 1)
            with eng.Fori(1, TILES // 2) as i:
                body(i * 2, 0)
                body(i * 2 + 1, 1)

        def late(t):
            return not isinstance(t, int)

        @block.gpsimd
        def _(pool):
            def body(t, b):
                if late(t):
                    pool.wait_ge(oT_done, t - 1)
                pool.dma_start(o_st[:, b, :], o_tile(t)).then_inc(staged[b], 16)
            tiles(pool, body)

        @block.tensor
        def _(pe):
            def body(t, b):
                pe.wait_ge(staged[b], (t - b) * 8 + 16)
                if late(t):
                    pe.wait_ge(oT_out, t - 1)
                for k in range(KT):
                    ins = pe.transpose(psT[b][:, k * P:(k + 1) * P], o_st[:, b, k * P:(k + 1) * P], ident[:])
                ins.then_inc(oT_done, 1)
                pe.wait_ge(oT_out, t + 1)
                if late(t):
                    pe.wait_ge(s_out, t - 1)
                for k in range(KT):
                    ins = pe.matmul(psS[b][:], oT[:, b, k * P:(k + 1) * P], wo[:, k, :], start=k == 0, stop=k == KT - 1)
                ins.then_inc(s_done, 1)
            tiles(pe, body)

        @block.scalar
        def _(act):
            def body(t, b):
                act.wait_ge(oT_done, t + 1)
                if late(t):
                    act.wait_ge(s_done, t - 1)
                act.activation(oT[:, b, :], psT[b][:], ACT.Copy).then_inc(oT_out, 1)
            tiles(act, body)

        @block.vector
        def _(dve):
            def body(t, b):
                dve.wait_ge(s_done, t + 1)
                if late(t):
                    dve.wait_ge(stored[b], (t - b) * 8)
                dve.scalar_tensor_tensor(s_sb[:, b, :], psS[b][:], scale, bo[:], ALU.mult, ALU.add).then_inc(s_out, 1)
            tiles(dve, body)

        @block.sync
        def _(sp):
            def body(t, b):
                row = sp.snap(t) if not isinstance(t, int) else t
                sp.wait_ge(s_out, t + 1)
                sp.dma_start(s_dram[bass.ds(row, 1), :, :].rearrange("a p n -> p (a n)"), s_sb[:, b, :]).then_inc(stored[b], 16)
            tiles(sp, body)
            for b in range(2):
                sp.wait_ge(stored[b], 8 * TILES)


def build(nc, a, out):
    x_v = a["x"].rearrange("(t p) n -> t p n", p=P)
    out_v = out.rearrange("b (t p) n -> (b t) p n", p=P)
    s0_dram = nc.dram_tensor("s0_scratch", [TILES, P, HID], F32, kind="Internal").ap()
    s1_dram = nc.dram_tensor("s1_scratch", [TILES, P, HID], F32, kind="Internal").ap()
    o_dram = nc.dram_tensor("o_scratch", [BATCH, HEADS, SEQ, D], F32, kind="Internal").ap()
    x1_dram = nc.dram_tensor("x1_scratch", [TILES, P, HID], F32, kind="Internal").ap()
    with ExitStack() as top:
        def sb(ctx, name, shape, dt=F32):
            return ctx.enter_context(nc.sbuf_tensor(name, shape, dt))
        XT_hi, XT_lo = sb(top, "XT_hi", [P, KT, TOKENS], F32R), sb(top, "XT_lo", [P, KT, TOKENS], F32R)
        ident = sb(top, "ident", [P, P])
        mean_rstd = sb(top, "mean_rstd", [P, TILES, 2])
        logits = sb(top, "logits", [P, TILES, RW1])

        def row(ap):
            return ap.rearrange("(a n) -> a n", a=1).partition_broadcast(P)

        with ExitStack() as c:
            wo, bo = sb(c, "wo_0", [P, KT, HID]), sb(c, "bo_0", [P, HID])
            n2 = sb(c, "n2_all", [P, TILES, QK_HEADS])
            proj, v = sb(c, "proj", [P, TILES, QK_HEADS * RF]), sb(c, "v_all", [P, TILES, KV_HEADS * D])
            with ExitStack() as c2:
                x_sb = sb(c2, "x_sb", [P, TILES, HID])
                wq_raw = sb(c2, "wq_raw", [P, KT, 512])
                wq_hi, wq_lo = sb(c2, "wq_hi", [P, KT, 512], F32R), sb(c2, "wq_lo", [P, KT, 512], F32R)
                wr_raw = sb(c2, "wr_raw", [P, KT, E0])
                wr_hi, wr_lo = sb(c2, "wr_hi", [P, KT, E0], F32R), sb(c2, "wr_lo", [P, KT, E0], F32R)
                rblk, bias = sb(c2, "rblk", [P, 64]), sb(c2, "bias", [P, 512])
                cos, sin = sb(c2, "cos", [P, POS_TILES, D]), sb(c2, "sin", [P, POS_TILES, D])
                split_weights(nc, "w0", [(wq_raw[:], wq_hi[:], wq_lo[:]), (wr_raw[:], wr_hi[:], wr_lo[:])], [
                    (ident[:], a["ident"]), (wq_raw[:], a["wqkv0"]), (wr_raw[:], a["wr0"]), (rblk[:], a["rblk"]),
                    (bias[:], a["bias0"].partition_broadcast(P)), (cos[:], a["cos"]), (sin[:], a["sin"]),
                    (wo[:], a["wo0"]), (bo[:], a["bo0"].partition_broadcast(P))])
                standardise(nc, x_sb, mean_rstd, lambda sp, i: sp.dma_start(
                    x_sb[:, 4 * i:4 * i + 4, :], x_v[4 * i:4 * i + 4].rearrange("t p n -> p t n")), "ln0")
                normalise_and_transpose(nc, "nt0", x_sb, mean_rstd, XT_hi, XT_lo, logits[:, :, 0:E0], wr_hi, wr_lo, E0, ident,
                                        {"w_hi": wq_hi, "w_lo": wq_lo, "bias": bias, "cos": cos, "sin": sin, "rblk": rblk,
                                         "n2": n2, "proj": proj, "v": v})
            linear_attention(nc, {"n2": n2, "proj": proj, "v": v}, o_dram)
            o_rows = o_dram.rearrange("b h s d -> (b h s d)").rearrange("(t p n) -> t p n", p=P, n=HID)
            project_out(nc, "po0", lambda t: o_rows[bass.ds(t, 1), :, :].rearrange("a p n -> p (a n)"), s0_dram, ident, wo, bo,
                        SHARE)
        with ExitStack() as c:
            acc = sb(c, "acc0", [P, TILES, HID])
            with ExitStack() as c2:
                CT = sb(c2, "CT0", [2 * E0, TOKENS], F32R)
                route(nc, "r0", logits[:, :, 0:E0], E0, E0, TOP0, 1e-20, CT, ident)
                experts(nc, "f0", a["ffn0"], NT0, G0, E0, XT_hi, XT_lo, CT, acc)
            gate_and_add(nc, "g0", x_v, s0_dram, acc, x1_dram)
            wr_raw = sb(c, "wr1_raw", [P, KT, RW1])
            wr_hi, wr_lo = sb(c, "wr1_hi", [P, KT, RW1], F32R), sb(c, "wr1_lo", [P, KT, RW1], F32R)
            split_weights(nc, "w1", [(wr_raw[:], wr_hi[:], wr_lo[:])], [
                (wr_raw[:], a["wr1"])])
            standardise(nc, acc, mean_rstd, lambda sp, i: sp.dma_start(
                acc[:, 4 * i:4 * i + 4, :], x1_dram[4 * i:4 * i + 4].rearrange("t p n -> p t n")), "ln1")
            normalise_and_transpose(nc, "nt1", acc, mean_rstd, XT_hi, XT_lo, logits, wr_hi, wr_lo, RW1, ident)
        with ExitStack() as c:
            ao = sb(c, "ao", [P, TILES, HID])
            ident_b, mqk, mkq = sb(c, "ident_b", [P, P], BF16), sb(c, "mask_qk", [P, P], BF16), sb(c, "mask_kq", [P, P], BF16)
            wo, bo = sb(c, "wo_1", [P, KT, HID]), sb(c, "bo_1", [P, HID])
            split_weights(nc, "wo1", [], [(wo[:], a["wo1"]), (bo[:], a["bo1"].partition_broadcast(P))])
            masks(nc, ident_b, mqk, mkq)
            causal_attention(nc, a["attn1"], XT_hi, XT_lo, ident, mqk, mkq, ident_b, ao)
            project_out(nc, "po1", lambda t: ao[:, bass.ds(t, 1), :].rearrange("p a n -> p (a n)"), s1_dram, ident, wo, bo, 1.0)
        with ExitStack() as c:
            acc = sb(c, "acc1", [P, TILES, HID])
            with ExitStack() as c2:
                CT = sb(c2, "CT1", [2 * (E1 + 1), TOKENS], F32R)
                route(nc, "r1", logits[:, :, 0:E1 + 1], E1 + 1, E1, TOP1, 0.0, CT, ident)
                experts(nc, "f1", a["ffn1"], NT1, G1, E1 + 1, XT_hi, XT_lo, CT, acc)
            gate_and_add(nc, "g1", x1_dram, s1_dram, acc, out_v)


def masks(nc, ident_b, mqk, mkq):
    with ExitStack() as ctx:
        ctx.callback(nc.all_engine_barrier)
        filled = new_semaphore(nc, ctx, "mk_filled")
        done = new_semaphore(nc, ctx, "mk_done")
        block = ctx.enter_context(nc.Block())

        @block.gpsimd
        def _(pool):
            for m in (ident_b, mqk, mkq):
                pool.memset(m[:, :], 0.0).then_inc(filled, 1)
            pool.wait_ge(filled, 3)
            pool.affine_select(out=ident_b[:, :], in_=ident_b[:, :], compare_op=ALU.not_equal, fill=1.0, base=0,
                               pattern=[[-1, P]], channel_multiplier=1).then_inc(done, 1)
            pool.affine_select(out=mqk[:, :], in_=mqk[:, :], compare_op=ALU.is_ge, fill=NEG, base=0,
                               pattern=[[-1, P]], channel_multiplier=1).then_inc(done, 1)
            pool.affine_select(out=mkq[:, :], in_=mkq[:, :], compare_op=ALU.is_ge, fill=NEG, base=0,
                               pattern=[[1, P]], channel_multiplier=-1).then_inc(done, 1)
            pool.wait_ge(done, 3)


def kernel(**inputs):
    import numpy as np
    import concourse.bacc as bacc
    from concourse.bass_utils import run_bass_kernel_spmd

    w = {k: np.asarray(v) for k, v in inputs.items()}

    def kmajor(m):
        return np.ascontiguousarray(m.reshape(KT, P, -1).transpose(1, 0, 2))

    def ffn(gate, up, down, nt, owner, n_experts):
        mid = gate.shape[1]
        pad = nt * P - mid
        gate, up = (np.concatenate([m, np.zeros((HID, pad), m.dtype)], 1) for m in (gate, up))
        down = np.concatenate([down, np.zeros((pad, HID), down.dtype)], 0)
        sel = np.zeros((P, nt * P), np.float32)
        sel[owner, np.arange(mid)] = 1.0
        sel[n_experts + owner, np.arange(mid)] = 1.0
        packed = np.zeros((nt, P, WTS), gate.dtype)
        gu = np.stack([gate, up]).reshape(2, KT, P, nt, P)
        packed[:, :, :2 * KT * P] = gu.transpose(3, 2, 0, 1, 4).reshape(nt, P, 2 * KT * P)
        packed[:, :, 2 * KT * P:WT] = down.reshape(nt, P, HID)
        packed[:, :, WT:] = sel.reshape(P, nt, P).transpose(1, 0, 2)
        return packed

    a = {"x": w["L0_attn_hidden_states"].reshape(TOKENS, HID), "ident": np.eye(P, dtype=np.float32)}
    a["wqkv0"] = kmajor(np.concatenate([w["L0_attn_Wq"], w["L0_attn_Wk"], w["L0_attn_Wv"]], 0).T)
    a["bias0"] = np.concatenate([w["L0_attn_bq"], w["L0_attn_bk"], w["L0_attn_bv"]])
    a["wr0"] = kmajor(w["L0_ffn_wg"].T)
    a["wo0"], a["bo0"] = kmajor(w["L0_attn_Wo"].T), w["L0_attn_bo"]
    a["wo1"], a["bo1"] = kmajor(w["L1_attn_Wo"].T), w["L1_attn_bo"]
    rblk = np.zeros((P, P // D, RF), np.float32)
    for h in range(P // D):
        rblk[h * D:(h + 1) * D, h, :] = w["L0_attn_rand_matrix"].T
    a["rblk"] = rblk.reshape(P, P // D * RF)
    inv_freq = (1.0 / 10000.0 ** (np.arange(0, D, 2, dtype=np.float32) / np.float32(D))).astype(np.float32)
    angle = (np.arange(SEQ, dtype=np.float32)[:, None] * inv_freq[None, :]).reshape(POS_TILES, P, RF).transpose(1, 0, 2)
    a["cos"] = np.concatenate([np.cos(angle), np.cos(angle)], -1).astype(np.float32)
    a["sin"] = np.concatenate([-np.sin(angle), np.sin(angle)], -1).astype(np.float32)
    w1, w2 = w["L0_ffn_w1"], w["L0_ffn_w2"]
    a["ffn0"] = ffn(w1[:, :, :MID].transpose(1, 0, 2).reshape(HID, E0 * MID), w1[:, :, MID:].transpose(1, 0, 2).reshape(HID, E0 * MID),
                    w2.reshape(E0 * MID, HID), NT0, np.repeat(np.arange(E0), MID), E0)
    gu, sgu = w["L1_ffn_expert_gate_up"], w["L1_ffn_shared_gate_up"]
    gate = np.concatenate([gu[:, :MID].reshape(E1 * MID, HID), sgu[:SHARED]], 0).T
    up = np.concatenate([gu[:, MID:].reshape(E1 * MID, HID), sgu[SHARED:]], 0).T
    down = np.concatenate([w["L1_ffn_expert_down"].transpose(0, 2, 1).reshape(E1 * MID, HID), w["L1_ffn_shared_down"].T], 0)
    owner = np.concatenate([np.repeat(np.arange(E1), MID), np.full(SHARED, E1)])
    a["ffn1"] = ffn(gate, up, down, NT1, owner, E1 + 1)
    a["wr1"] = kmajor(np.concatenate([w["L1_ffn_gate_w"], w["L1_ffn_shared_gate_vec"], np.zeros((1, HID), np.float32)], 0).T)
    attn = np.zeros((GROUPS, P, AW + 4), np.float32)
    for n, (m, bias, one) in enumerate((("Wq", "bq", 0.0), ("Wk", "bk", 1.0), ("Wv", "bv", 1.0))):
        strip = np.zeros((HEADS, 32, HID), np.float32)
        strip[:, :D] = w[f"L1_attn_{m}"].reshape(HEADS, D, HID)
        wt = strip.reshape(GROUPS, GH * 32, KT, P).transpose(0, 3, 2, 1)
        attn[:, :, n * KT * P:(n + 1) * KT * P] = wt.reshape(GROUPS, P, KT * P)
        b = np.zeros((HEADS, 32), np.float32)
        b[:, :D] = w[f"L1_attn_{bias}"].reshape(HEADS, D)
        b[:, D] = one
        attn[:, :, AW + n] = b.reshape(GROUPS, P)
    a["attn1"] = attn
    a = {k: np.ascontiguousarray(v) for k, v in a.items()}

    nc = bacc.Bacc("TRN2", target_bir_lowering=False, num_devices=1)
    aps = {k: nc.dram_tensor(f"in_{k}", v.shape, mybir.dt.from_np(v.dtype), kind="ExternalInput").ap() for k, v in a.items()}
    out = nc.dram_tensor("out_0", (BATCH, SEQ, HID), F32, kind="ExternalOutput").ap()
    build(nc, aps, out)
    r = run_bass_kernel_spmd(nc, [{f"in_{k}": v for k, v in a.items()}], core_ids=[0])
    return r.results[0]["out_0"]
```

```python
from contextlib import ExitStack

import concourse.bass as bass
from concourse import mybir

F32 = mybir.dt.float32
F32R = mybir.dt.float32r
BF16 = mybir.dt.bfloat16
ALU = mybir.AluOpType
ACT = mybir.ActivationFunctionType
AX = mybir.AxisListType

P = 128
BATCH, SEQ, HID = 4, 1024, 256
TOKENS = BATCH * SEQ
TILES = TOKENS // P
KT = HID // P
CHUNK = 512
CHUNKS = TOKENS // CHUNK
TPC = CHUNK // P
HEADS, D = 16, 16
KV_HEADS = 8
QK_HEADS = HEADS + KV_HEADS
SHARE = (HEADS // KV_HEADS) / D
RF = D // 2
POS_TILES = SEQ // P
EPS = 1e-5
NEG = -1e30
ROUND = 1.5 * 2.0 ** 23
TWO_PI = 6.283185005187988
MID = 176
E0, TOP0 = 8, 2
E1, TOP1 = 16, 4
RW1 = E1 + 2
SHARED = 704
NT0 = E0 * MID // P
NT1 = -(-(E1 * MID + SHARED) // P)
G0, G1 = 11, 7
WT = 2 * KT * P + HID
WTS = WT + P
GH = 4
GROUPS = HEADS // GH
STRIP = 32
QK_TILES = 2 * HID // P
STACK = 4 * D
ROWS = STACK + 2
PADDED = 96
SPAN = SEQ // CHUNK


def new_semaphore(nc, ctx, name):
    handle = ctx.enter_context(nc.semaphore(name))
    ctx.callback(lambda: nc.gpsimd.sem_clear(handle))
    return handle


class Steps:

    def __init__(self, eng, sem):
        self.eng, self.sem, self.n, self.base = eng, sem, 0, 0

    def link(self, ins):
        self.n += 1
        ins.then_inc(self.sem, 1)
        self.eng.wait_ge(self.sem, self.base + self.n)


def three_passes(pe, out, w_hi, w_lo, x_hi, x_lo, kt, first=True, last=True, check=False):
    n = 0
    for k in range(kt):
        for w, x in ((w_hi, x_hi), (w_hi, x_lo), (w_lo, x_hi)):
            ins = pe.matmul(out, w(k), x(k), start=first and n == 0, stop=last and n == 3 * kt - 1,
                            skip_group_check=check)
            n += 1
    return ins


def standardise(nc, x_sb, mean_rstd, load, tag):
    LOADS = TILES // 4
    with ExitStack() as ctx:
        ctx.callback(nc.all_engine_barrier)
        def sem(name):
            return new_semaphore(nc, ctx, f"{tag}_{name}")
        stats = ctx.enter_context(nc.sbuf_tensor(f"{tag}_stats", [P, 2, 6], F32))
        x_in = [sem(f"x_in{c}") for c in range(LOADS)]
        stats_step, aggr_step = sem("stats_step"), sem("aggr_step")
        stats_done, root_done, mr_done = sem("stats_done"), sem("root_done"), sem("mr_done")
        block = ctx.enter_context(nc.Block())

        @block.sync
        def _(sp):
            for c in range(LOADS):
                load(sp, c).then_inc(x_in[c], 16)

        @block.vector
        def _(dve):
            for t in range(TILES):
                dve.wait_ge(x_in[t // 4], 16)
                dve.bn_stats(stats[:, t % 2, :], x_sb[:, t, :]).then_inc(stats_step, 1)
                dve.wait_ge(stats_step, t + 1)
                dve.bn_aggr(mean_rstd[:, t, :], stats[:, t % 2, :]).then_inc(aggr_step, 1)
            dve.wait_ge(aggr_step, TILES)
            ins = dve.tensor_scalar(mean_rstd[:, :, 1], mean_rstd[:, :, 1], EPS, None, ALU.add)
            ins.then_inc(stats_done, 1)
            dve.wait_ge(root_done, 1)
            dve.reciprocal(mean_rstd[:, :, 1], mean_rstd[:, :, 1]).then_inc(mr_done, 1)
            dve.wait_ge(mr_done, 1)

        @block.scalar
        def _(act):
            act.wait_ge(stats_done, 1)
            act.activation(mean_rstd[:, :, 1], mean_rstd[:, :, 1], ACT.Sqrt).then_inc(root_done, 1)


def split_weights(nc, tag, pairs, loads, scale=()):
    with ExitStack() as ctx:
        ctx.callback(nc.all_engine_barrier)
        w_in = new_semaphore(nc, ctx, f"{tag}_w_in")
        hi_done = new_semaphore(nc, ctx, f"{tag}_hi_done")
        lo_done = new_semaphore(nc, ctx, f"{tag}_lo_done")
        scaled = new_semaphore(nc, ctx, f"{tag}_scaled")
        block = ctx.enter_context(nc.Block())

        @block.sync
        def _(sp):
            for dst, src in loads:
                sp.dma_start(dst, src).then_inc(w_in, 16)

        @block.vector
        def _(dve):
            dve.wait_ge(w_in, 16 * len(loads))
            for dst, src, factor in scale:
                dve.tensor_scalar(dst, src, factor, None, ALU.mult).then_inc(scaled, 1)
            if scale:
                dve.wait_ge(scaled, len(scale))
            for raw, hi, lo in pairs:
                dve.tensor_copy(hi, raw).then_inc(hi_done, 1)
            for n, (raw, hi, lo) in enumerate(pairs):
                dve.wait_ge(hi_done, n + 1)
                dve.tensor_tensor(lo, raw, hi.bitcast(F32), ALU.subtract).then_inc(lo_done, 1)
            if pairs:
                dve.wait_ge(lo_done, len(pairs))


def normalise_and_transpose(nc, tag, x_sb, mean_rstd, XT_hi, XT_lo, logits, wr_hi, wr_lo, NE, ident,
                            extra=None, qkv=None):
    with ExitStack() as ctx:
        ctx.callback(nc.all_engine_barrier)
        def sem(name):
            return new_semaphore(nc, ctx, f"{tag}_{name}")

        def sb(name, shape, dt=F32):
            return ctx.enter_context(nc.sbuf_tensor(f"{tag}_{name}", shape, dt))

        def ps(name, shape):
            return [ctx.enter_context(nc.psum_tensor(f"{tag}_{name}{i}", shape, F32)) for i in range(2)]
        xn = sb("xn", [P, 2, HID])
        st_hi, st_lo = sb("st_hi", [P, 2, HID], F32R), sb("st_lo", [P, 2, HID], F32R)
        psT, psL = ps("psT", [P, HID]), ps("psL", [P, CHUNK])
        xn_done, xT_done, hi_done, lo_done = (sem(x) for x in ("xn_done", "xT_done", "hi_done", "lo_done"))
        stored = [sem("stored0"), sem("stored1")]
        logits_done, logits_out = sem("logits_done"), sem("logits_out")
        if extra:
            e = extra
            psQ, psR = ps("psQ", [P, 512]), ps("psR", [P, QK_HEADS * D])
            qk = sb("qk", [P, 2, QK_HEADS * D])
            rot_a, rot_b, rot = (sb(x, [P, 2, QK_HEADS * D]) for x in ("rot_a", "rot_b", "rot"))
            sq = sb("sq", [P, 2, QK_HEADS * D])
            rotT = sb("rotT", [P, 2, QK_HEADS * D])
            n2 = sb("n2", [P, 2, QK_HEADS])
            qkv_done, qk_out, v_out, rot_parts, rot_done = (sem(x) for x in ("qkv_done", "qk_out", "v_out", "rot_parts", "rot_done"))
            sq_done, n2_done, n2_out, rotT_done, rotT_out, p_done, p_out = (
                sem(x) for x in ("sq_done", "n2_done", "n2_out", "rotT_done", "rotT_out", "p_done", "p_out"))
        if qkv:
            psK, psV = ps("psK", [P, QK_TILES * P]), ps("psV", [P, HID])
            qk_f = sb("qk_f", [P, 2, QK_TILES, P])
            qk_hi, qk_lo = sb("qk_hi", [P, 2, QK_TILES, P], F32R), sb("qk_lo", [P, 2, QK_TILES, P], F32R)
            v_st = sb("v_st", [P, 2, HEADS, STRIP])
            pads_done, qk_done, v_done, qkf_out, qkhi_out, qklo_out, vst_out = (
                sem(x) for x in ("pads_done", "qk_done", "v_done", "qkf_out", "qkhi_out", "qklo_out", "vst_out"))
            qkv_stored = [sem("qkv_stored0"), sem("qkv_stored1")]
        block = ctx.enter_context(nc.Block())

        def tiles(front, back):
            def loop(eng):
                front(0, 0)
                front(1, 1)
                back(0, 0)
                front(2, 0)
                back(1, 1)
                with eng.Fori(1, TILES // 2 - 1) as i:
                    front(i * 2 + 1, 1)
                    back(i * 2, 0)
                    front(i * 2 + 2, 0)
                    back(i * 2 + 1, 1)
                front(TILES - 1, 1)
                back(TILES - 2, 0)
                back(TILES - 1, 1)
            return loop

        def nothing(t, b):
            pass

        def late(t):
            return not (isinstance(t, int) and t < 2)

        @block.sync
        def _(sp):
            def store(t, b):
                t0 = sp.snap(t * P) if not isinstance(t, int) else t * P
                sp.wait_ge(lo_done, t + 1)
                for st, XT in ((st_hi, XT_hi), (st_lo, XT_lo)):
                    sp.dma_start(XT[:, :, bass.ds(t0, P)].bitcast(F32),
                                 st[:, b, :].rearrange("p (k n) -> p k n", k=KT).bitcast(F32)).then_inc(stored[b], 16)
                if qkv:
                    sp.wait_ge(qklo_out, t + 1)
                    for n, st in enumerate((qk_hi, qk_lo)):
                        sp.dma_start(qkv["qk"][n, :, :, bass.ds(t0, P)].rearrange("m p n -> p m n"),
                                     st[:, b, :, :].bitcast(F32)).then_inc(qkv_stored[b], 16)
                    sp.wait_ge(vst_out, t + 1)
                    sp.dma_start(qkv["v"][bass.ds(t0, P), :], v_st[:, b, :, :].rearrange("p h c -> p (h c)"))\
                        .then_inc(qkv_stored[b], 16)
            tiles(nothing, store)(sp)
            for b in range(2):
                sp.wait_ge(stored[b], 16 * TILES)
                if qkv:
                    sp.wait_ge(qkv_stored[b], 24 * TILES)

        @block.vector
        def _(dve):
            def front(t, b):
                if isinstance(t, int) and t < 2:
                    pass
                else:
                    dve.wait_ge(xT_done, t - 1)
                dve.tensor_scalar(xn[:, b, :], x_sb[:, bass.ds(t, 1), :].rearrange("p a n -> p (a n)"),
                                  mean_rstd[:, bass.ds(t, 1), 0], mean_rstd[:, bass.ds(t, 1), 1],
                                  ALU.subtract, ALU.mult).then_inc(xn_done, 1)
                dve.wait_ge(hi_done, t + 1)
                dve.tensor_tensor(st_lo[:, b, :], psT[b][:], st_hi[:, b, :].bitcast(F32), ALU.subtract)\
                   .then_inc(lo_done, 1)

            def back(t, b):
                if qkv:
                    dve.wait_ge(qk_done, t + 1)
                    if late(t):
                        dve.wait_ge(qkhi_out, t - 1)
                    dve.tensor_tensor(qk_f[:, b, :, :], psK[b][:].rearrange("p (m n) -> p m n", n=P),
                                      qkv["bias_qk"][:].unsqueeze(2).broadcast_to([P, QK_TILES, P]), ALU.add).then_inc(qkf_out, 1)
                    dve.wait_ge(v_done, t + 1)
                    if late(t):
                        dve.wait_ge(qkv_stored[b], (t - b) * 24)
                    dve.tensor_tensor(v_st[:, b, :, 0:D], psV[b][:].rearrange("p (h d) -> p h d", d=D),
                                      qkv["bias_v"][:].rearrange("p (h d) -> p h d", d=D), ALU.add).then_inc(vst_out, 1)
                    dve.wait_ge(qkhi_out, t + 1)
                    dve.tensor_tensor(qk_lo[:, b, :, :], qk_f[:, b, :, :], qk_hi[:, b, :, :].bitcast(F32), ALU.subtract)\
                       .then_inc(qklo_out, 1)
                if not extra:
                    return
                dve.wait_ge(qkv_done, t + 1)
                if not (isinstance(t, int) and t < 2):
                    dve.wait_ge(rot_done, t - 1)
                nq = QK_HEADS * D
                dve.tensor_tensor(qk[:, b, :], psQ[b][:, 0:nq], e["bias"][:, 0:nq], ALU.add).then_inc(qk_out, 1)
                dve.tensor_tensor(e["v"][:, bass.ds(t, 1), :].rearrange("p a n -> p (a n)"), psQ[b][:, nq:512],
                                  e["bias"][:, nq:512], ALU.add).then_inc(v_out, 1)
                dve.wait_ge(rot_done, t + 1)
                dve.tensor_tensor(sq[:, b, :], rot[:, b, :], rot[:, b, :], ALU.mult).then_inc(sq_done, 1)
                dve.wait_ge(sq_done, t + 1)
                dve.tensor_reduce(n2[:, b, :], sq[:, b, :].rearrange("p (h d) -> p h d", d=D), AX.X, ALU.add)\
                   .then_inc(n2_done, 1)
                dve.wait_ge(n2_done, t + 1)
                dve.tensor_copy(e["n2"][:, bass.ds(t, 1), :].rearrange("p a n -> p (a n)"), n2[:, b, :])\
                   .then_inc(n2_out, 1)
            if qkv:
                dve.wait_ge(pads_done, 4)
            tiles(front, back)(dve)
            if extra:
                dve.wait_ge(v_out, TILES)
                dve.wait_ge(n2_out, TILES)

        @block.scalar
        def _(act):
            def front(t, b):
                act.wait_ge(xT_done, t + 1)
                if not (isinstance(t, int) and t < 2):
                    act.wait_ge(stored[b], (t - b) * 16)
                act.activation(st_hi[:, b, :], psT[b][:], ACT.Copy).then_inc(hi_done, 1)
                act.wait_ge(logits_done, t + 1)
                act.activation(logits[:, bass.ds(t, 1), :].rearrange("p a n -> p (a n)"), psL[b][:, 0:NE], ACT.Copy)\
                   .then_inc(logits_out, 1)

            def back(t, b):
                if qkv:
                    act.wait_ge(qkf_out, t + 1)
                    if late(t):
                        act.wait_ge(qkv_stored[b], (t - b) * 24)
                    act.activation(qk_hi[:, b, :, :], qk_f[:, b, :, :], ACT.Copy).then_inc(qkhi_out, 1)
                if not extra:
                    return
                act.wait_ge(rotT_done, t + 1)
                act.activation(rotT[:, b, :], psR[b][:], ACT.Copy).then_inc(rotT_out, 1)
                act.wait_ge(p_done, t + 1)
                act.activation(e["proj"][:, bass.ds(t, 1), :].rearrange("p a n -> p (a n)"),
                               psL[b][:, 64:64 + QK_HEADS * RF], ACT.Copy).then_inc(p_out, 1)
            tiles(front, back)(act)

        if qkv:
            @block.gpsimd
            def _(pool):
                for b in range(2):
                    pool.memset(v_st[:, b, :, D:D + 1], 1.0).then_inc(pads_done, 1)
                    pool.memset(v_st[:, b, :, D + 1:STRIP], 0.0).then_inc(pads_done, 1)

        if extra:
            @block.gpsimd
            def _(pool):
                def rotate(t, b, pos):
                    pool.wait_ge(qk_out, t + 1)
                    if not (isinstance(t, int) and t < 2):
                        pool.wait_ge(rotT_done, t - 1)
                        pool.wait_ge(sq_done, t - 1)
                    cos = e["cos"][:, pos, :].unsqueeze(1).broadcast_to([P, QK_HEADS, D])
                    q3 = qk[:, b, :].rearrange("p (h d) -> p h d", d=D)
                    a3 = rot_a[:, b, :].rearrange("p (h d) -> p h d", d=D)
                    b3 = rot_b[:, b, :].rearrange("p (h d) -> p h d", d=D)
                    pool.tensor_tensor(a3, q3, cos, ALU.mult).then_inc(rot_parts, 1)
                    for half in range(2):
                        sin = e["sin"][:, pos, half * RF:half * RF + RF].unsqueeze(1).broadcast_to([P, QK_HEADS, RF])
                        other = (1 - half) * RF
                        pool.tensor_tensor(b3[:, :, half * RF:half * RF + RF], q3[:, :, other:other + RF], sin, ALU.mult)\
                            .then_inc(rot_parts, 1)
                    pool.wait_ge(rot_parts, t * 3 + 3)
                    pool.tensor_tensor(rot[:, b, :], rot_a[:, b, :], rot_b[:, b, :], ALU.add).then_inc(rot_done, 1)
                for pos in range(POS_TILES):
                    rotate(pos, pos % 2, pos)
                with pool.Fori(1, BATCH) as i:
                    for pos in range(POS_TILES):
                        rotate(i * POS_TILES + pos, pos % 2, pos)

        @block.tensor
        def _(pe):
            def front(t, b):
                pe.wait_ge(xn_done, t + 1)
                if not (isinstance(t, int) and t < 2):
                    pe.wait_ge(lo_done, t - 1)
                for k in range(KT):
                    ins = pe.transpose(psT[b][:, k * P:(k + 1) * P], xn[:, b, k * P:(k + 1) * P], ident[:])
                ins.then_inc(xT_done, 1)
                pe.wait_ge(lo_done, t + 1)
                x_hi = lambda k: st_hi[:, b, k * P:(k + 1) * P]
                x_lo = lambda k: st_lo[:, b, k * P:(k + 1) * P]
                if not (isinstance(t, int) and t < 2):
                    pe.wait_ge(p_out if extra else logits_out, t - 1)
                three_passes(pe, psL[b][:, 0:NE], x_hi, x_lo, lambda k: wr_hi[:, k, :], lambda k: wr_lo[:, k, :], KT)\
                    .then_inc(logits_done, 1)
                if extra:
                    if not (isinstance(t, int) and t < 2):
                        pe.wait_ge(v_out, t - 1)
                    three_passes(pe, psQ[b][:], x_hi, x_lo, lambda k: e["w_hi"][:, k, :], lambda k: e["w_lo"][:, k, :], KT)\
                        .then_inc(qkv_done, 1)
                if qkv:
                    if late(t):
                        pe.wait_ge(qkf_out, t - 1)
                        pe.wait_ge(vst_out, t - 1)
                    for m in range(QK_TILES):
                        ins = three_passes(pe, psK[b][:, m * P:(m + 1) * P], lambda k: qkv["w_hi"][:, k, m * P:(m + 1) * P],
                                           lambda k: qkv["w_lo"][:, k, m * P:(m + 1) * P], x_hi, x_lo, KT)
                    ins.then_inc(qk_done, 1)
                    three_passes(pe, psV[b][:], x_hi, x_lo, lambda k: qkv["w_hi"][:, k, QK_TILES * P:],
                                 lambda k: qkv["w_lo"][:, k, QK_TILES * P:], KT).then_inc(v_done, 1)

            def back(t, b):
                if not extra:
                    return
                pe.wait_ge(rot_done, t + 1)
                for k in range(3):
                    ins = pe.transpose(psR[b][:, k * P:(k + 1) * P], rot[:, b, k * P:(k + 1) * P], ident[:])
                ins.then_inc(rotT_done, 1)
                pe.wait_ge(rotT_out, t + 1)
                pe.wait_ge(logits_out, t + 1)
                for k in range(3):
                    ins = pe.matmul(psL[b][:, 64 + k * 64:128 + k * 64], rotT[:, b, k * P:(k + 1) * P], e["rblk"][:],
                                    start=k == 0, stop=True, skip_group_check=True)
                ins.then_inc(p_done, 1)
            tiles(front, back)(pe)


def linear_attention(nc, e, o_dram):
    NQ = HEADS * D
    with ExitStack() as ctx:
        ctx.callback(nc.all_engine_barrier)
        def sem(name):
            return new_semaphore(nc, ctx, f"la_{name}")

        def sb(name, shape, dt=F32):
            return ctx.enter_context(nc.sbuf_tensor(f"la_{name}", shape, dt))
        arg, whole, feat = (sb(x, [P, 2, QK_HEADS, D]) for x in ("arg", "whole", "feat"))
        qk_prod = sb("qk_prod", [P, 2, HEADS * KV_HEADS * D])
        av_prod = sb("av_prod", [P, HEADS * D * KV_HEADS])
        A = sb("A", [P, HEADS, KV_HEADS])
        out = sb("out", [P, 2, NQ])
        (steps, root_done, arg_done, feat_done, prod_done, A_done, av_done, out_done) = (
            sem(x) for x in ("steps", "root_done", "arg_done", "feat_done", "prod_done", "A_done", "av_done", "out_done"))
        stored = [sem("stored0"), sem("stored1")]
        block = ctx.enter_context(nc.Block())
        inv = e["n2"]

        def tiles(front, back):
            def loop(eng):
                front(0, 0)
                front(1, 1)
                back(0, 0)
                front(2, 0)
                back(1, 1)
                with eng.Fori(1, TILES // 2 - 1) as i:
                    front(i * 2 + 1, 1)
                    back(i * 2, 0)
                    front(i * 2 + 2, 0)
                    back(i * 2 + 1, 1)
                front(TILES - 1, 1)
                back(TILES - 2, 0)
                back(TILES - 1, 1)
            return loop

        def nothing(t, b):
            pass

        def late(t):
            return not (isinstance(t, int) and t < 2)

        @block.scalar
        def _(act):
            act.activation(inv[:, :, :], inv[:, :, :], ACT.Sqrt).then_inc(root_done, 1)

            def front(t, b):
                act.wait_ge(arg_done, t + 1)
                if late(t):
                    act.wait_ge(prod_done, t - 1)
                act.activation(feat[:, b, :, :], arg[:, b, :, :], ACT.Sin, scale=TWO_PI).then_inc(feat_done, 1)
            tiles(front, nothing)(act)

        @block.gpsimd
        def _(pool):
            def front(t, b):
                pool.wait_ge(feat_done, t + 1)
                if late(t):
                    pool.wait_ge(A_done, t - 1)
                q4 = feat[:, b, 0:HEADS, :].unsqueeze(2).broadcast_to([P, HEADS, KV_HEADS, D])
                k4 = feat[:, b, HEADS:QK_HEADS, :].unsqueeze(1).broadcast_to([P, HEADS, KV_HEADS, D])
                pool.tensor_tensor(qk_prod[:, b, :].rearrange("p (h g d) -> p h g d", g=KV_HEADS, d=D), q4, k4, ALU.mult)\
                    .then_inc(prod_done, 1)
            tiles(front, nothing)(pool)

        @block.vector
        def _(dve):
            s = Steps(dve, steps)
            dve.wait_ge(root_done, 1)
            s.link(dve.tensor_scalar(inv[:, :, :], inv[:, :, :], 1e-6, None, ALU.max))
            s.link(dve.reciprocal(inv[:, :, :], inv[:, :, :]))
            s.link(dve.tensor_scalar(inv[:, :, :], inv[:, :, :], 0.15915494309189535, None, ALU.mult))
            done = 3
            per_front = 3

            def front(t, b):
                s.base, s.n = done + t * per_front, 0
                if late(t):
                    dve.wait_ge(feat_done, t - 1)
                p3 = e["proj"][:, bass.ds(t, 1), :].rearrange("p a (h f) -> p (a h) f", f=RF)
                i3 = inv[:, bass.ds(t, 1), :].rearrange("p a h -> p (a h)").unsqueeze(2).broadcast_to([P, QK_HEADS, RF])
                s.link(dve.tensor_tensor(arg[:, b, :, 0:RF], p3, i3, ALU.mult))
                s.link(dve.tensor_scalar(arg[:, b, :, RF:D], arg[:, b, :, 0:RF], 0.25, None, ALU.add))
                s.link(dve.tensor_scalar(whole[:, b, :, :], arg[:, b, :, :], ROUND, ROUND, ALU.add, ALU.subtract))
                dve.tensor_tensor(arg[:, b, :, :], arg[:, b, :, :], whole[:, b, :, :], ALU.subtract).then_inc(arg_done, 1)

            def back(t, b):
                dve.wait_ge(prod_done, t + 1)
                dve.tensor_reduce(A[:, :, :], qk_prod[:, b, :].rearrange("p (h g d) -> p h g d", g=KV_HEADS, d=D),
                                  AX.X, ALU.add).then_inc(A_done, 1)
                dve.wait_ge(A_done, t + 1)
                v4 = e["v"][:, bass.ds(t, 1), :].rearrange("p a (g d) -> p a d g", d=D).broadcast_to([P, HEADS, D, KV_HEADS])
                a4 = A[:, :, :].unsqueeze(2).broadcast_to([P, HEADS, D, KV_HEADS])
                prod = av_prod[:, :].rearrange("p (h d g) -> p h d g", d=D, g=KV_HEADS)
                dve.tensor_tensor(prod, a4, v4, ALU.mult).then_inc(av_done, 1)
                dve.wait_ge(av_done, t + 1)
                if late(t):
                    dve.wait_ge(stored[b], (t - b) * 8)
                dve.tensor_reduce(out[:, b, :].rearrange("p (h d) -> p h d", d=D), prod, AX.X, ALU.add)\
                   .then_inc(out_done, 1)
            tiles(front, back)(dve)

        @block.sync
        def _(sp):
            with sp.Fori(0, BATCH) as i:
                for pos in range(POS_TILES):
                    t = i * POS_TILES + pos
                    seq = sp.snap(i)
                    sp.wait_ge(out_done, t + 1)
                    sp.dma_start(o_dram[bass.ds(seq, 1), :, pos * P:(pos + 1) * P, :].rearrange("b h s d -> s (b h) d"),
                                 out[:, pos % 2, :].rearrange("p (h d) -> p h d", d=D)).then_inc(stored[pos % 2], 16)
            for b in range(2):
                sp.wait_ge(stored[b], 8 * TILES)


def route(nc, tag, logits, NE, E, TOP, guard, CT, ident):
    T = TILES
    with ExitStack() as ctx:
        ctx.callback(nc.all_engine_barrier)
        def sem(name):
            return new_semaphore(nc, ctx, f"{tag}_{name}")

        def sb(name, shape, dt=F32):
            return ctx.enter_context(nc.sbuf_tensor(f"{tag}_{name}", shape, dt))
        prob, left, same, comb = (sb(x, [P, T, E]) for x in ("prob", "left", "same", "comb"))
        rank = sb("rank", [P, E])
        top, one = sb("top", [P, T]), sb("one", [P, T])
        total = sb("total", [P, T])
        split = sb("split", [P, T, 2 * NE])
        rounded = sb("rounded", [P, T, NE], F32R)
        psC = [ctx.enter_context(nc.psum_tensor(f"{tag}_psC{i}", [2 * NE, CHUNK], F32)) for i in range(2)]
        steps, shifted, exp_done, gate_done, split_done, cT_done, cT_out, rank_done = (
            sem(x) for x in ("steps", "shifted", "exp_done", "gate_done", "split_done", "cT_done", "cT_out", "rank_done"))
        block = ctx.enter_context(nc.Block())

        def over(x):
            return x[:, :].unsqueeze(2).broadcast_to([P, T, E])

        @block.gpsimd
        def _(pool):
            for j in range(E):
                pool.memset(rank[:, j:j + 1], float(E - j)).then_inc(rank_done, 1)

        @block.vector
        def _(dve):
            s = Steps(dve, steps)
            s.link(dve.tensor_reduce(top[:, :], logits[:, :, 0:E], AX.X, ALU.max))
            dve.tensor_tensor(prob[:, :, :], logits[:, :, 0:E], over(top), ALU.subtract).then_inc(shifted, 1)
            dve.wait_ge(exp_done, 1)
            s.link(dve.tensor_reduce(total[:, :], prob[:, :, :], AX.X, ALU.add))
            s.link(dve.reciprocal(total[:, :], total[:, :]))
            s.link(dve.tensor_tensor(prob[:, :, :], prob[:, :, :], over(total), ALU.mult))
            s.link(dve.tensor_copy(left[:, :, :], prob[:, :, :]))
            s.link(dve.memset(comb[:, :, :], 0.0))
            dve.wait_ge(rank_done, E)
            r3 = rank[:, :].unsqueeze(1).broadcast_to([P, T, E])
            for _k in range(TOP):
                s.link(dve.tensor_reduce(top[:, :], left[:, :, :], AX.X, ALU.max))
                s.link(dve.tensor_tensor(same[:, :, :], left[:, :, :], over(top), ALU.is_equal))
                s.link(dve.tensor_tensor(same[:, :, :], same[:, :, :], r3, ALU.mult))
                s.link(dve.tensor_reduce(one[:, :], same[:, :, :], AX.X, ALU.max))
                s.link(dve.tensor_tensor(same[:, :, :], over(one), r3, ALU.is_equal))
                s.link(dve.tensor_tensor(comb[:, :, :], comb[:, :, :], same[:, :, :], ALU.add))
                s.link(dve.scalar_tensor_tensor(left[:, :, :], same[:, :, :], -4.0, left[:, :, :], ALU.mult, ALU.add))
            s.link(dve.tensor_tensor(comb[:, :, :], comb[:, :, :], prob[:, :, :], ALU.mult))
            s.link(dve.tensor_reduce(total[:, :], comb[:, :, :], AX.X, ALU.add))
            if guard:
                s.link(dve.tensor_scalar(total[:, :], total[:, :], guard, None, ALU.add))
            s.link(dve.reciprocal(total[:, :], total[:, :]))
            s.link(dve.tensor_tensor(split[:, :, 0:E], comb[:, :, :], over(total), ALU.mult))
            if NE > E:
                dve.wait_ge(gate_done, 1)
            s.link(dve.tensor_copy(rounded[:, :, :], split[:, :, 0:NE]))
            s.link(dve.tensor_tensor(split[:, :, NE:2 * NE], split[:, :, 0:NE], rounded[:, :, :].bitcast(F32), ALU.subtract))
            dve.tensor_copy(split[:, :, 0:NE], rounded[:, :, :].bitcast(F32)).then_inc(split_done, 1)

        @block.scalar
        def _(act):
            act.wait_ge(shifted, 1)
            act.activation(prob[:, :, :], prob[:, :, :], ACT.Exp).then_inc(exp_done, 1)
            if NE > E:
                act.activation(split[:, :, E:NE], logits[:, :, E:NE], ACT.Sigmoid).then_inc(gate_done, 1)
            for c in range(CHUNKS):
                act.wait_ge(cT_done, c + 1)
                act.activation(CT[:, c * CHUNK:(c + 1) * CHUNK], psC[c % 2][:, :], ACT.Copy).then_inc(cT_out, 1)

        @block.tensor
        def _(pe):
            pe.wait_ge(split_done, 1)
            for c in range(CHUNKS):
                if c >= 2:
                    pe.wait_ge(cT_out, c - 1)
                for j in range(TPC):
                    ins = pe.transpose(psC[c % 2][:, j * P:(j + 1) * P], split[:, c * TPC + j, :], ident[:])
                ins.then_inc(cT_done, 1)


def experts(nc, tag, w_dram, NT, G, NE, XT_hi, XT_lo, CT, acc):
    NG = NT // G
    with ExitStack() as ctx:
        ctx.callback(nc.all_engine_barrier)
        def sem(name):
            return new_semaphore(nc, ctx, f"{tag}_{name}")

        def sb(name, shape, dt=F32):
            return ctx.enter_context(nc.sbuf_tensor(f"{tag}_{name}", shape, dt))
        RAW = 2
        raw = sb("raw", [P, RAW, WTS])
        w_hi, w_lo = sb("w_hi", [P, G, WTS], F32R), sb("w_lo", [P, G, WT], F32R)
        h = sb("h", [P, 2, CHUNK])
        h_hi, h_lo = sb("h_hi", [P, 2, CHUNK], F32R), sb("h_lo", [P, 2, CHUNK], F32R)
        psG, psU, psC = ([ctx.enter_context(nc.psum_tensor(f"{tag}_{n}{i}", [P, CHUNK], F32)) for i in range(2)]
                         for n in ("psG", "psU", "psC"))
        psY = ctx.enter_context(nc.psum_tensor(f"{tag}_psY", [P, TPC, HID], F32))
        raw_in = [sem(f"raw_in{i}") for i in range(RAW)]
        (hiw_done, low_done, up_done, silu_done, gu_done, h_done, hi_done, lo_done, down_done, y_done, y_out, zeroed) = (
            sem(x) for x in ("hiw_done", "low_done", "up_done", "silu_done", "gu_done", "h_done", "hi_done", "lo_done",
                             "down_done", "y_done", "y_out", "zeroed"))
        block = ctx.enter_context(nc.Block())

        @block.sync
        def _(sp):
            for w in range(NT):
                if w >= RAW:
                    sp.wait_ge(low_done, w - RAW + 1)
                sp.dma_start(raw[:, w % RAW, :], w_dram[w]).then_inc(raw_in[w % RAW], 16)

        @block.gpsimd
        def _(pool):
            pool.memset(acc[:, :, :], 0.0).then_inc(zeroed, 1)

        def groups(eng, first, chunk, tail):
            for g in range(NG):
                first(g)
                chunk(g, 1)
                with eng.Fori(1, CHUNKS // 2) as i:
                    chunk(g, i * 2, 0)
                    chunk(g, i * 2 + 1, 1)
                tail(g)

        def step(g, c, j):
            return (g * CHUNKS + c) * G + j

        def b_of(g, cpar, j):
            return (g * CHUNKS * G + cpar * G + j) % 2

        @block.vector
        def _(dve):
            def weights(g, j):
                w = g * G + j
                dve.wait_ge(raw_in[w % RAW], 16 * (w // RAW + 1))
                dve.wait_ge(hiw_done, w + 1)
                dve.tensor_tensor(w_lo[:, j, :], raw[:, w % RAW, 0:WT], w_hi[:, j, 0:WT].bitcast(F32), ALU.subtract)\
                   .then_inc(low_done, 1)

            def tile(g, c, j, b):
                n = step(g, c, j)
                dve.wait_ge(silu_done, n + 1)
                dve.tensor_tensor(h[:, b, :], h[:, b, :], psU[b][:, :], ALU.mult).then_inc(gu_done, 1)
                dve.wait_ge(gu_done, n + 1)
                dve.tensor_tensor(h[:, b, :], h[:, b, :], psC[b][:, :], ALU.mult).then_inc(h_done, 1)
                dve.wait_ge(hi_done, n + 1)
                dve.tensor_tensor(h_lo[:, b, :], h[:, b, :], h_hi[:, b, :].bitcast(F32), ALU.subtract).then_inc(lo_done, 1)

            def collect(g, c):
                m = g * CHUNKS + c
                dve.wait_ge(y_done, m + 1)
                for half in range(2):
                    a = acc[:, bass.ds(c * TPC + 2 * half, 2), :]
                    dve.tensor_tensor(a, a, psY[:, 2 * half:2 * half + 2, :], ALU.add).then_inc(y_out, 1)

            def first(g):
                if g:
                    dve.wait_ge(down_done, step(g, 0, 0))
                for j in range(G):
                    weights(g, j)
                    tile(g, 0, j, b_of(g, 0, j))

            def chunk(g, c, cpar=1):
                for j in range(G):
                    tile(g, c, j, b_of(g, cpar, j))
                    if j == 0:
                        collect(g, c - 1)
            dve.wait_ge(zeroed, 1)
            groups(dve, first, chunk, lambda g: collect(g, CHUNKS - 1))
            dve.wait_ge(y_out, 2 * NG * CHUNKS)

        @block.scalar
        def _(act):
            def weights(g, j):
                w = g * G + j
                act.wait_ge(raw_in[w % RAW], 16 * (w // RAW + 1))
                act.activation(w_hi[:, j, :], raw[:, w % RAW, :], ACT.Copy).then_inc(hiw_done, 1)

            def tile(g, c, j, b):
                n = step(g, c, j)
                act.wait_ge(up_done, n + 1)
                if not (isinstance(n, int) and n < 2):
                    act.wait_ge(lo_done, n - 1)
                act.activation(h[:, b, :], psG[b][:, :], ACT.Silu).then_inc(silu_done, 1)
                act.wait_ge(h_done, n + 1)
                if not (isinstance(n, int) and n < 2):
                    act.wait_ge(down_done, n - 1)
                act.activation(h_hi[:, b, :], h[:, b, :], ACT.Copy).then_inc(hi_done, 1)

            def first(g):
                if g:
                    act.wait_ge(down_done, step(g, 0, 0))
                for j in range(G):
                    weights(g, j)
                    tile(g, 0, j, b_of(g, 0, j))

            def chunk(g, c, cpar=1):
                for j in range(G):
                    tile(g, c, j, b_of(g, cpar, j))
            groups(act, first, chunk, lambda g: None)

        @block.tensor
        def _(pe):
            def up(g, c, j, b):
                n = step(g, c, j)
                if not (isinstance(n, int) and n < 2):
                    pe.wait_ge(h_done, n - 1)
                x_hi = lambda k: XT_hi[:, k, bass.ds(c * CHUNK, CHUNK)]
                x_lo = lambda k: XT_lo[:, k, bass.ds(c * CHUNK, CHUNK)]
                for half, out in ((0, psG[b]), (1, psU[b])):
                    col = lambda k: (half * KT + k) * P
                    three_passes(pe, out[:, :], lambda k: w_hi[:, j, col(k):col(k) + P],
                                 lambda k: w_lo[:, j, col(k):col(k) + P], x_hi, x_lo, KT)
                pe.matmul(psC[b][:, :], w_hi[0:2 * NE, j, WT:WTS], CT[:, bass.ds(c * CHUNK, CHUNK)], start=True, stop=True)\
                    .then_inc(up_done, 1)

            def down(g, c, j, b):
                n = step(g, c, j)
                pe.wait_ge(lo_done, n + 1)
                if j == 0 and not (isinstance(c, int) and g * CHUNKS + c == 0):
                    pe.wait_ge(y_out, (g * CHUNKS + c) * 2)
                for m in range(TPC):
                    ins = three_passes(pe, psY[:, m, :], lambda k: h_hi[:, b, m * P:(m + 1) * P],
                                       lambda k: h_lo[:, b, m * P:(m + 1) * P],
                                       lambda k: w_hi[:, j, 2 * KT * P:WT], lambda k: w_lo[:, j, 2 * KT * P:WT], 1,
                                       first=j == 0 and m % 2 == 0, last=j == G - 1, check=True)
                ins.then_inc(down_done, 1)
                if j == G - 1:
                    pe.wait_ge(down_done, n + 1)
                    pe.sem_inc(y_done, 1)

            def first(g):
                for j in range(G):
                    pe.wait_ge(low_done, g * G + j + 1)
                    up(g, 0, j, b_of(g, 0, j))
                    if j:
                        down(g, 0, j - 1, b_of(g, 0, j - 1))

            def chunk(g, c, cpar=1):
                for j in range(G):
                    up(g, c, j, b_of(g, cpar, j))
                    if j:
                        down(g, c, j - 1, b_of(g, cpar, j - 1))
                    else:
                        down(g, c - 1, G - 1, b_of(g, 1 - cpar, G - 1))
            groups(pe, first, chunk, lambda g: down(g, CHUNKS - 1, G - 1, b_of(g, 1, G - 1)))


def gate_and_add(nc, tag, x_dram, s_dram, acc, out_dram):
    with ExitStack() as ctx:
        ctx.callback(nc.all_engine_barrier)
        def sem(name):
            return new_semaphore(nc, ctx, f"{tag}_{name}")
        STEP = 4
        xt = ctx.enter_context(nc.sbuf_tensor(f"{tag}_xt", [P, 2, STEP, HID], F32))
        stt = ctx.enter_context(nc.sbuf_tensor(f"{tag}_stt", [P, 2, STEP, HID], F32))
        gate = ctx.enter_context(nc.sbuf_tensor(f"{tag}_gate", [P, 2, STEP, HID], F32))
        x_in, s_in = [sem("x_in0"), sem("x_in1")], [sem("s_in0"), sem("s_in1")]
        gate_done, mul_done, sum_done, stored = (sem(x) for x in ("gate_done", "mul_done", "sum_done", "stored"))
        block = ctx.enter_context(nc.Block())
        N = TILES // STEP

        @block.sync
        def _(sp):
            for t in range(N):
                if t >= 2:
                    sp.wait_ge(sum_done, t - 1)
                for src, dst, sems in ((x_dram, xt, x_in), (s_dram, stt, s_in)):
                    sp.dma_start(dst[:, t % 2, :, :], src[t * STEP:(t + 1) * STEP].rearrange("t p n -> p t n"))\
                        .then_inc(sems[t % 2], 16)

        @block.gpsimd
        def _(pool):
            for t in range(N):
                pool.wait_ge(sum_done, t + 1)
                pool.dma_start(out_dram[t * STEP:(t + 1) * STEP].rearrange("t p n -> p t n"),
                               acc[:, t * STEP:(t + 1) * STEP, :]).then_inc(stored, 16)
            pool.wait_ge(stored, 16 * N)

        @block.scalar
        def _(act):
            for t in range(N):
                if t >= 2:
                    act.wait_ge(mul_done, t - 1)
                act.activation(gate[:, t % 2, :, :], acc[:, t * STEP:(t + 1) * STEP, :], ACT.Silu).then_inc(gate_done, 1)

        @block.vector
        def _(dve):
            for t in range(N):
                b = t % 2
                dve.wait_ge(gate_done, t + 1)
                dve.wait_ge(s_in[b], 16 * (t // 2 + 1))
                dve.tensor_tensor(stt[:, b, :, :], stt[:, b, :, :], gate[:, b, :, :], ALU.mult).then_inc(mul_done, 1)
                dve.wait_ge(mul_done, t + 1)
                dve.wait_ge(x_in[b], 16 * (t // 2 + 1))
                dve.tensor_tensor(acc[:, t * STEP:(t + 1) * STEP, :], stt[:, b, :, :], xt[:, b, :, :], ALU.add)\
                   .then_inc(sum_done, 1)


def causal_attention(nc, qk_dram, v_dram, ident, mask_qk, mask_kq, ident_b, m_dram, ao_dram):
    SLOTS = 3
    ROUNDS = GROUPS * BATCH
    with ExitStack() as ctx:
        ctx.callback(nc.all_engine_barrier)

        def sem(name):
            return new_semaphore(nc, ctx, f"ca_{name}")

        def sb(name, shape, dt=F32):
            return ctx.enter_context(nc.sbuf_tensor(f"ca_{name}", shape, dt))
        QS, KS = sb("QS", [PADDED, SLOTS, GH, SEQ], F32R), sb("KS", [PADDED, SLOTS, GH, SEQ], F32R)
        zero_rows = sb("zero_rows", [2, CHUNK])
        VA = sb("VA", [P, SLOTS, POS_TILES, GH * STRIP])
        PT = sb("PT", [P, 2, GH, CHUNK])
        units = [(qt, k0, w, h0, min(CHUNK // w, GH)) for qt in range(POS_TILES)
                 for k0, w in [(k, min(CHUNK, (qt + 1) * P - k)) for k in range(0, (qt + 1) * P, CHUNK)]
                 for h0 in range(0, GH, min(CHUNK // w, GH))]
        NU = len(units)
        steps = [(c, kt, max(kt * P - c * CHUNK, 0)) for c in range(SPAN) for kt in range((c + 1) * TPC)]
        NS = len(steps)
        AHEAD = 6
        last_step = [max(s for s, (c, _, _) in enumerate(steps) if c == cc) for cc in range(SPAN)]
        part = sb("part", [P, SPAN, GH, POS_TILES])
        maxima = sb("maxima", [P, GH, POS_TILES])
        NR = GH * POS_TILES
        m_f, m_hi, m_lo = sb("m_f", [NR, P]), sb("m_hi", [NR, P], F32R), sb("m_lo", [NR, P], F32R)
        OT = sb("OT", [P, CHUNK])
        rsum = sb("rsum", [P, TPC, GH])
        o_sb = sb("o_sb", [P, 2, TPC, GH, D])
        psM = [ctx.enter_context(nc.psum_tensor(f"ca_psM{i}", [P, CHUNK], F32)) for i in range(2)]
        psS = [ctx.enter_context(nc.psum_tensor(f"ca_psS{i}", [P, 2, CHUNK], F32)) for i in range(2)]
        psO = ctx.enter_context(nc.psum_tensor("ca_psO", [P, CHUNK], F32))
        psX = ctx.enter_context(nc.psum_tensor("ca_psX", [P, CHUNK], F32))
        (ones_done, zeros_done, unit_done, unit_out, whole_done, mT_done, m_neg, mhi_done, mlo_done, s_done, exp_done, pv_done,
         ot_out, oT_done, sum_done, o_out, m_kept) = (sem(x) for x in (
             "ones_done", "zeros_done", "unit_done", "unit_out", "whole_done", "mT_done", "m_neg", "mhi_done", "mlo_done",
             "s_done", "exp_done", "pv_done", "ot_out", "oT_done", "sum_done", "o_out", "m_kept"))
        stack_in = [sem(f"stack_in{i}") for i in range(SLOTS)]
        m_in = [sem(f"m_in{i}") for i in range(SLOTS)]
        ao_stored = [sem("ao_stored0"), sem("ao_stored1")]
        LOADS = 10
        block = ctx.enter_context(nc.Block())

        def rounds(eng, both, front, back):
            front(0, 0)
            both(0, 0)
            both(1, 1)
            both(2, 2)
            with eng.Fori(1, (ROUNDS - 1) // SLOTS) as i:
                for slot in range(SLOTS):
                    both(i * SLOTS + slot, slot)
            back(ROUNDS - 1, (ROUNDS - 1) % SLOTS)

        def pull(eng, n, slot, g, b):
            pos = bass.ds(b * SEQ, SEQ) if isinstance(b, int) else bass.ds(b, SEQ)
            rows = g * (GH * D)
            for dst, first, order in ((QS, 0, (0, 0, 1, 1)), (KS, KT, (0, 1, 0, 1))):
                for r, half in enumerate(order):
                    src = qk_dram[half, :, :, pos].rearrange("m p n -> (m p) n")
                    if isinstance(rows, int):
                        src = src[first * P + rows:first * P + rows + GH * D, :]
                    else:
                        src = src[bass.ds(rows + first * P, GH * D), :]
                    eng.dma_start(dst[r * D:(r + 1) * D, slot, :, :].bitcast(F32),
                                  src.rearrange("(h r) n -> r h n", h=GH)).then_inc(stack_in[slot], 16)
            eng.dma_start(QS[STACK:ROWS, slot, :, :].rearrange("r h (c n) -> r (h c) n", n=CHUNK).bitcast(F32),
                          zero_rows[:, :].unsqueeze(1).broadcast_to([2, GH * SPAN, CHUNK]))\
               .then_inc(stack_in[slot], 16)
            v = v_dram[pos, :].rearrange("(t p) c -> p t c", p=P)
            cols = g * (GH * STRIP)
            v = v[:, :, cols:cols + GH * STRIP] if isinstance(cols, int) else v[:, :, bass.ds(cols, GH * STRIP)]
            eng.dma_start(VA[:, slot, :, :], v).then_inc(stack_in[slot], 16)

        @block.sync
        def _(sp):
            sp.wait_ge(zeros_done, 1 + 2 * SLOTS)
            for n in range(ROUNDS):
                g, b = divmod(n, BATCH)
                if n >= SLOTS:
                    sp.wait_ge(oT_done, (n - SLOTS + 1) * SPAN)
                pull(sp, n, n % SLOTS, g, b)

        @block.gpsimd
        def _(pool):
            pool.memset(zero_rows[:, :], 0.0).then_inc(zeros_done, 1)
            for slot in range(SLOTS):
                pool.memset(QS[STACK:PADDED, slot, :, :].bitcast(F32), 0.0).then_inc(zeros_done, 1)
                pool.memset(KS[STACK:PADDED, slot, :, :].bitcast(F32), 0.0).then_inc(zeros_done, 1)
            pool.wait_ge(zeros_done, 1 + 2 * SLOTS)
            for slot in range(SLOTS):
                pool.memset(KS[STACK:ROWS, slot, :, :].bitcast(F32), 1.0).then_inc(ones_done, 1)

            def maxima_rows(n, slot):
                pool.wait_ge(mlo_done, n + 1)
                for r, m in enumerate((m_hi, m_lo)):
                    pool.dma_start(m_dram[r], m[:, :].bitcast(F32)).then_inc(m_kept, 16)
                pool.wait_ge(m_kept, (n + 1) * 32)
                pool.dma_start(QS[STACK:ROWS, slot, :, :].rearrange("r h n -> r (h n)").bitcast(F32),
                               m_dram.rearrange("r m p -> r (m p)")).then_inc(m_in[slot], 16)

            def outputs(n):
                g, b = divmod(n, BATCH)
                for c in range(SPAN):
                    pool.wait_ge(o_out, n * SPAN + c + 1)
                    t0 = b * POS_TILES + c * TPC
                    pool.dma_start(ao_dram[t0:t0 + TPC, :, g * GH * D:(g + 1) * GH * D].rearrange("t p c -> p t c"),
                                   o_sb[:, c, :, :, :].rearrange("p t h d -> p t (h d)")).then_inc(ao_stored[c], 16)
            maxima_rows(0, 0)
            for n in range(ROUNDS):
                if n + 1 < ROUNDS:
                    maxima_rows(n + 1, (n + 1) % SLOTS)
                outputs(n)
            for c in range(SPAN):
                pool.wait_ge(ao_stored[c], 16 * ROUNDS)

        @block.vector
        def _(dve):
            def unit(n, u):
                qt, k0, w, h0, nh = units[u]
                dve.wait_ge(unit_done, n * NU + u + 1)
                dst = part[:, k0 // CHUNK, h0:h0 + nh, qt]
                dve.tensor_reduce(dst, psM[u % 2][:, 0:nh * w].rearrange("p (h k) -> p h k", h=nh), AX.X, ALU.max)\
                   .then_inc(unit_out, 1)

            def whole(n):
                dve.wait_ge(unit_out, n * NU + NU)
                first, second = part[:, 0, :, :], part[:, 1, :, TPC:]
                if not (isinstance(n, int) and n == 0):
                    dve.wait_ge(mT_done, n)
                dve.tensor_copy(maxima[:, :, 0:TPC], first[:, :, 0:TPC]).then_inc(whole_done, 1)
                dve.tensor_tensor(maxima[:, :, TPC:], first[:, :, TPC:], second, ALU.max).then_inc(whole_done, 1)
                dve.wait_ge(mT_done, n + 1)
                if not (isinstance(n, int) and n == 0):
                    slot_of_last(n)
                dve.tensor_scalar(m_f[:, :], psX[0:NR, 0:P], -1.0, None, ALU.mult).then_inc(m_neg, 1)
                dve.wait_ge(m_neg, n + 1)
                dve.tensor_copy(m_hi[:, :], m_f[:, :]).then_inc(mhi_done, 1)
                dve.wait_ge(mhi_done, n + 1)
                dve.tensor_tensor(m_lo[:, :], m_f[:, :], m_hi[:, :].bitcast(F32), ALU.subtract).then_inc(mlo_done, 1)

            def slot_of_last(n):
                dve.wait_ge(s_done, (n - 1) * (2 * NS) + 1)

            def collect(n, c):
                dve.wait_ge(pv_done, n * NS + last_step[c] + 1)
                dve.tensor_copy(OT[:, :], psO[:, :]).then_inc(ot_out, 1)

            def divide(n, c):
                dve.wait_ge(oT_done, n * SPAN + c + 1)
                o4 = psX[:, :].rearrange("p (q h d) -> p q h d", q=TPC, h=GH)
                dve.reciprocal(rsum[:, :, :], o4[:, :, :, D]).then_inc(sum_done, 1)
                dve.wait_ge(sum_done, n * SPAN + c + 1)
                if not (isinstance(n, int) and n == 0):
                    dve.wait_ge(ao_stored[c], n * 16)
                dve.tensor_tensor(o_sb[:, c, :, :, :], o4[:, :, :, 0:D], rsum[:, :, :].unsqueeze(3).broadcast_to([P, TPC, GH, D]),
                                  ALU.mult).then_inc(o_out, 1)

            def both(n, slot):
                done = 0
                for s in range(NS):
                    upto = min(NU, NU * (s + 1) // AHEAD)
                    for u in range(done, upto):
                        unit(n + 1, u)
                    done = upto
                    if s == last_step[0] + 1:
                        collect(n, 0)
                    if s == last_step[0] + 2:
                        divide(n, 0)
                    if s == AHEAD:
                        whole(n + 1)
                collect(n, 1)
                divide(n, 1)

            def front(n, slot):
                for u in range(NU):
                    unit(n, u)
                whole(n)

            def back(n, slot):
                for c in range(SPAN):
                    collect(n, c)
                    divide(n, c)
            rounds(dve, both, front, back)

        @block.scalar
        def _(act):
            def exps(n):
                for s, (c, kt, off) in enumerate(steps):
                    for pair in range(2):
                        act.wait_ge(s_done, n * (2 * NS) + 2 * s + pair + 1)
                        if s >= 2 or not (isinstance(n, int) and n == 0):
                            act.wait_ge(pv_done, n * NS + s - 1)
                        act.activation(PT[:, s % 2, 2 * pair:2 * pair + 2, off:CHUNK], psS[pair][:, :, off:CHUNK], ACT.Exp)\
                           .then_inc(exp_done, 1)
            rounds(act, lambda n, slot: exps(n), lambda n, slot: None, lambda n, slot: exps(n))

        @block.tensor
        def _(pe):
            def unit(n, slot, u):
                qt, k0, w, h0, nh = units[u]
                if u >= 2 or not (isinstance(n, int) and n == 0):
                    pe.wait_ge(unit_out, n * NU + u - 1)
                diag = k0 + w == (qt + 1) * P
                for h in range(nh):
                    out = psM[u % 2][:, h * w:(h + 1) * w]
                    ins = pe.matmul(out, QS[:, slot, h0 + h, qt * P:(qt + 1) * P], KS[:, slot, h0 + h, k0:k0 + w],
                                    start=True, stop=not diag, skip_group_check=True)
                    if diag:
                        ins = pe.matmul(out[:, w - P:w], ident_b[:, :], mask_qk[:, :], start=False, stop=True,
                                        skip_group_check=True)
                ins.then_inc(unit_done, 1)

            def transpose_maxima(n):
                pe.wait_ge(whole_done, n * 2 + 2)
                if not (isinstance(n, int) and n == 0):
                    pe.wait_ge(o_out, (n - 1) * SPAN + 1)
                pe.transpose(psX[0:NR, 0:P], maxima[:, :, :].rearrange("p h t -> p (h t)"), ident[:, :]).then_inc(mT_done, 1)

            def scores(n, slot, s):
                c, kt, off = steps[s]
                for pair in range(2):
                    if s >= 1 or not (isinstance(n, int) and n == 0):
                        pe.wait_ge(exp_done, n * (2 * NS) + 2 * (s - 1) + pair + 1)
                    diag = kt * P >= c * CHUNK
                    for j in range(2):
                        h = 2 * pair + j
                        ins = pe.matmul(psS[pair][:, j, off:CHUNK], KS[:, slot, h, kt * P:(kt + 1) * P],
                                        QS[:, slot, h, c * CHUNK + off:(c + 1) * CHUNK], start=True, stop=not diag,
                                        skip_group_check=True)
                        if diag:
                            ins = pe.matmul(psS[pair][:, j, off:off + P], ident_b[:, :], mask_kq[:, :], start=False, stop=True,
                                            skip_group_check=True)
                    ins.then_inc(s_done, 1)

            def values(n, slot, s):
                c, kt, off = steps[s]
                pe.wait_ge(exp_done, n * (2 * NS) + 2 * s + 2)
                if kt == 0 and not (isinstance(n, int) and n == 0 and c == 0):
                    pe.wait_ge(ot_out, n * SPAN + c)
                for h in range(GH):
                    ins = pe.matmul(psO[STRIP * h:STRIP * (h + 1), off:CHUNK], VA[:, slot, kt, STRIP * h:STRIP * (h + 1)],
                                    PT[:, s % 2, h, off:CHUNK], start=kt == 0, stop=s == last_step[c],
                                    tile_position=(0, STRIP * h), skip_group_check=True)
                ins.then_inc(pv_done, 1)

            def transpose_out(n, c):
                pe.wait_ge(ot_out, n * SPAN + c + 1)
                if c == 0:
                    if not (isinstance(n, int) and n == 0):
                        pe.wait_ge(o_out, n * SPAN)
                else:
                    pe.wait_ge(o_out, n * SPAN + 1)
                    if not (isinstance(n, int) and n == ROUNDS - 1):
                        pe.wait_ge(m_neg, n + 2)
                for q in range(TPC):
                    ins = pe.transpose(psX[:, q * P:(q + 1) * P], OT[:, q * P:(q + 1) * P], ident[:, :])
                ins.then_inc(oT_done, 1)

            def front(n, slot):
                pe.wait_ge(stack_in[slot], 16 * LOADS)
                for u in range(NU):
                    unit(n, slot, u)
                transpose_maxima(n)

            def both(n, slot, turn=None):
                nxt = (slot + 1) % SLOTS
                pe.wait_ge(m_in[slot], turn[0] * 16 + 16)
                pe.wait_ge(stack_in[nxt], turn[1] * (16 * LOADS) + 16 * LOADS)
                done = 0
                for s in range(NS):
                    upto = min(NU, NU * (s + 1) // AHEAD)
                    for u in range(done, upto):
                        unit(n + 1, nxt, u)
                    done = upto
                    scores(n, slot, s)
                    if s:
                        values(n, slot, s - 1)
                    if s == last_step[0] + 2:
                        transpose_out(n, 0)
                    if s == AHEAD:
                        transpose_maxima(n + 1)
                values(n, slot, NS - 1)
                transpose_out(n, 1)

            def back(n, slot):
                pe.wait_ge(m_in[slot], n // SLOTS * 16 + 16)
                for s in range(NS):
                    scores(n, slot, s)
                    if s:
                        values(n, slot, s - 1)
                    if s == last_step[0] + 2:
                        transpose_out(n, 0)
                values(n, slot, NS - 1)
                transpose_out(n, 1)
            pe.wait_ge(ones_done, SLOTS)
            front(0, 0)
            for n in range(SLOTS):
                both(n, n, (0, (n + 1) // SLOTS))
            with pe.Fori(1, (ROUNDS - 1) // SLOTS) as i:
                for slot in range(SLOTS):
                    both(i * SLOTS + slot, slot, (i, i + (slot + 1) // SLOTS))
            back(ROUNDS - 1, (ROUNDS - 1) % SLOTS)


def project_out(nc, tag, o_tile, s_dram, ident, wo, bo, scale):
    with ExitStack() as ctx:
        ctx.callback(nc.all_engine_barrier)
        def sem(name):
            return new_semaphore(nc, ctx, f"{tag}_{name}")
        o_st = ctx.enter_context(nc.sbuf_tensor(f"{tag}_o_st", [P, 2, HID], F32))
        oT = ctx.enter_context(nc.sbuf_tensor(f"{tag}_oT", [P, 2, HID], F32))
        s_sb = ctx.enter_context(nc.sbuf_tensor(f"{tag}_s_sb", [P, 2, HID], F32))
        psT = [ctx.enter_context(nc.psum_tensor(f"{tag}_psT{i}", [P, HID], F32)) for i in range(2)]
        psS = [ctx.enter_context(nc.psum_tensor(f"{tag}_psS{i}", [P, HID], F32)) for i in range(2)]
        oT_done, oT_out, s_done, s_out = (sem(x) for x in ("oT_done", "oT_out", "s_done", "s_out"))
        staged = [sem("staged0"), sem("staged1")]
        stored = [sem("stored0"), sem("stored1")]
        block = ctx.enter_context(nc.Block())

        def tiles(eng, body):
            body(0, 0)
            body(1, 1)
            with eng.Fori(1, TILES // 2) as i:
                body(i * 2, 0)
                body(i * 2 + 1, 1)

        def late(t):
            return not isinstance(t, int)

        @block.gpsimd
        def _(pool):
            def body(t, b):
                if late(t):
                    pool.wait_ge(oT_done, t - 1)
                pool.dma_start(o_st[:, b, :], o_tile(t)).then_inc(staged[b], 16)
            tiles(pool, body)

        @block.tensor
        def _(pe):
            def body(t, b):
                pe.wait_ge(staged[b], (t - b) * 8 + 16)
                if late(t):
                    pe.wait_ge(oT_out, t - 1)
                for k in range(KT):
                    ins = pe.transpose(psT[b][:, k * P:(k + 1) * P], o_st[:, b, k * P:(k + 1) * P], ident[:])
                ins.then_inc(oT_done, 1)
                pe.wait_ge(oT_out, t + 1)
                if late(t):
                    pe.wait_ge(s_out, t - 1)
                for k in range(KT):
                    ins = pe.matmul(psS[b][:], oT[:, b, k * P:(k + 1) * P], wo[:, k, :], start=k == 0, stop=k == KT - 1)
                ins.then_inc(s_done, 1)
            tiles(pe, body)

        @block.scalar
        def _(act):
            def body(t, b):
                act.wait_ge(oT_done, t + 1)
                if late(t):
                    act.wait_ge(s_done, t - 1)
                act.activation(oT[:, b, :], psT[b][:], ACT.Copy).then_inc(oT_out, 1)
            tiles(act, body)

        @block.vector
        def _(dve):
            def body(t, b):
                dve.wait_ge(s_done, t + 1)
                if late(t):
                    dve.wait_ge(stored[b], (t - b) * 8)
                dve.scalar_tensor_tensor(s_sb[:, b, :], psS[b][:], scale, bo[:], ALU.mult, ALU.add).then_inc(s_out, 1)
            tiles(dve, body)

        @block.sync
        def _(sp):
            def body(t, b):
                row = sp.snap(t) if not isinstance(t, int) else t
                sp.wait_ge(s_out, t + 1)
                sp.dma_start(s_dram[bass.ds(row, 1), :, :].rearrange("a p n -> p (a n)"), s_sb[:, b, :]).then_inc(stored[b], 16)
            tiles(sp, body)
            for b in range(2):
                sp.wait_ge(stored[b], 8 * TILES)


def build(nc, a, out):
    x_v = a["x"].rearrange("(t p) n -> t p n", p=P)
    out_v = out.rearrange("b (t p) n -> (b t) p n", p=P)
    s0_dram = nc.dram_tensor("s0_scratch", [TILES, P, HID], F32, kind="Internal").ap()
    s1_dram = nc.dram_tensor("s1_scratch", [TILES, P, HID], F32, kind="Internal").ap()
    o_dram = nc.dram_tensor("o_scratch", [BATCH, HEADS, SEQ, D], F32, kind="Internal").ap()
    qk_dram = nc.dram_tensor("qk_scratch", [2, QK_TILES, P, TOKENS], F32, kind="Internal").ap()
    v_dram = nc.dram_tensor("v_scratch", [TOKENS, HEADS * STRIP], F32, kind="Internal").ap()
    m_dram = nc.dram_tensor("m_scratch", [2, GH * POS_TILES, P], F32, kind="Internal").ap()
    ao_dram = nc.dram_tensor("ao_scratch", [TILES, P, HID], F32, kind="Internal").ap()
    x1_dram = nc.dram_tensor("x1_scratch", [TILES, P, HID], F32, kind="Internal").ap()
    with ExitStack() as top:
        def sb(ctx, name, shape, dt=F32):
            return ctx.enter_context(nc.sbuf_tensor(name, shape, dt))
        XT_hi, XT_lo = sb(top, "XT_hi", [P, KT, TOKENS], F32R), sb(top, "XT_lo", [P, KT, TOKENS], F32R)
        ident = sb(top, "ident", [P, P])
        mean_rstd = sb(top, "mean_rstd", [P, TILES, 2])
        logits = sb(top, "logits", [P, TILES, RW1])

        def row(ap):
            return ap.rearrange("(a n) -> a n", a=1).partition_broadcast(P)

        with ExitStack() as c:
            wo, bo = sb(c, "wo_0", [P, KT, HID]), sb(c, "bo_0", [P, HID])
            n2 = sb(c, "n2_all", [P, TILES, QK_HEADS])
            proj, v = sb(c, "proj", [P, TILES, QK_HEADS * RF]), sb(c, "v_all", [P, TILES, KV_HEADS * D])
            with ExitStack() as c2:
                x_sb = sb(c2, "x_sb", [P, TILES, HID])
                wq_raw = sb(c2, "wq_raw", [P, KT, 512])
                wq_hi, wq_lo = sb(c2, "wq_hi", [P, KT, 512], F32R), sb(c2, "wq_lo", [P, KT, 512], F32R)
                wr_raw = sb(c2, "wr_raw", [P, KT, E0])
                wr_hi, wr_lo = sb(c2, "wr_hi", [P, KT, E0], F32R), sb(c2, "wr_lo", [P, KT, E0], F32R)
                rblk, bias = sb(c2, "rblk", [P, 64]), sb(c2, "bias", [P, 512])
                cos, sin = sb(c2, "cos", [P, POS_TILES, D]), sb(c2, "sin", [P, POS_TILES, D])
                split_weights(nc, "w0", [(wq_raw[:], wq_hi[:], wq_lo[:]), (wr_raw[:], wr_hi[:], wr_lo[:])], [
                    (ident[:], a["ident"]), (wq_raw[:], a["wqkv0"]), (wr_raw[:], a["wr0"]), (rblk[:], a["rblk"]),
                    (bias[:], a["bias0"].partition_broadcast(P)), (cos[:], a["cos"]), (sin[:], a["sin"]),
                    (wo[:], a["wo0"]), (bo[:], a["bo0"].partition_broadcast(P))])
                standardise(nc, x_sb, mean_rstd, lambda sp, i: sp.dma_start(
                    x_sb[:, 4 * i:4 * i + 4, :], x_v[4 * i:4 * i + 4].rearrange("t p n -> p t n")), "ln0")
                normalise_and_transpose(nc, "nt0", x_sb, mean_rstd, XT_hi, XT_lo, logits[:, :, 0:E0], wr_hi, wr_lo, E0, ident,
                                        {"w_hi": wq_hi, "w_lo": wq_lo, "bias": bias, "cos": cos, "sin": sin, "rblk": rblk,
                                         "n2": n2, "proj": proj, "v": v})
            linear_attention(nc, {"n2": n2, "proj": proj, "v": v}, o_dram)
            o_rows = o_dram.rearrange("b h s d -> (b h s d)").rearrange("(t p n) -> t p n", p=P, n=HID)
            project_out(nc, "po0", lambda t: o_rows[bass.ds(t, 1), :, :].rearrange("a p n -> p (a n)"), s0_dram, ident, wo, bo,
                        SHARE)
        with ExitStack() as c:
            acc = sb(c, "acc0", [P, TILES, HID])
            with ExitStack() as c2:
                CT = sb(c2, "CT0", [2 * E0, TOKENS], F32R)
                route(nc, "r0", logits[:, :, 0:E0], E0, E0, TOP0, 1e-20, CT, ident)
                experts(nc, "f0", a["ffn0"], NT0, G0, E0, XT_hi, XT_lo, CT, acc)
            gate_and_add(nc, "g0", x_v, s0_dram, acc, x1_dram)
            wr_raw = sb(c, "wr1_raw", [P, KT, RW1])
            wr_hi, wr_lo = sb(c, "wr1_hi", [P, KT, RW1], F32R), sb(c, "wr1_lo", [P, KT, RW1], F32R)
            W3 = 3 * HID
            w_raw = sb(c, "wqkv1_raw", [P, KT, W3])
            w_hi, w_lo = sb(c, "wqkv1_hi", [P, KT, W3], F32R), sb(c, "wqkv1_lo", [P, KT, W3], F32R)
            b_raw, bias_qk, bias_v = sb(c, "b_raw", [P, QK_TILES]), sb(c, "bias_qk", [P, QK_TILES]), sb(c, "bias_v", [P, HID])
            split_weights(nc, "w1", [(wr_raw[:], wr_hi[:], wr_lo[:]), (w_raw[:], w_hi[:], w_lo[:])], [
                (wr_raw[:], a["wr1"]), (w_raw[:], a["wqkv1"]), (b_raw[:], a["bias_qk1"]),
                (bias_v[:], a["bias_v1"].partition_broadcast(P))],
                scale=[(w_raw[:, :, 0:HID], w_raw[:, :, 0:HID], 0.25), (bias_qk[:, 0:KT], b_raw[:, 0:KT], 0.25),
                       (bias_qk[:, KT:QK_TILES], b_raw[:, KT:QK_TILES], 1.0)])
            standardise(nc, acc, mean_rstd, lambda sp, i: sp.dma_start(
                acc[:, 4 * i:4 * i + 4, :], x1_dram[4 * i:4 * i + 4].rearrange("t p n -> p t n")), "ln1")
            normalise_and_transpose(nc, "nt1", acc, mean_rstd, XT_hi, XT_lo, logits, wr_hi, wr_lo, RW1, ident,
                                    qkv={"w_hi": w_hi, "w_lo": w_lo, "bias_qk": bias_qk, "bias_v": bias_v,
                                         "qk": qk_dram, "v": v_dram})
        with ExitStack() as c:
            ident_b, mqk, mkq = sb(c, "ident_b", [P, P], BF16), sb(c, "mask_qk", [P, P], BF16), sb(c, "mask_kq", [P, P], BF16)
            wo, bo = sb(c, "wo_1", [P, KT, HID]), sb(c, "bo_1", [P, HID])
            split_weights(nc, "wo1", [], [(wo[:], a["wo1"]), (bo[:], a["bo1"].partition_broadcast(P))])
            masks(nc, ident_b, mqk, mkq)
            causal_attention(nc, qk_dram, v_dram, ident, mqk, mkq, ident_b, m_dram, ao_dram)
            project_out(nc, "po1", lambda t: ao_dram[bass.ds(t, 1), :, :].rearrange("a p n -> p (a n)"), s1_dram, ident, wo, bo, 1.0)
        with ExitStack() as c:
            acc = sb(c, "acc1", [P, TILES, HID])
            with ExitStack() as c2:
                CT = sb(c2, "CT1", [2 * (E1 + 1), TOKENS], F32R)
                route(nc, "r1", logits[:, :, 0:E1 + 1], E1 + 1, E1, TOP1, 0.0, CT, ident)
                experts(nc, "f1", a["ffn1"], NT1, G1, E1 + 1, XT_hi, XT_lo, CT, acc)
            gate_and_add(nc, "g1", x1_dram, s1_dram, acc, out_v)


def masks(nc, ident_b, mqk, mkq):
    with ExitStack() as ctx:
        ctx.callback(nc.all_engine_barrier)
        filled = new_semaphore(nc, ctx, "mk_filled")
        done = new_semaphore(nc, ctx, "mk_done")
        block = ctx.enter_context(nc.Block())

        @block.gpsimd
        def _(pool):
            for m in (ident_b, mqk, mkq):
                pool.memset(m[:, :], 0.0).then_inc(filled, 1)
            pool.wait_ge(filled, 3)
            pool.affine_select(out=ident_b[:, :], in_=ident_b[:, :], compare_op=ALU.not_equal, fill=1.0, base=0,
                               pattern=[[-1, P]], channel_multiplier=1).then_inc(done, 1)
            pool.affine_select(out=mqk[:, :], in_=mqk[:, :], compare_op=ALU.is_ge, fill=NEG, base=0,
                               pattern=[[-1, P]], channel_multiplier=1).then_inc(done, 1)
            pool.affine_select(out=mkq[:, :], in_=mkq[:, :], compare_op=ALU.is_ge, fill=NEG, base=0,
                               pattern=[[1, P]], channel_multiplier=-1).then_inc(done, 1)
            pool.wait_ge(done, 3)


def kernel(**inputs):
    import numpy as np
    import concourse.bacc as bacc
    from concourse.bass_utils import run_bass_kernel_spmd

    w = {k: np.asarray(v) for k, v in inputs.items()}

    def kmajor(m):
        return np.ascontiguousarray(m.reshape(KT, P, -1).transpose(1, 0, 2))

    def ffn(gate, up, down, nt, owner, n_experts):
        mid = gate.shape[1]
        pad = nt * P - mid
        gate, up = (np.concatenate([m, np.zeros((HID, pad), m.dtype)], 1) for m in (gate, up))
        down = np.concatenate([down, np.zeros((pad, HID), down.dtype)], 0)
        sel = np.zeros((P, nt * P), np.float32)
        sel[owner, np.arange(mid)] = 1.0
        sel[n_experts + owner, np.arange(mid)] = 1.0
        packed = np.zeros((nt, P, WTS), gate.dtype)
        gu = np.stack([gate, up]).reshape(2, KT, P, nt, P)
        packed[:, :, :2 * KT * P] = gu.transpose(3, 2, 0, 1, 4).reshape(nt, P, 2 * KT * P)
        packed[:, :, 2 * KT * P:WT] = down.reshape(nt, P, HID)
        packed[:, :, WT:] = sel.reshape(P, nt, P).transpose(1, 0, 2)
        return packed

    a = {"x": w["L0_attn_hidden_states"].reshape(TOKENS, HID), "ident": np.eye(P, dtype=np.float32)}
    a["wqkv0"] = kmajor(np.concatenate([w["L0_attn_Wq"], w["L0_attn_Wk"], w["L0_attn_Wv"]], 0).T)
    a["bias0"] = np.concatenate([w["L0_attn_bq"], w["L0_attn_bk"], w["L0_attn_bv"]])
    a["wr0"] = kmajor(w["L0_ffn_wg"].T)
    a["wo0"], a["bo0"] = kmajor(w["L0_attn_Wo"].T), w["L0_attn_bo"]
    a["wo1"], a["bo1"] = kmajor(w["L1_attn_Wo"].T), w["L1_attn_bo"]
    rblk = np.zeros((P, P // D, RF), np.float32)
    for h in range(P // D):
        rblk[h * D:(h + 1) * D, h, :] = w["L0_attn_rand_matrix"].T
    a["rblk"] = rblk.reshape(P, P // D * RF)
    inv_freq = (1.0 / 10000.0 ** (np.arange(0, D, 2, dtype=np.float32) / np.float32(D))).astype(np.float32)
    angle = (np.arange(SEQ, dtype=np.float32)[:, None] * inv_freq[None, :]).reshape(POS_TILES, P, RF).transpose(1, 0, 2)
    a["cos"] = np.concatenate([np.cos(angle), np.cos(angle)], -1).astype(np.float32)
    a["sin"] = np.concatenate([-np.sin(angle), np.sin(angle)], -1).astype(np.float32)
    w1, w2 = w["L0_ffn_w1"], w["L0_ffn_w2"]
    a["ffn0"] = ffn(w1[:, :, :MID].transpose(1, 0, 2).reshape(HID, E0 * MID), w1[:, :, MID:].transpose(1, 0, 2).reshape(HID, E0 * MID),
                    w2.reshape(E0 * MID, HID), NT0, np.repeat(np.arange(E0), MID), E0)
    gu, sgu = w["L1_ffn_expert_gate_up"], w["L1_ffn_shared_gate_up"]
    gate = np.concatenate([gu[:, :MID].reshape(E1 * MID, HID), sgu[:SHARED]], 0).T
    up = np.concatenate([gu[:, MID:].reshape(E1 * MID, HID), sgu[SHARED:]], 0).T
    down = np.concatenate([w["L1_ffn_expert_down"].transpose(0, 2, 1).reshape(E1 * MID, HID), w["L1_ffn_shared_down"].T], 0)
    owner = np.concatenate([np.repeat(np.arange(E1), MID), np.full(SHARED, E1)])
    a["ffn1"] = ffn(gate, up, down, NT1, owner, E1 + 1)
    a["wr1"] = kmajor(np.concatenate([w["L1_ffn_gate_w"], w["L1_ffn_shared_gate_vec"], np.zeros((1, HID), np.float32)], 0).T)
    a["wqkv1"] = kmajor(np.concatenate([w["L1_attn_Wq"], w["L1_attn_Wk"], w["L1_attn_Wv"]], 0).T)
    a["bias_qk1"] = np.concatenate([w["L1_attn_bq"], w["L1_attn_bk"]]).reshape(QK_TILES, P).T
    a["bias_v1"] = w["L1_attn_bv"]
    a = {k: np.ascontiguousarray(v) for k, v in a.items()}

    nc = bacc.Bacc("TRN2", target_bir_lowering=False, num_devices=1)
    aps = {k: nc.dram_tensor(f"in_{k}", v.shape, mybir.dt.from_np(v.dtype), kind="ExternalInput").ap() for k, v in a.items()}
    out = nc.dram_tensor("out_0", (BATCH, SEQ, HID), F32, kind="ExternalOutput").ap()
    build(nc, aps, out)
    r = run_bass_kernel_spmd(nc, [{f"in_{k}": v for k, v in a.items()}], core_ids=[0])
    return r.results[0]["out_0"]
```

```python
from contextlib import ExitStack, contextmanager

import concourse.bass as bass
from concourse import mybir

F32 = mybir.dt.float32
F32R = mybir.dt.float32r
BF16 = mybir.dt.bfloat16
ALU = mybir.AluOpType
ACT = mybir.ActivationFunctionType
AX = mybir.AxisListType

P = 128
BATCH, SEQ, HID = 4, 1024, 256
TOKENS = BATCH * SEQ
TILES = TOKENS // P
KT = HID // P
CHUNK = 512
CHUNKS = TOKENS // CHUNK
TPC = CHUNK // P
HEADS, D = 16, 16
KV_HEADS = 8
QK_HEADS = HEADS + KV_HEADS
SHARE = (HEADS // KV_HEADS) / D
RF = D // 2
POS_TILES = SEQ // P
EPS = 1e-5
NEG = -1e30
ROUND = 1.5 * 2.0 ** 23
TWO_PI = 6.283185005187988
MID = 176
E0, TOP0 = 8, 2
E1, TOP1 = 16, 4
RW1 = E1 + 2
SHARED = 704
NT0 = E0 * MID // P
NT1 = -(-(E1 * MID + SHARED) // P)
G0, G1 = 11, 7
RAW0, RAW1 = 2, 7
WT = 2 * KT * P + HID
WTS = WT + P
GH = 4
GROUPS = HEADS // GH
STRIP = 32
QK_TILES = 2 * HID // P
STACK = 4 * D
ROWS = STACK + 2
ROUNDS = GROUPS * BATCH
PADDED = 96
SPAN = SEQ // CHUNK


@contextmanager
def phase(nc, shared=None):
    if shared is not None:
        yield shared
        return
    with ExitStack() as ctx:
        ctx.callback(nc.all_engine_barrier)
        with nc.Block() as block:
            yield ctx, block


def new_semaphore(nc, ctx, name):
    handle = ctx.enter_context(nc.semaphore(name))
    ctx.callback(lambda: nc.gpsimd.sem_clear(handle))
    return handle


class Steps:

    def __init__(self, eng, sem):
        self.eng, self.sem, self.n, self.base = eng, sem, 0, 0

    def link(self, ins):
        self.n += 1
        ins.then_inc(self.sem, 1)
        self.eng.wait_ge(self.sem, self.base + self.n)


def three_passes(pe, out, w_hi, w_lo, x_hi, x_lo, kt, first=True, last=True, check=False):
    n = 0
    for k in range(kt):
        for w, x in ((w_hi, x_hi), (w_hi, x_lo), (w_lo, x_hi)):
            ins = pe.matmul(out, w(k), x(k), start=first and n == 0, stop=last and n == 3 * kt - 1,
                            skip_group_check=check)
            n += 1
    return ins


def tile_statistics(nc, ctx, tag, x_sb, mean_rstd):
    stats = ctx.enter_context(nc.sbuf_tensor(f"{tag}_stats", [P, 2, 6], F32))
    stats_step, aggr_step = new_semaphore(nc, ctx, f"{tag}_stats_step"), new_semaphore(nc, ctx, f"{tag}_aggr_step")

    def count(dve, t):
        dve.bn_stats(stats[:, t % 2, :], x_sb[:, t, :]).then_inc(stats_step, 1)
        dve.wait_ge(stats_step, t + 1)
        dve.bn_aggr(mean_rstd[:, t, :], stats[:, t % 2, :]).then_inc(aggr_step, 1)
    return count, aggr_step


def standardise(nc, tag, mean_rstd, statistics, load=None, shared=None):
    LOADS = TILES // 4
    with phase(nc, shared) as (ctx, block):
        def sem(name):
            return new_semaphore(nc, ctx, f"{tag}_{name}")
        count, aggr_step = statistics(ctx)
        x_in = [sem(f"x_in{c}") for c in range(LOADS)] if load else []
        stats_done, root_done, mr_done = sem("stats_done"), sem("root_done"), sem("mr_done")

        if load:
            @block.sync
            def _(sp):
                for c in range(LOADS):
                    load(sp, c).then_inc(x_in[c], 16)

        @block.vector
        def _(dve):
            if load:
                for t in range(TILES):
                    dve.wait_ge(x_in[t // 4], 16)
                    count(dve, t)
            dve.wait_ge(aggr_step, TILES)
            ins = dve.tensor_scalar(mean_rstd[:, :, 1], mean_rstd[:, :, 1], EPS, None, ALU.add)
            ins.then_inc(stats_done, 1)
            dve.wait_ge(root_done, 1)
            dve.reciprocal(mean_rstd[:, :, 1], mean_rstd[:, :, 1]).then_inc(mr_done, 1)
            dve.wait_ge(mr_done, 1)

        @block.scalar
        def _(act):
            act.wait_ge(stats_done, 1)
            act.activation(mean_rstd[:, :, 1], mean_rstd[:, :, 1], ACT.Sqrt).then_inc(root_done, 1)


def split_weights(nc, tag, pairs, loads, scale=(), shared=None):
    with phase(nc, shared) as (ctx, block):
        w_in = new_semaphore(nc, ctx, f"{tag}_w_in")
        hi_done = new_semaphore(nc, ctx, f"{tag}_hi_done")
        lo_done = new_semaphore(nc, ctx, f"{tag}_lo_done")
        scaled = new_semaphore(nc, ctx, f"{tag}_scaled")

        @block.sync
        def _(sp):
            for dst, src in loads:
                sp.dma_start(dst, src).then_inc(w_in, 16)

        @block.vector
        def _(dve):
            dve.wait_ge(w_in, 16 * len(loads))
            for dst, src, factor in scale:
                dve.tensor_scalar(dst, src, factor, None, ALU.mult).then_inc(scaled, 1)
            if scale:
                dve.wait_ge(scaled, len(scale))
            for raw, hi, lo in pairs:
                dve.tensor_copy(hi, raw).then_inc(hi_done, 1)
            for n, (raw, hi, lo) in enumerate(pairs):
                dve.wait_ge(hi_done, n + 1)
                dve.tensor_tensor(lo, raw, hi.bitcast(F32), ALU.subtract).then_inc(lo_done, 1)
            if pairs:
                dve.wait_ge(lo_done, len(pairs))


def in_steps(eng, *stages):
    most = max(lag for lag, _ in stages)
    assert most < POS_TILES

    def step(n):
        for lag, stage in stages:
            if lag <= n < TILES + lag:
                stage(n - lag, (n - lag) % POS_TILES, (n - lag) // POS_TILES)
    for n in range(POS_TILES):
        step(n)
    with eng.Fori(1, BATCH) as b:
        for i in range(POS_TILES):
            for lag, stage in stages:
                stage(b * POS_TILES + (i - lag), (i - lag) % POS_TILES, b if i >= lag else b - 1)
    for n in range(TILES, TILES + most):
        step(n)


def late(t, n):
    return not (isinstance(t, int) and t < n)


def tile_of(ap, t):
    return ap[:, bass.ds(t, 1), :].rearrange("p a n -> p (a n)")


def first_attention(nc, x_sb, mean_rstd, XT_hi, XT_lo, logits, wr, wqkv, bias, cos, sin, rblk, ident, o_dram, shared=None):
    NQ, NQK = HEADS * D, QK_HEADS * D
    NE = E0
    with phase(nc, shared) as (ctx, block):

        def sem(name):
            return new_semaphore(nc, ctx, f"fa_{name}")

        def sb(name, shape, dt=F32):
            return ctx.enter_context(nc.sbuf_tensor(f"fa_{name}", shape, dt))

        def ps(name, shape, n):
            return [ctx.enter_context(nc.psum_tensor(f"fa_{name}{i}", shape, F32)) for i in range(n)]
        VBUFS = 8
        xn = sb("xn", [P, 2, HID])
        st_hi, st_lo = sb("st_hi", [P, 2, HID], F32R), sb("st_lo", [P, 2, HID], F32R)
        qk, rot_a, rot_b, rot, sq, rotT = (sb(x, [P, 2, NQK]) for x in ("qk", "rot_a", "rot_b", "rot", "sq", "rotT"))
        v = sb("v", [P, VBUFS, KV_HEADS * D])
        n2, inv = sb("n2", [P, 2, QK_HEADS]), sb("inv", [P, 2, QK_HEADS])
        arg, whole, feat = (sb(x, [P, 2, QK_HEADS, D]) for x in ("arg", "whole", "feat"))
        qk_prod, av_prod = (sb(x, [P, 2, HEADS * KV_HEADS * D]) for x in ("qk_prod", "av_prod"))
        ones = sb("ones", [1, P], F32R)
        A = sb("A", [P, 2, HEADS, KV_HEADS])
        out = sb("out", [P, 2, NQ])
        psT, psL, psQ = ps("psT", [P, CHUNK], 2), ps("psL", [P, CHUNK], 2), ps("psQ", [P, CHUNK], 2)
        psR, psP = ps("psR", [P, CHUNK], 1)[0], ps("psP", [P, CHUNK], 1)[0]
        names = ("xn_done", "xT_done", "hi_done", "lo_done", "logits_done", "logits_out", "qkv_done", "qk_out", "v_out",
                 "rot_parts", "rot_done", "sq_done", "n2_done", "norm_done", "inv_part", "inv_done", "rotT_done", "rotT_out", "p_done",
                 "arg_part", "arg_done", "feat_done", "prod_done", "A_done", "av_done", "out_done", "ones_done")
        (xn_done, xT_done, hi_done, lo_done, logits_done, logits_out, qkv_done, qk_out, v_out, rot_parts, rot_done,
         sq_done, n2_done, norm_done, inv_part, inv_done, rotT_done, rotT_out, p_done, arg_part, arg_done, feat_done, prod_done, A_done,
         av_done, out_done, ones_done) = (sem(x) for x in names)
        kept, stored = [sem("kept0"), sem("kept1")], [sem("stored0"), sem("stored1")]

        @block.sync
        def _(sp):
            def keep(t, i, b):
                t0 = sp.snap(t * P) if not isinstance(t, int) else t * P
                sp.wait_ge(lo_done, t + 1)
                for st, XT in ((st_hi, XT_hi), (st_lo, XT_lo)):
                    sp.dma_start(XT[:, :, bass.ds(t0, P)].bitcast(F32),
                                 st[:, i % 2, :].rearrange("p (k n) -> p k n", k=KT).bitcast(F32)).then_inc(kept[i % 2], 16)

            def store(t, i, b):
                seq = sp.snap(b) if not isinstance(b, int) else b
                sp.wait_ge(out_done, t + 1)
                sp.dma_start(o_dram[bass.ds(seq, 1), :, i * P:(i + 1) * P, :].rearrange("b h s d -> s (b h) d"),
                             out[:, i % 2, :].rearrange("p (h d) -> p h d", d=D)).then_inc(stored[i % 2], 16)
            in_steps(sp, (1, keep), (5, store))
            for i in range(2):
                sp.wait_ge(kept[i], 16 * TILES)
                sp.wait_ge(stored[i], 8 * TILES)

        @block.vector
        def _(dve):
            def normalise(t, i, b):
                if late(t, 2):
                    dve.wait_ge(xT_done, t - 1)
                dve.tensor_scalar(xn[:, i % 2, :], tile_of(x_sb, t), mean_rstd[:, bass.ds(t, 1), 0],
                                  mean_rstd[:, bass.ds(t, 1), 1], ALU.subtract, ALU.mult).then_inc(xn_done, 1)

            def low_half(t, i, b):
                dve.wait_ge(hi_done, t + 1)
                dve.tensor_tensor(st_lo[:, i % 2, :], psT[i % 2][:, 0:HID], st_hi[:, i % 2, :].bitcast(F32), ALU.subtract)\
                   .then_inc(lo_done, 1)

            def square_norm(t, i, b):
                dve.wait_ge(sq_done, t + 1)
                if late(t, 2):
                    dve.wait_ge(norm_done, t - 1)
                dve.tensor_reduce(n2[:, i % 2, :], sq[:, i % 2, :].rearrange("p (h d) -> p h d", d=D), AX.X, ALU.add)\
                   .then_inc(n2_done, 1)

            def bounded_norm(t, i, b):
                n = inv[:, i % 2, :]
                dve.wait_ge(norm_done, t + 1)
                dve.tensor_scalar(n, n, 1e-6, None, ALU.max).then_inc(inv_part, 1)

            def inverse_norm(t, i, b):
                n = inv[:, i % 2, :]
                dve.wait_ge(inv_part, t + 1)
                dve.reciprocal(n, n).then_inc(inv_done, 1)

            def sine_turns(t, i, b):
                dve.wait_ge(p_done, t + 1)
                dve.wait_ge(inv_done, t + 1)
                if late(t, 2):
                    dve.wait_ge(feat_done, t - 1)
                p3 = psP[:, 0:QK_HEADS * RF].rearrange("p (h f) -> p h f", f=RF)
                i3 = inv[:, i % 2, :].unsqueeze(2).broadcast_to([P, QK_HEADS, RF])
                dve.scalar_tensor_tensor(arg[:, i % 2, :, 0:RF], p3, 0.15915494309189535, i3, ALU.mult, ALU.mult)\
                   .then_inc(arg_part, 1)

            def cosine_turns(t, i, b):
                dve.wait_ge(arg_part, t * 3 + 1)
                dve.tensor_scalar(arg[:, i % 2, :, RF:D], arg[:, i % 2, :, 0:RF], 0.25, None, ALU.add).then_inc(arg_part, 1)

            def whole_turns(t, i, b):
                dve.wait_ge(arg_part, t * 3 + 2)
                dve.tensor_scalar(whole[:, i % 2, :, :], arg[:, i % 2, :, :], ROUND, ROUND, ALU.add, ALU.subtract)\
                   .then_inc(arg_part, 1)

            def fraction(t, i, b):
                dve.wait_ge(arg_part, t * 3 + 3)
                a = arg[:, i % 2, :, :]
                dve.tensor_tensor(a, a, whole[:, i % 2, :, :], ALU.subtract).then_inc(arg_done, 1)

            def qk_sums(t, i, b):
                dve.wait_ge(prod_done, t + 1)
                if late(t, 2):
                    dve.wait_ge(av_done, t - 1)
                dve.tensor_reduce(A[:, i % 2, :, :], qk_prod[:, i % 2, :].rearrange("p (h g d) -> p h g d", g=KV_HEADS, d=D),
                                  AX.X, ALU.add).then_inc(A_done, 1)

            def av_products(t, i, b):
                dve.wait_ge(A_done, t + 1)
                dve.wait_ge(v_out, t + 1)
                if late(t, 2):
                    dve.wait_ge(out_done, t - 1)
                v4 = v[:, i % VBUFS, :].rearrange("p (g d) -> p d g", d=D).unsqueeze(1).broadcast_to([P, HEADS, D, KV_HEADS])
                a4 = A[:, i % 2, :, :].unsqueeze(2).broadcast_to([P, HEADS, D, KV_HEADS])
                dve.tensor_tensor(av_prod[:, i % 2, :].rearrange("p (h d g) -> p h d g", d=D, g=KV_HEADS), a4, v4, ALU.mult)\
                   .then_inc(av_done, 1)

            def av_sums(t, i, b):
                dve.wait_ge(av_done, t + 1)
                if late(t, 2):
                    dve.wait_ge(stored[i % 2], (t - i % 2) * 8)
                dve.tensor_reduce(out[:, i % 2, :].rearrange("p (h d) -> p h d", d=D),
                                  av_prod[:, i % 2, :].rearrange("p (h d g) -> p h d g", d=D, g=KV_HEADS), AX.X, ALU.add)\
                   .then_inc(out_done, 1)
            in_steps(dve, (1, low_half), (3, bounded_norm), (0, normalise), (3, inverse_norm), (5, qk_sums),
                     (3, sine_turns), (5, av_products), (3, cosine_turns), (2, square_norm), (3, whole_turns), (5, av_sums),
                     (3, fraction))

        @block.scalar
        def _(act):
            def high_half(t, i, b):
                act.wait_ge(xT_done, t + 1)
                if late(t, 2):
                    act.wait_ge(kept[i % 2], (t - i % 2) * 16)
                    act.wait_ge(logits_done, t - 1)
                act.activation(st_hi[:, i % 2, :], psT[i % 2][:, 0:HID], ACT.Copy).then_inc(hi_done, 1)

            def keep_logits(t, i, b):
                act.wait_ge(logits_done, t + 1)
                act.activation(tile_of(logits, t), psL[i % 2][:, 0:NE], ACT.Copy).then_inc(logits_out, 1)

            def take_qkv(t, i, b):
                act.wait_ge(qkv_done, t + 1)
                if late(t, 2):
                    act.wait_ge(rot_done, t - 1)
                act.activation(qk[:, i % 2, :], psQ[i % 2][:, 0:NQK], ACT.Copy).then_inc(qk_out, 1)
                if late(t, VBUFS):
                    act.wait_ge(av_done, t - (VBUFS - 1))
                act.activation(v[:, i % VBUFS, :], psQ[i % 2][:, NQK:], ACT.Copy).then_inc(v_out, 1)

            def keep_rotT(t, i, b):
                act.wait_ge(rotT_done, t + 1)
                if late(t, 2):
                    act.wait_ge(p_done, t - 1)
                act.activation(rotT[:, i % 2, :], psR[:, 0:NQK], ACT.Copy).then_inc(rotT_out, 1)

            def norm(t, i, b):
                act.wait_ge(n2_done, t + 1)
                if late(t, 2):
                    act.wait_ge(arg_done, t - 1)
                act.activation(inv[:, i % 2, :], n2[:, i % 2, :], ACT.Sqrt).then_inc(norm_done, 1)

            def features(t, i, b):
                act.wait_ge(arg_done, t + 1)
                if late(t, 2):
                    act.wait_ge(prod_done, t - 1)
                act.activation(feat[:, i % 2, :, :], arg[:, i % 2, :, :], ACT.Sin, scale=TWO_PI).then_inc(feat_done, 1)
            in_steps(act, (0, high_half), (1, take_qkv), (1, keep_logits), (2, keep_rotT), (2, norm), (3, features))

        @block.gpsimd
        def _(pool):
            def qk_products(t, i, b):
                pool.wait_ge(feat_done, t + 1)
                if late(t, 2):
                    pool.wait_ge(A_done, t - 1)
                q4 = feat[:, i % 2, 0:HEADS, :].unsqueeze(2).broadcast_to([P, HEADS, KV_HEADS, D])
                k4 = feat[:, i % 2, HEADS:QK_HEADS, :].unsqueeze(1).broadcast_to([P, HEADS, KV_HEADS, D])
                pool.tensor_tensor(qk_prod[:, i % 2, :].rearrange("p (h g d) -> p h g d", g=KV_HEADS, d=D), q4, k4, ALU.mult)\
                    .then_inc(prod_done, 1)

            def rotate(t, i, b):
                pool.wait_ge(qk_out, t + 1)
                if late(t, 2):
                    pool.wait_ge(rotT_done, t - 1)
                    pool.wait_ge(sq_done, t - 1)
                q3, a3, b3 = (x[:, i % 2, :].rearrange("p (h d) -> p h d", d=D) for x in (qk, rot_a, rot_b))
                cos_i = cos[:, i, :].unsqueeze(1).broadcast_to([P, QK_HEADS, D])
                pool.tensor_tensor(a3, q3, cos_i, ALU.mult).then_inc(rot_parts, 1)
                for half in range(2):
                    sin_i = sin[:, i, half * RF:half * RF + RF].unsqueeze(1).broadcast_to([P, QK_HEADS, RF])
                    other = (1 - half) * RF
                    pool.tensor_tensor(b3[:, :, half * RF:half * RF + RF], q3[:, :, other:other + RF], sin_i, ALU.mult)\
                        .then_inc(rot_parts, 1)
                pool.wait_ge(rot_parts, t * 3 + 3)
                pool.tensor_tensor(rot[:, i % 2, :], rot_a[:, i % 2, :], rot_b[:, i % 2, :], ALU.add).then_inc(rot_done, 1)
                pool.wait_ge(rot_done, t + 1)
                if late(t, 2):
                    pool.wait_ge(n2_done, t - 1)
                pool.tensor_tensor(sq[:, i % 2, :], rot[:, i % 2, :], rot[:, i % 2, :], ALU.mult).then_inc(sq_done, 1)
            pool.memset(ones[:].bitcast(F32), 1.0).then_inc(ones_done, 1)
            in_steps(pool, (4, qk_products), (1, rotate))

        @block.tensor
        def _(pe):
            def transpose(t, i, b):
                pe.wait_ge(xn_done, t + 1)
                if late(t, 2):
                    pe.wait_ge(lo_done, t - 1)
                for k in range(KT):
                    ins = pe.transpose(psT[i % 2][:, k * P:(k + 1) * P], xn[:, i % 2, k * P:(k + 1) * P], ident[:])
                ins.then_inc(xT_done, 1)

            def project(t, i, b):
                pe.wait_ge(lo_done, t + 1)
                if late(t, 2):
                    pe.wait_ge(logits_out, t - 1)
                x = [lambda k: st_hi[:, i % 2, k * P:(k + 1) * P], lambda k: st_lo[:, i % 2, k * P:(k + 1) * P]]
                if late(t, 2):
                    pe.wait_ge(v_out, t - 1)
                three_passes(pe, psQ[i % 2][:], *x, lambda k: wqkv[0][:, k, :], lambda k: wqkv[1][:, k, :], KT, last=False)
                pe.matmul(psQ[i % 2][:], ones[:], bias[0][:], start=False, stop=False)
                pe.matmul(psQ[i % 2][:], ones[:], bias[1][:], start=False, stop=True).then_inc(qkv_done, 1)
                three_passes(pe, psL[i % 2][:, 0:NE], *x, lambda k: wr[0][:, k, :], lambda k: wr[1][:, k, :], KT)\
                    .then_inc(logits_done, 1)

            def transpose_rotated(t, i, b):
                pe.wait_ge(rot_done, t + 1)
                if late(t, 1):
                    pe.wait_ge(rotT_out, t)
                for k in range(NQK // P):
                    ins = pe.transpose(psR[:, k * P:(k + 1) * P], rot[:, i % 2, k * P:(k + 1) * P], ident[:])
                ins.then_inc(rotT_done, 1)

            def random_projection(t, i, b):
                pe.wait_ge(rotT_out, t + 1)
                if late(t, 1):
                    pe.wait_ge(arg_part, t * 3 - 2)
                for k in range(NQK // P):
                    ins = pe.matmul(psP[:, k * 64:(k + 1) * 64], rotT[:, i % 2, k * P:(k + 1) * P], rblk[:],
                                    start=k == 0, stop=True, skip_group_check=True)
                ins.then_inc(p_done, 1)
            pe.wait_ge(ones_done, 1)
            in_steps(pe, (1, project), (0, transpose), (2, transpose_rotated), (2, random_projection))


def project_second(nc, x_sb, mean_rstd, XT_hi, XT_lo, logits, w_qk, w_vr, bias_qk, bias_v, ident, qk_dram, v_dram, shared=None):
    BUFS = 4
    QK_LAG = 5
    assert BUFS == TPC == QK_TILES
    NV = HID + RW1
    with phase(nc, shared) as (ctx, block):

        def sem(name):
            return new_semaphore(nc, ctx, f"ps_{name}")

        def sb(name, shape, dt=F32):
            return ctx.enter_context(nc.sbuf_tensor(f"ps_{name}", shape, dt))

        def ps(name, shape, n):
            return [ctx.enter_context(nc.psum_tensor(f"ps_{name}{i}", shape, F32)) for i in range(n)]
        xn = sb("xn", [P, 2, HID])
        st_hi, st_lo = sb("st_hi", [P, BUFS, HID], F32R), sb("st_lo", [P, BUFS, HID], F32R)
        v_st = sb("v_st", [P, BUFS, HEADS, STRIP])
        qk_hi, qk_lo = sb("qk_hi", [P, BUFS, CHUNK], F32R), sb("qk_lo", [P, BUFS, CHUNK], F32R)
        psT, psV, psK = ps("psT", [P, HID], 2), ps("psV", [P, CHUNK], 2), ps("psK", [P, CHUNK], BUFS)
        xn_done, xT_done, hi_done, lo_done, kept, v_done, v_out, logits_out, pads_done, qk_done, qkhi_out, qklo_out = (
            sem(x) for x in ("xn_done", "xT_done", "hi_done", "lo_done", "kept", "v_done", "v_out", "logits_out", "pads_done",
                             "qk_done", "qkhi_out", "qklo_out"))
        v_stored = [sem(f"v_stored{i}") for i in range(BUFS)]
        qk_stored = [sem(f"qk_stored{i}") for i in range(BUFS)]

        @block.vector
        def _(dve):
            def normalise(t, i, b):
                if late(t, 2):
                    dve.wait_ge(xT_done, t - 1)
                dve.tensor_scalar(xn[:, i % 2, :], tile_of(x_sb, t), mean_rstd[:, bass.ds(t, 1), 0],
                                  mean_rstd[:, bass.ds(t, 1), 1], ALU.subtract, ALU.mult).then_inc(xn_done, 1)

            def low_half(t, i, b):
                dve.wait_ge(hi_done, t + 1)
                if late(t, BUFS):
                    dve.wait_ge(kept, (t - BUFS) * 2 + 2)
                    dve.wait_ge(v_done, t - (BUFS - 1))
                dve.tensor_tensor(st_lo[:, i % BUFS, :], psT[i % 2][:], st_hi[:, i % BUFS, :].bitcast(F32), ALU.subtract)\
                   .then_inc(lo_done, 1)

            def values(t, i, b):
                dve.wait_ge(v_done, t + 1)
                if late(t, BUFS):
                    dve.wait_ge(v_stored[i % BUFS], (t - i % BUFS) * 4)
                dve.tensor_tensor(v_st[:, i % BUFS, :, 0:D], psV[i % 2][:, 0:HID].rearrange("p (h d) -> p h d", d=D),
                                  bias_v[:].rearrange("p (h d) -> p h d", d=D), ALU.add).then_inc(v_out, 1)

            def qk_low_half(k, i, b):
                m = i % BUFS
                dve.wait_ge(qkhi_out, k + 1)
                if late(k, BUFS):
                    dve.wait_ge(qk_stored[m], (k - m) * 8)
                dve.scalar_tensor_tensor(qk_lo[:, m, :], psK[m][:], bias_qk[:, m:m + 1], qk_hi[:, m, :].bitcast(F32),
                                         ALU.add, ALU.subtract).then_inc(qklo_out, 1)
            dve.wait_ge(pads_done, 2 * BUFS)
            in_steps(dve, (0, normalise), (1, low_half), (2, values), (QK_LAG + 1, qk_low_half))

        @block.scalar
        def _(act):
            def high_half(t, i, b):
                act.wait_ge(xT_done, t + 1)
                if late(t, BUFS):
                    act.wait_ge(kept, (t - BUFS) * 2 + 2)
                    act.wait_ge(v_done, t - (BUFS - 1))
                act.activation(st_hi[:, i % BUFS, :], psT[i % 2][:], ACT.Copy).then_inc(hi_done, 1)

            def keep_logits(t, i, b):
                act.wait_ge(v_out, t + 1)
                act.activation(tile_of(logits, t), psV[i % 2][:, HID:NV], ACT.Copy).then_inc(logits_out, 1)

            def qk_high_half(k, i, b):
                m = i % BUFS
                act.wait_ge(qk_done, k + 1)
                if late(k, BUFS):
                    act.wait_ge(qk_stored[m], (k - m) * 8)
                act.activation(qk_hi[:, m, :], psK[m][:], ACT.Identity, bias=bias_qk[:, m:m + 1]).then_inc(qkhi_out, 1)
            in_steps(act, (0, high_half), (QK_LAG, qk_high_half), (2, keep_logits))

        @block.gpsimd
        def _(pool):
            for b in range(BUFS):
                pool.memset(v_st[:, b, :, D:D + 1], 1.0).then_inc(pads_done, 1)
                pool.memset(v_st[:, b, :, D + 1:STRIP], 0.0).then_inc(pads_done, 1)

            def keep(t, i, b):
                for done, st, XT in ((hi_done, st_hi, XT_hi), (lo_done, st_lo, XT_lo)):
                    pool.wait_ge(done, t + 1)
                    pool.tensor_copy(XT[:, :, bass.ds(t * P, P)], st[:, i % BUFS, :].rearrange("p (k n) -> p k n", k=KT))\
                        .then_inc(kept, 1)
            in_steps(pool, (0, keep))

        @block.tensor
        def _(pe):
            def transpose(t, i, b):
                pe.wait_ge(xn_done, t + 1)
                if late(t, 2):
                    pe.wait_ge(lo_done, t - 1)
                for k in range(KT):
                    ins = pe.transpose(psT[i % 2][:, k * P:(k + 1) * P], xn[:, i % 2, k * P:(k + 1) * P], ident[:])
                ins.then_inc(xT_done, 1)

            def values_and_logits(t, i, b):
                pe.wait_ge(lo_done, t + 1)
                if late(t, 2):
                    pe.wait_ge(logits_out, t - 1)
                three_passes(pe, psV[i % 2][:, 0:NV], lambda k: st_hi[:, i % BUFS, k * P:(k + 1) * P],
                             lambda k: st_lo[:, i % BUFS, k * P:(k + 1) * P], lambda k: w_vr[0][:, k, :],
                             lambda k: w_vr[1][:, k, :], KT).then_inc(v_done, 1)

            def features(k, i, b):
                m = i % BUFS
                if m == 0:
                    pe.wait_ge(kept, k * 2 + 2 * TPC)
                if late(k, BUFS):
                    pe.wait_ge(qklo_out, k - (BUFS - 1))
                chunk = bass.ds(k * P - m * P, CHUNK)
                three_passes(pe, psK[m][:], lambda j: w_qk[0][:, j, m * P:(m + 1) * P],
                             lambda j: w_qk[1][:, j, m * P:(m + 1) * P], lambda j: XT_hi[:, j, chunk],
                             lambda j: XT_lo[:, j, chunk], KT).then_inc(qk_done, 1)
            in_steps(pe, (0, transpose), (1, values_and_logits), (QK_LAG, features))

        @block.sync
        def _(sp):
            def store_v(t, i, b):
                sp.wait_ge(v_out, t + 1)
                sp.dma_start(v_dram.rearrange("(b g) t p c -> b t p g c", g=GROUPS)[bass.ds(b, 1), i]
                             .rearrange("a p g c -> p (a g) c"),
                             v_st[:, i % BUFS, :, :].rearrange("p (g h) c -> p g (h c)", g=GROUPS))\
                    .then_inc(v_stored[i % BUFS], 16)

            def store_qk(k, i, b):
                m = i % BUFS
                side, rows = m // KT, bass.ds(m % KT * P, P)
                first = i // TPC * CHUNK
                sp.wait_ge(qklo_out, k + 1)
                for half, st in enumerate((qk_hi, qk_lo)):
                    dst = qk_dram[half, side].rearrange("(b g) r n -> b (g r) n", g=GROUPS)[bass.ds(b, 1), rows, first:first + CHUNK]
                    sp.dma_start(dst.rearrange("a r n -> r (a n)"), st[:, m, :].bitcast(F32)).then_inc(qk_stored[m], 16)
            in_steps(sp, (2, store_v), (QK_LAG + 1, store_qk))
            for b in range(BUFS):
                sp.wait_ge(v_stored[b], 16 * TILES // BUFS)
                sp.wait_ge(qk_stored[b], 32 * TILES // BUFS)


def route(nc, tag, logits, NE, E, TOP, guard, CT, ident, shared=None):
    T = TILES
    with phase(nc, shared) as (ctx, block):
        def sem(name):
            return new_semaphore(nc, ctx, f"{tag}_{name}")

        def sb(name, shape, dt=F32):
            return ctx.enter_context(nc.sbuf_tensor(f"{tag}_{name}", shape, dt))
        prob, left, same, comb = (sb(x, [P, T, E]) for x in ("prob", "left", "same", "comb"))
        rank = sb("rank", [P, E])
        top, one = sb("top", [P, T]), sb("one", [P, T])
        total = sb("total", [P, T])
        split = sb("split", [P, T, 2 * NE])
        rounded = sb("rounded", [P, T, NE], F32R)
        psC = [ctx.enter_context(nc.psum_tensor(f"{tag}_psC{i}", [2 * NE, CHUNK], F32)) for i in range(2)]
        steps, shifted, exp_done, gate_done, split_done, cT_done, cT_out, rank_done, padded = (
            sem(x) for x in ("steps", "shifted", "exp_done", "gate_done", "split_done", "cT_done", "cT_out", "rank_done", "padded"))

        def over(x):
            return x[:, :].unsqueeze(2).broadcast_to([P, T, E])

        @block.gpsimd
        def _(pool):
            for j in range(E):
                pool.memset(rank[:, j:j + 1], float(E - j)).then_inc(rank_done, 1)
            pool.memset(CT[:, :].bitcast(F32), 0.0).then_inc(padded, 1)

        @block.vector
        def _(dve):
            s = Steps(dve, steps)
            s.link(dve.tensor_reduce(top[:, :], logits[:, :, 0:E], AX.X, ALU.max))
            dve.tensor_tensor(prob[:, :, :], logits[:, :, 0:E], over(top), ALU.subtract).then_inc(shifted, 1)
            dve.wait_ge(exp_done, 1)
            s.link(dve.tensor_reduce(total[:, :], prob[:, :, :], AX.X, ALU.add))
            s.link(dve.reciprocal(total[:, :], total[:, :]))
            s.link(dve.tensor_tensor(prob[:, :, :], prob[:, :, :], over(total), ALU.mult))
            s.link(dve.tensor_copy(left[:, :, :], prob[:, :, :]))
            s.link(dve.memset(comb[:, :, :], 0.0))
            dve.wait_ge(rank_done, E)
            r3 = rank[:, :].unsqueeze(1).broadcast_to([P, T, E])
            for _k in range(TOP):
                s.link(dve.tensor_reduce(top[:, :], left[:, :, :], AX.X, ALU.max))
                s.link(dve.tensor_tensor(same[:, :, :], left[:, :, :], over(top), ALU.is_equal))
                s.link(dve.tensor_tensor(same[:, :, :], same[:, :, :], r3, ALU.mult))
                s.link(dve.tensor_reduce(one[:, :], same[:, :, :], AX.X, ALU.max))
                s.link(dve.tensor_tensor(same[:, :, :], over(one), r3, ALU.is_equal))
                s.link(dve.tensor_tensor(comb[:, :, :], comb[:, :, :], same[:, :, :], ALU.add))
                s.link(dve.scalar_tensor_tensor(left[:, :, :], same[:, :, :], -4.0, left[:, :, :], ALU.mult, ALU.add))
            s.link(dve.tensor_tensor(comb[:, :, :], comb[:, :, :], prob[:, :, :], ALU.mult))
            s.link(dve.tensor_reduce(total[:, :], comb[:, :, :], AX.X, ALU.add))
            if guard:
                s.link(dve.tensor_scalar(total[:, :], total[:, :], guard, None, ALU.add))
            s.link(dve.reciprocal(total[:, :], total[:, :]))
            s.link(dve.tensor_tensor(split[:, :, 0:E], comb[:, :, :], over(total), ALU.mult))
            if NE > E:
                dve.wait_ge(gate_done, 1)
            s.link(dve.tensor_copy(rounded[:, :, :], split[:, :, 0:NE]))
            s.link(dve.tensor_tensor(split[:, :, NE:2 * NE], split[:, :, 0:NE], rounded[:, :, :].bitcast(F32), ALU.subtract))
            dve.tensor_copy(split[:, :, 0:NE], rounded[:, :, :].bitcast(F32)).then_inc(split_done, 1)

        @block.scalar
        def _(act):
            act.wait_ge(shifted, 1)
            act.activation(prob[:, :, :], prob[:, :, :], ACT.Exp).then_inc(exp_done, 1)
            if NE > E:
                act.activation(split[:, :, E:NE], logits[:, :, E:NE], ACT.Sigmoid).then_inc(gate_done, 1)
            act.wait_ge(padded, 1)
            for c in range(CHUNKS):
                act.wait_ge(cT_done, c + 1)
                act.activation(CT[0:2 * NE, c * CHUNK:(c + 1) * CHUNK], psC[c % 2][:, :], ACT.Copy).then_inc(cT_out, 1)

        @block.tensor
        def _(pe):
            pe.wait_ge(split_done, 1)
            for c in range(CHUNKS):
                if c >= 2:
                    pe.wait_ge(cT_out, c - 1)
                for j in range(TPC):
                    ins = pe.transpose(psC[c % 2][:, j * P:(j + 1) * P], split[:, c * TPC + j, :], ident[:])
                ins.then_inc(cT_done, 1)


def experts(nc, tag, w_dram, NT, G, RAW, NE, XT_hi, XT_lo, CT, acc, shared=None):
    NG = NT // G
    with phase(nc, shared) as (ctx, block):
        def sem(name):
            return new_semaphore(nc, ctx, f"{tag}_{name}")

        def sb(name, shape, dt=F32):
            return ctx.enter_context(nc.sbuf_tensor(f"{tag}_{name}", shape, dt))
        raw = sb("raw", [P, RAW, WTS])
        w_hi, w_lo = sb("w_hi", [P, G, WTS], F32R), sb("w_lo", [P, G, WT], F32R)
        h = sb("h", [P, 2, CHUNK])
        h_hi, h_lo = sb("h_hi", [P, 2, CHUNK], F32R), sb("h_lo", [P, 2, CHUNK], F32R)
        psG, psU, psC = ([ctx.enter_context(nc.psum_tensor(f"{tag}_{n}{i}", [P, CHUNK], F32)) for i in range(2)]
                         for n in ("psG", "psU", "psC"))
        psY = ctx.enter_context(nc.psum_tensor(f"{tag}_psY", [P, TPC, HID], F32))
        raw_in = [sem(f"raw_in{i}") for i in range(RAW)]
        (hiw_done, low_done, up_done, silu_done, gu_done, h_done, hi_done, lo_done, down_done, y_done, y_out, zeroed) = (
            sem(x) for x in ("hiw_done", "low_done", "up_done", "silu_done", "gu_done", "h_done", "hi_done", "lo_done",
                             "down_done", "y_done", "y_out", "zeroed"))

        @block.sync
        def _(sp):
            for w in range(NT):
                if w >= RAW:
                    sp.wait_ge(low_done, w - RAW + 1)
                sp.dma_start(raw[:, w % RAW, :], w_dram[w]).then_inc(raw_in[w % RAW], 16)

        @block.gpsimd
        def _(pool):
            pool.memset(acc[:, :, :], 0.0).then_inc(zeroed, 1)

        def groups(eng, chunk, tail):
            for g in range(NG):
                chunk(g, 0, 0)
                chunk(g, 1, 1)
                with eng.Fori(1, CHUNKS // 2 - 1) as i:
                    chunk(g, i * 2, 0)
                    chunk(g, i * 2 + 1, 1)
                chunk(g, CHUNKS - 2, 0)
                chunk(g, CHUNKS - 1, 1)
            tail()

        def splits(g, c, j):
            if not isinstance(c, int):
                return [], []
            if g == 0 and c == 0:
                return ([0, 1] if j == 0 else [j + 1] if j + 1 < G else []), []
            if c == CHUNKS - 1 and g + 1 < NG and j >= 2:
                return [], [(g + 1) * G + j - 2]
            if c == 0 and j < 2:
                return [], [g * G + G - 2 + j]
            return [], []

        def in_splits(g, c, j, split, tile):
            before, after = splits(g, c, j)
            for w in before:
                split(w)
            tile()
            for w in after:
                split(w)

        def step(g, c, j):
            return (g * CHUNKS + c) * G + j

        def b_of(g, cpar, j):
            return (g * CHUNKS * G + cpar * G + j) % 2

        @block.vector
        def _(dve):
            def weights(w):
                j = w % G
                dve.wait_ge(raw_in[w % RAW], 16 * (w // RAW + 1))
                dve.wait_ge(hiw_done, w + 1)
                dve.tensor_tensor(w_lo[:, j, :], raw[:, w % RAW, 0:WT], w_hi[:, j, 0:WT].bitcast(F32), ALU.subtract)\
                   .then_inc(low_done, 1)

            def tile(g, c, j, b, collected):
                n = step(g, c, j)
                dve.wait_ge(silu_done, n + 1)
                dve.tensor_tensor(h[:, b, :], h[:, b, :], psU[b][:, :], ALU.mult).then_inc(gu_done, 1)
                dve.wait_ge(gu_done, n + 1)
                dve.tensor_tensor(h[:, b, :], h[:, b, :], psC[b][:, :], ALU.mult).then_inc(h_done, 1)
                if collected:
                    collect(*collected, 0)
                dve.wait_ge(hi_done, n + 1)
                dve.tensor_tensor(h_lo[:, b, :], h[:, b, :], h_hi[:, b, :].bitcast(F32), ALU.subtract).then_inc(lo_done, 1)

                if collected:
                    collect(*collected, 1)

            def collect(g, c, half):
                dve.wait_ge(y_done, g * CHUNKS + c + 1)
                a = acc[:, bass.ds(c * TPC + 2 * half, 2), :]
                dve.tensor_tensor(a, a, psY[:, 2 * half:2 * half + 2, :], ALU.add).then_inc(y_out, 1)

            def chunk(g, c, cpar):
                if not isinstance(c, int) or c:
                    last = (g, c - 1)
                else:
                    last = (g - 1, CHUNKS - 1) if g else None
                for j in range(G):
                    in_splits(g, c, j, weights, lambda: tile(g, c, j, b_of(g, cpar, j), last if j == 0 else None))

            def tail():
                for half in range(2):
                    collect(NG - 1, CHUNKS - 1, half)
            dve.wait_ge(zeroed, 1)
            groups(dve, chunk, tail)
            dve.wait_ge(y_out, 2 * NG * CHUNKS)

        @block.scalar
        def _(act):
            def weights(w):
                g, j = divmod(w, G)
                act.wait_ge(raw_in[w % RAW], 16 * (w // RAW + 1))
                if g:
                    act.wait_ge(down_done, step(g - 1, CHUNKS - 1, j) + 1)
                act.activation(w_hi[:, j, :], raw[:, w % RAW, :], ACT.Copy).then_inc(hiw_done, 1)

            def tile(g, c, j, b):
                n = step(g, c, j)
                act.wait_ge(up_done, n + 1)
                if not (isinstance(n, int) and n < 2):
                    act.wait_ge(lo_done, n - 1)
                act.activation(h[:, b, :], psG[b][:, :], ACT.Silu).then_inc(silu_done, 1)
                act.wait_ge(h_done, n + 1)
                if not (isinstance(n, int) and n < 2):
                    act.wait_ge(down_done, n - 1)
                act.activation(h_hi[:, b, :], h[:, b, :], ACT.Copy).then_inc(hi_done, 1)

            def chunk(g, c, cpar):
                for j in range(G):
                    in_splits(g, c, j, weights, lambda: tile(g, c, j, b_of(g, cpar, j)))
            groups(act, chunk, lambda: None)

        @block.tensor
        def _(pe):
            def up(g, c, j, b):
                n = step(g, c, j)
                if not (isinstance(n, int) and n < 2):
                    pe.wait_ge(h_done, n - 1)
                x_hi = lambda k: XT_hi[:, k, bass.ds(c * CHUNK, CHUNK)]
                x_lo = lambda k: XT_lo[:, k, bass.ds(c * CHUNK, CHUNK)]
                for half, out in ((0, psG[b]), (1, psU[b])):
                    col = lambda k: (half * KT + k) * P
                    three_passes(pe, out[:, :], lambda k: w_hi[:, j, col(k):col(k) + P],
                                 lambda k: w_lo[:, j, col(k):col(k) + P], x_hi, x_lo, KT)
                pe.matmul(psC[b][:, :], w_hi[0:PADDED, j, WT:WTS], CT[:, bass.ds(c * CHUNK, CHUNK)], start=True, stop=True)\
                    .then_inc(up_done, 1)

            def down(g, c, j, b):
                n = step(g, c, j)
                pe.wait_ge(lo_done, n + 1)
                for m in range(TPC):
                    if j == 0 and m % 2 == 0 and not (isinstance(c, int) and g * CHUNKS + c == 0):
                        pe.wait_ge(y_out, (g * CHUNKS + c) * 2 + (m // 2 - 1))
                    ins = three_passes(pe, psY[:, m, :], lambda k: h_hi[:, b, m * P:(m + 1) * P],
                                       lambda k: h_lo[:, b, m * P:(m + 1) * P],
                                       lambda k: w_hi[:, j, 2 * KT * P:WT], lambda k: w_lo[:, j, 2 * KT * P:WT], 1,
                                       first=j == 0 and m % 2 == 0, last=j == G - 1, check=True)
                ins.then_inc(down_done, 1)
                if j == G - 1:
                    pe.wait_ge(down_done, n + 1)
                    pe.sem_inc(y_done, 1)

            def chunk(g, c, cpar):
                for j in range(G):
                    if isinstance(c, int) and c == 0:
                        pe.wait_ge(low_done, g * G + j + 1)
                    up(g, c, j, b_of(g, cpar, j))
                    if j:
                        down(g, c, j - 1, b_of(g, cpar, j - 1))
                    elif not isinstance(c, int) or c:
                        down(g, c - 1, G - 1, b_of(g, 1 - cpar, G - 1))
                    elif g:
                        down(g - 1, CHUNKS - 1, G - 1, b_of(g - 1, 1, G - 1))
            groups(pe, chunk, lambda: down(NG - 1, CHUNKS - 1, G - 1, b_of(NG - 1, 1, G - 1)))


def gate_and_add(nc, tag, x_dram, s_dram, acc, out_dram, count=None, shared=None):
    with phase(nc, shared) as (ctx, block):
        def sem(name):
            return new_semaphore(nc, ctx, f"{tag}_{name}")
        STEP = 4
        xt = ctx.enter_context(nc.sbuf_tensor(f"{tag}_xt", [P, 2, STEP, HID], F32))
        stt = ctx.enter_context(nc.sbuf_tensor(f"{tag}_stt", [P, 2, STEP, HID], F32))
        gate = ctx.enter_context(nc.sbuf_tensor(f"{tag}_gate", [P, 2, STEP, HID], F32))
        x_in, s_in = [sem("x_in0"), sem("x_in1")], [sem("s_in0"), sem("s_in1")]
        gate_done, mul_done, sum_done, stored = (sem(x) for x in ("gate_done", "mul_done", "sum_done", "stored"))
        N = TILES // STEP

        @block.sync
        def _(sp):
            for t in range(N):
                if t >= 2:
                    sp.wait_ge(sum_done, t - 1)
                for src, dst, sems in ((x_dram, xt, x_in), (s_dram, stt, s_in)):
                    sp.dma_start(dst[:, t % 2, :, :], src[t * STEP:(t + 1) * STEP].rearrange("t p n -> p t n"))\
                        .then_inc(sems[t % 2], 16)

        @block.gpsimd
        def _(pool):
            for t in range(N):
                pool.wait_ge(sum_done, t + 1)
                pool.dma_start(out_dram[t * STEP:(t + 1) * STEP].rearrange("t p n -> p t n"),
                               acc[:, t * STEP:(t + 1) * STEP, :]).then_inc(stored, 16)
            pool.wait_ge(stored, 16 * N)

        @block.scalar
        def _(act):
            for t in range(N):
                if t >= 2:
                    act.wait_ge(mul_done, t - 1)
                act.activation(gate[:, t % 2, :, :], acc[:, t * STEP:(t + 1) * STEP, :], ACT.Silu).then_inc(gate_done, 1)

        @block.vector
        def _(dve):
            for t in range(N):
                b = t % 2
                dve.wait_ge(gate_done, t + 1)
                dve.wait_ge(s_in[b], 16 * (t // 2 + 1))
                dve.tensor_tensor(stt[:, b, :, :], stt[:, b, :, :], gate[:, b, :, :], ALU.mult).then_inc(mul_done, 1)
                dve.wait_ge(mul_done, t + 1)
                dve.wait_ge(x_in[b], 16 * (t // 2 + 1))
                dve.tensor_tensor(acc[:, t * STEP:(t + 1) * STEP, :], stt[:, b, :, :], xt[:, b, :, :], ALU.add)\
                   .then_inc(sum_done, 1)
                if count:
                    dve.wait_ge(sum_done, t + 1)
                    for tile in range(t * STEP, (t + 1) * STEP):
                        count(dve, tile)


def causal_attention(nc, qk_dram, v_dram, ident, mask_qk, ident_b, m_dram, ao_dram, shared=None):
    SLOTS = 3
    with phase(nc, shared) as (ctx, block):
        def sem(name):
            return new_semaphore(nc, ctx, f"ca_{name}")

        def sb(name, shape, dt=F32):
            return ctx.enter_context(nc.sbuf_tensor(f"ca_{name}", shape, dt))
        QS, KS = sb("QS", [PADDED, SLOTS, GH, SEQ], F32R), sb("KS", [PADDED, SLOTS, GH, SEQ], F32R)
        zero_rows = sb("zero_rows", [2, CHUNK])
        VA = sb("VA", [P, SLOTS, POS_TILES, GH * STRIP])
        PT = sb("PT", [P, 2, GH, CHUNK])
        units = [(qt, k0, w, h0, min(CHUNK // w, GH)) for qt in range(POS_TILES)
                 for k0, w in [(k, min(CHUNK, (qt + 1) * P - k)) for k in range(0, (qt + 1) * P, CHUNK)]
                 for h0 in range(0, GH, min(CHUNK // w, GH))]
        NU = len(units)
        steps = [(c, kt, max(kt * P - c * CHUNK, 0)) for c in range(SPAN) for kt in range((c + 1) * TPC)]
        NS = len(steps)
        cut_steps = [s for s, (c, kt, _) in enumerate(steps) if kt * P >= c * CHUNK]
        WHOLE, FIRST = 7, NU * 7 // 16
        ORDER = "0u1u2u3uv"
        ahead = [list(range(FIRST + (NU - FIRST) * s // WHOLE, FIRST + (NU - FIRST) * (s + 1) // WHOLE)) if s < WHOLE else
                 list(range(FIRST * (s - WHOLE) // (NS - WHOLE), FIRST * (s - WHOLE + 1) // (NS - WHOLE))) for s in range(NS)]
        assert NS * GH % SLOTS == 0
        last_step = [max(s for s, (c, _, _) in enumerate(steps) if c == cc) for cc in range(SPAN)]
        part = sb("part", [P, SPAN, GH, POS_TILES])
        maxima = sb("maxima", [P, GH, POS_TILES])
        NR = GH * POS_TILES
        m_f, m_hi, m_lo = sb("m_f", [NR, P]), sb("m_hi", [NR, P], F32R), sb("m_lo", [NR, P], F32R)
        OT = sb("OT", [P, CHUNK])
        rsum = sb("rsum", [P, TPC, GH])
        waited = sb("waited", [1, 3])
        o_sb = sb("o_sb", [P, 2, TPC, GH, D])
        psM = [ctx.enter_context(nc.psum_tensor(f"ca_psM{i}", [P, CHUNK], F32)) for i in range(SLOTS)]
        psS = [ctx.enter_context(nc.psum_tensor(f"ca_psS{i}", [P, CHUNK], F32)) for i in range(SLOTS)]
        psO = ctx.enter_context(nc.psum_tensor("ca_psO", [P, CHUNK], F32))
        psX = ctx.enter_context(nc.psum_tensor("ca_psX", [P, CHUNK], F32))
        (ones_done, zeros_done, unit_done, unit_out, whole_done, mT_done, m_neg, mhi_done, mlo_done, s_done, exp_done, cut_done, pv_done,
         ot_out, oT_done, sum_done, o_out, m_kept) = (sem(x) for x in (
             "ones_done", "zeros_done", "unit_done", "unit_out", "whole_done", "mT_done", "m_neg", "mhi_done", "mlo_done",
             "s_done", "exp_done", "cut_done", "pv_done", "ot_out", "oT_done", "sum_done", "o_out", "m_kept"))
        stack_in = [sem(f"stack_in{i}") for i in range(SLOTS)]
        m_in = [sem(f"m_in{i}") for i in range(SLOTS)]
        ao_stored = [sem("ao_stored0"), sem("ao_stored1")]
        LOADS = 10

        def rounds(eng, both, front, back):
            front()
            both(0, 0, 0, True)
            with eng.Fori(0, (ROUNDS - 1) // SLOTS - 1) as i:
                for k in range(1, SLOTS + 1):
                    both(i * SLOTS + k, k % SLOTS, i + k // SLOTS, True)
            for n in range(ROUNDS - SLOTS, ROUNDS - 1):
                both(n, n % SLOTS, n // SLOTS, n + 2 < ROUNDS)
            back(ROUNDS - 1, (ROUNDS - 1) % SLOTS, (ROUNDS - 1) // SLOTS)

        def first(n):
            return isinstance(n, int) and n == 0

        @block.sync
        def _(sp):
            def pull(n, slot):
                at = sp.snap(n) if not isinstance(n, int) else n
                if not (isinstance(n, int) and n < SLOTS):
                    sp.wait_ge(oT_done, (n - SLOTS + 1) * SPAN)
                for side, dst, order in ((0, QS, (0, 0, 1, 1)), (1, KS, (0, 1, 0, 1))):
                    for r, half in enumerate(order):
                        sp.dma_start(dst[r * D:(r + 1) * D, slot, :, :].bitcast(F32),
                                     qk_dram[half, side, bass.ds(at, 1), :, :].rearrange("a (h r) n -> r (a h) n", h=GH))\
                            .then_inc(stack_in[slot], 16)
                sp.dma_start(QS[STACK:ROWS, slot, :, :].rearrange("r h (c n) -> r (h c) n", n=CHUNK).bitcast(F32),
                             zero_rows[:, :].unsqueeze(1).broadcast_to([2, GH * SPAN, CHUNK])).then_inc(stack_in[slot], 16)
                sp.dma_start(VA[:, slot, :, :], v_dram[bass.ds(at, 1), :, :, :].rearrange("a t p c -> p (a t) c"))\
                    .then_inc(stack_in[slot], 16)

            def maxima_rows(n, slot):
                sp.wait_ge(mlo_done, n + 1)
                for r, m in enumerate((m_hi, m_lo)):
                    sp.dma_start(m_dram[r], m[:, :].bitcast(F32)).then_inc(m_kept, 16)
                sp.wait_ge(m_kept, n * 32 + 32)
                sp.dma_start(QS[STACK:ROWS, slot, :, :].rearrange("r h n -> r (h n)").bitcast(F32),
                             m_dram.rearrange("r m p -> r (m p)")).then_inc(m_in[slot], 16)

            def output(n, c):
                at = sp.snap(n) if not isinstance(n, int) else n
                sp.wait_ge(o_out, n * SPAN + c + 1)
                sp.dma_start(ao_dram[bass.ds(at, 1), c * TPC:(c + 1) * TPC, :, :].rearrange("a t p c -> p (a t) c"),
                             o_sb[:, c, :, :, :].rearrange("p t h d -> p t (h d)")).then_inc(ao_stored[c], 16)
            sp.wait_ge(zeros_done, 2 + 2 * SLOTS)
            for n in range(SLOTS - 1):
                pull(n, n)
            maxima_rows(0, 0)

            def beside(n, slot, last=False):
                if not first(n):
                    output(n - 1, SPAN - 1)
                if not last:
                    pull(n + SLOTS - 1, (slot + SLOTS - 1) % SLOTS)
                output(n, 0)
                maxima_rows(n + 1, (slot + 1) % SLOTS)
            beside(0, 0)
            with sp.Fori(0, (ROUNDS - 1) // SLOTS - 1) as i:
                for k in range(1, SLOTS + 1):
                    beside(i * SLOTS + k, k % SLOTS)
            for n in range(ROUNDS - SLOTS, ROUNDS - 1):
                beside(n, n % SLOTS, n + SLOTS > ROUNDS)
            output(ROUNDS - 2, SPAN - 1)
            for c in range(SPAN):
                output(ROUNDS - 1, c)
                sp.wait_ge(ao_stored[c], 16 * ROUNDS)

        @block.gpsimd
        def _(pool):
            pool.memset(zero_rows[:, :], 0.0).then_inc(zeros_done, 1)
            pool.memset(waited[:, :], 0.0).then_inc(zeros_done, 1)
            for slot in range(SLOTS):
                pool.memset(QS[STACK:PADDED, slot, :, :].bitcast(F32), 0.0).then_inc(zeros_done, 1)
                pool.memset(KS[STACK:PADDED, slot, :, :].bitcast(F32), 0.0).then_inc(zeros_done, 1)
            pool.wait_ge(zeros_done, 2 + 2 * SLOTS)
            for slot in range(SLOTS):
                pool.memset(KS[STACK:ROWS, slot, :, :].bitcast(F32), 1.0).then_inc(ones_done, 1)

            def cuts(n):
                for d, s in enumerate(cut_steps):
                    off = steps[s][2]
                    pool.wait_ge(exp_done, n * (GH * NS) + GH * s + GH)
                    diagonal = PT[:, s % 2, :, off:off + P]
                    pool.tensor_tensor(waited[:, s % 2:s % 2 + 1], waited[:, 2:3], waited[:, 2:3], ALU.mult).then_inc(cut_done, 1)
                    pool.affine_select(out=diagonal, in_=diagonal, compare_op=ALU.is_ge, fill=0.0, base=0,
                                       pattern=[[0, GH], [1, P]], channel_multiplier=-1).then_inc(cut_done, 1)
            rounds(pool, lambda n, *_: cuts(n), lambda: None, lambda n, *_: cuts(n))

        @block.vector
        def _(dve):
            def unit(n, slot, u):
                qt, k0, w, h0, nh = units[u]
                dve.wait_ge(unit_done, n * NU + u + 1)
                if u == 0 and not first(n):
                    dve.wait_ge(whole_done, n * 2)
                dst = part[:, k0 // CHUNK, h0:h0 + nh, qt]
                dve.tensor_reduce(dst, psM[(slot * NU + u) % SLOTS][:, 0:nh * w].rearrange("p (h k) -> p h k", h=nh), AX.X, ALU.max)\
                   .then_inc(unit_out, 1)

            def whole(n):
                dve.wait_ge(unit_out, n * NU + NU)
                lower, upper = part[:, 0, :, :], part[:, 1, :, TPC:]
                if not first(n):
                    dve.wait_ge(mT_done, n)
                dve.tensor_copy(maxima[:, :, 0:TPC], lower[:, :, 0:TPC]).then_inc(whole_done, 1)
                dve.tensor_tensor(maxima[:, :, TPC:], lower[:, :, TPC:], upper, ALU.max).then_inc(whole_done, 1)
                dve.wait_ge(mT_done, n + 1)
                if not first(n):
                    slot_of_last(n)
                dve.tensor_scalar(m_f[:, :], psX[0:NR, 0:P], -1.0, None, ALU.mult).then_inc(m_neg, 1)
                dve.wait_ge(m_neg, n + 1)
                dve.tensor_copy(m_hi[:, :], m_f[:, :]).then_inc(mhi_done, 1)
                dve.wait_ge(mhi_done, n + 1)
                dve.tensor_tensor(m_lo[:, :], m_f[:, :], m_hi[:, :].bitcast(F32), ALU.subtract).then_inc(mlo_done, 1)

            def slot_of_last(n):
                dve.wait_ge(s_done, (n - 1) * (GH * NS) + 1)

            def collect(n, c):
                dve.wait_ge(pv_done, n * NS + last_step[c] + 1)
                dve.tensor_copy(OT[:, :], psO[:, :]).then_inc(ot_out, 1)

            def divide(n, c):
                dve.wait_ge(oT_done, n * SPAN + c + 1)
                o4 = psX[:, :].rearrange("p (q h d) -> p q h d", q=TPC, h=GH)
                dve.reciprocal(rsum[:, :, :], o4[:, :, :, D]).then_inc(sum_done, 1)
                dve.wait_ge(sum_done, n * SPAN + c + 1)
                if not first(n):
                    dve.wait_ge(ao_stored[c], n * 16)
                dve.tensor_tensor(o_sb[:, c, :, :, :], o4[:, :, :, 0:D], rsum[:, :, :].unsqueeze(3).broadcast_to([P, TPC, GH, D]),
                                  ALU.mult).then_inc(o_out, 1)

            def both(n, slot, turn, two_ahead):
                for s in range(NS):
                    for u in ahead[s]:
                        if s < WHOLE:
                            unit(n + 1, (slot + 1) % SLOTS, u)
                        elif two_ahead:
                            unit(n + 2, (slot + 2) % SLOTS, u)
                    if s == last_step[0] + 1:
                        collect(n, 0)
                    if s == last_step[0] + 2:
                        divide(n, 0)
                    if s == WHOLE - 1:
                        whole(n + 1)
                collect(n, 1)
                divide(n, 1)

            def front():
                for u in range(NU):
                    unit(0, 0, u)
                whole(0)
                for u in range(FIRST):
                    unit(1, 1, u)

            def back(n, slot, turn):
                for c in range(SPAN):
                    collect(n, c)
                    divide(n, c)
            rounds(dve, both, front, back)

        @block.scalar
        def _(act):
            def exps(n):
                for s, (c, kt, off) in enumerate(steps):
                    if s >= 2 or not first(n):
                        act.wait_ge(pv_done, n * NS + s - 1)
                    for h in range(GH):
                        act.wait_ge(s_done, n * (GH * NS) + GH * s + h + 1)
                        act.activation(PT[:, s % 2, h, off:CHUNK], psS[(GH * s + h) % SLOTS][:, off:CHUNK], ACT.Exp)\
                           .then_inc(exp_done, 1)
            rounds(act, lambda n, *_: exps(n), lambda: None, lambda n, *_: exps(n))

        @block.tensor
        def _(pe):
            def unit(n, slot, u):
                qt, k0, w, h0, nh = units[u]
                bank = psM[(slot * NU + u) % SLOTS]
                if u >= SLOTS or not first(n):
                    pe.wait_ge(unit_out, n * NU + u - (SLOTS - 1))
                diag = k0 + w == (qt + 1) * P
                for h in range(nh):
                    ins = pe.matmul(bank[:, h * w:(h + 1) * w], QS[:, slot, h0 + h, qt * P:(qt + 1) * P],
                                    KS[:, slot, h0 + h, k0:k0 + w], start=True, stop=not diag, skip_group_check=True)
                if diag:
                    m = min(w, 2 * P)
                    mask = mask_qk[:, 2 * P - m:2 * P].unsqueeze(1).broadcast_to([P, nh, m])
                    ins = pe.matmul(bank[:, 0:nh * w].rearrange("p (h k) -> p h k", h=nh)[:, :, w - m:w], ident_b[:, :], mask,
                                    start=False, stop=True, skip_group_check=True)
                ins.then_inc(unit_done, 1)

            def transpose_maxima(n):
                pe.wait_ge(whole_done, n * 2 + 2)
                if not first(n):
                    pe.wait_ge(o_out, (n - 1) * SPAN + 1)
                pe.transpose(psX[0:NR, 0:P], maxima[:, :, :].rearrange("p h t -> p (h t)"), ident[:, :]).then_inc(mT_done, 1)

            def scores(n, slot, s, h):
                c, kt, off = steps[s]
                tile = GH * s + h
                if tile >= SLOTS or not first(n):
                    pe.wait_ge(exp_done, n * (GH * NS) + tile - (SLOTS - 1))
                pe.matmul(psS[tile % SLOTS][:, off:CHUNK], KS[:, slot, h, kt * P:(kt + 1) * P],
                          QS[:, slot, h, c * CHUNK + off:(c + 1) * CHUNK], start=True, stop=True).then_inc(s_done, 1)

            def values(n, slot, s):
                c, kt, off = steps[s]
                if s in cut_steps:
                    pe.wait_ge(cut_done, (n * len(cut_steps) + cut_steps.index(s)) * 2 + 2)
                else:
                    pe.wait_ge(exp_done, n * (GH * NS) + GH * s + GH)
                if kt == 0 and not (first(n) and c == 0):
                    pe.wait_ge(ot_out, n * SPAN + c)
                for h in range(GH):
                    ins = pe.matmul(psO[STRIP * h:STRIP * (h + 1), off:CHUNK], VA[:, slot, kt, STRIP * h:STRIP * (h + 1)],
                                    PT[:, s % 2, h, off:CHUNK], start=kt == 0, stop=s == last_step[c],
                                    tile_position=(0, STRIP * h), skip_group_check=True)
                ins.then_inc(pv_done, 1)

            def transpose_out(n, c):
                pe.wait_ge(ot_out, n * SPAN + c + 1)
                if c == 0:
                    if not first(n):
                        pe.wait_ge(o_out, n * SPAN)
                else:
                    pe.wait_ge(o_out, n * SPAN + 1)
                    if not (isinstance(n, int) and n == ROUNDS - 1):
                        pe.wait_ge(m_neg, n + 2)
                for q in range(TPC):
                    ins = pe.transpose(psX[:, q * P:(q + 1) * P], OT[:, q * P:(q + 1) * P], ident[:, :])
                ins.then_inc(oT_done, 1)

            def front():
                pe.wait_ge(stack_in[0], 16 * LOADS)
                for u in range(NU):
                    unit(0, 0, u)
                transpose_maxima(0)
                pe.wait_ge(stack_in[1], 16 * LOADS)
                for u in range(FIRST):
                    unit(1, 1, u)

            def both(n, slot, turn, two_ahead):
                pe.wait_ge(m_in[slot], turn * 16 + 16)
                for s in range(NS):
                    todo = [(n + 1 + s // WHOLE, (slot + 1 + s // WHOLE) % SLOTS, u) for u in ahead[s]]
                    if s >= WHOLE and not two_ahead:
                        todo = []
                    if s == WHOLE and two_ahead:
                        pe.wait_ge(stack_in[(slot + 2) % SLOTS], (turn + (slot + 2) // SLOTS) * (16 * LOADS) + 16 * LOADS)
                    for part in ORDER:
                        if part == "u":
                            if todo:
                                unit(*todo.pop(0))
                        elif part == "v":
                            if s:
                                values(n, slot, s - 1)
                        else:
                            scores(n, slot, s, int(part))
                    for t in todo:
                        unit(*t)
                    if s == last_step[0] + 2:
                        transpose_out(n, 0)
                    if s == WHOLE - 1:
                        transpose_maxima(n + 1)
                values(n, slot, NS - 1)
                transpose_out(n, 1)

            def back(n, slot, turn):
                pe.wait_ge(m_in[slot], turn * 16 + 16)
                for s in range(NS):
                    for h in range(GH):
                        scores(n, slot, s, h)
                    if s:
                        values(n, slot, s - 1)
                    if s == last_step[0] + 2:
                        transpose_out(n, 0)
                values(n, slot, NS - 1)
                transpose_out(n, 1)
            pe.wait_ge(ones_done, SLOTS)
            rounds(pe, both, front, back)


def project_out(nc, tag, o_tile, s_dram, ident, wo_dram, bo_dram, scale, shared=None):
    with phase(nc, shared) as (ctx, block):
        def sem(name):
            return new_semaphore(nc, ctx, f"{tag}_{name}")

        def sb(name, shape):
            return ctx.enter_context(nc.sbuf_tensor(f"{tag}_{name}", shape, F32))
        BUFS = 4
        wo, bo = sb("wo", [P, KT, HID]), sb("bo", [P, HID])
        wo_in, bo_in = sem("wo_in"), sem("bo_in")
        o_st, oT, s_sb = sb("o_st", [P, BUFS, HID]), sb("oT", [P, 2, HID]), sb("s_sb", [P, BUFS, HID])
        psT = [ctx.enter_context(nc.psum_tensor(f"{tag}_psT{i}", [P, HID], F32)) for i in range(2)]
        psS = [ctx.enter_context(nc.psum_tensor(f"{tag}_psS{i}", [P, HID], F32)) for i in range(2)]
        oT_done, oT_out, s_done, s_out = (sem(x) for x in ("oT_done", "oT_out", "s_done", "s_out"))
        staged = [sem(f"staged{i}") for i in range(BUFS)]
        stored = [sem(f"stored{i}") for i in range(BUFS)]

        @block.gpsimd
        def _(pool):
            def load(t, i, b):
                if late(t, BUFS):
                    pool.wait_ge(oT_done, t - (BUFS - 1))
                src = o_tile(b, i)
                pool.dma_start(o_st[:, i % BUFS, :].rearrange("p (g n) -> p g n", g=src.shape[1]), src)\
                    .then_inc(staged[i % BUFS], 16)
            in_steps(pool, (0, load))

        @block.tensor
        def _(pe):
            def transpose(t, i, b):
                pe.wait_ge(staged[i % BUFS], (t - i % BUFS) * 4 + 16)
                if late(t, 2):
                    pe.wait_ge(oT_out, t - 1)
                for k in range(KT):
                    ins = pe.transpose(psT[i % 2][:, k * P:(k + 1) * P], o_st[:, i % BUFS, k * P:(k + 1) * P], ident[:])
                ins.then_inc(oT_done, 1)

            def project(t, i, b):
                pe.wait_ge(oT_out, t + 1)
                if late(t, 2):
                    pe.wait_ge(s_out, t - 1)
                for k in range(KT):
                    ins = pe.matmul(psS[i % 2][:], oT[:, i % 2, k * P:(k + 1) * P], wo[:, k, :], start=k == 0, stop=k == KT - 1)
                ins.then_inc(s_done, 1)
            pe.wait_ge(wo_in, 16)
            in_steps(pe, (0, transpose), (1, project))

        @block.scalar
        def _(act):
            def take(t, i, b):
                act.wait_ge(oT_done, t + 1)
                if late(t, 2):
                    act.wait_ge(s_done, t - 1)
                act.activation(oT[:, i % 2, :], psT[i % 2][:], ACT.Copy).then_inc(oT_out, 1)
            in_steps(act, (0, take))

        @block.vector
        def _(dve):
            def add_bias(t, i, b):
                dve.wait_ge(s_done, t + 1)
                if late(t, BUFS):
                    dve.wait_ge(stored[i % BUFS], (t - i % BUFS) * 4)
                dve.scalar_tensor_tensor(s_sb[:, i % BUFS, :], psS[i % 2][:], scale, bo[:], ALU.mult, ALU.add).then_inc(s_out, 1)
            dve.wait_ge(bo_in, 16)
            in_steps(dve, (0, add_bias))

        @block.sync
        def _(sp):
            def store(t, i, b):
                row = sp.snap(t) if not isinstance(t, int) else t
                sp.wait_ge(s_out, t + 1)
                sp.dma_start(s_dram[bass.ds(row, 1), :, :].rearrange("a p n -> p (a n)"), s_sb[:, i % BUFS, :])\
                    .then_inc(stored[i % BUFS], 16)
            sp.dma_start(wo[:], wo_dram).then_inc(wo_in, 16)
            sp.dma_start(bo[:], bo_dram.partition_broadcast(P)).then_inc(bo_in, 16)
            in_steps(sp, (0, store))
            for i in range(BUFS):
                sp.wait_ge(stored[i], 16 * TILES // BUFS)


def build(nc, a, out):
    x_v = a["x"].rearrange("(t p) n -> t p n", p=P)
    out_v = out.rearrange("b (t p) n -> (b t) p n", p=P)
    s0_dram = nc.dram_tensor("s0_scratch", [TILES, P, HID], F32, kind="Internal").ap()
    s1_dram = nc.dram_tensor("s1_scratch", [TILES, P, HID], F32, kind="Internal").ap()
    o_dram = nc.dram_tensor("o_scratch", [BATCH, HEADS, SEQ, D], F32, kind="Internal").ap()
    qk_dram = nc.dram_tensor("qk_scratch", [2, 2, ROUNDS, GH * D, SEQ], F32, kind="Internal").ap()
    v_dram = nc.dram_tensor("v_scratch", [ROUNDS, POS_TILES, P, GH * STRIP], F32, kind="Internal").ap()
    m_dram = nc.dram_tensor("m_scratch", [2, GH * POS_TILES, P], F32, kind="Internal").ap()
    ao_dram = nc.dram_tensor("ao_scratch", [ROUNDS, POS_TILES, P, GH * D], F32, kind="Internal").ap()
    x1_dram = nc.dram_tensor("x1_scratch", [TILES, P, HID], F32, kind="Internal").ap()
    with ExitStack() as top:
        def sb(ctx, name, shape, dt=F32):
            return ctx.enter_context(nc.sbuf_tensor(name, shape, dt))
        XT_hi, XT_lo = sb(top, "XT_hi", [P, KT, TOKENS], F32R), sb(top, "XT_lo", [P, KT, TOKENS], F32R)
        ident = sb(top, "ident", [P, P])
        mean_rstd = sb(top, "mean_rstd", [P, TILES, 2])
        logits = sb(top, "logits", [P, TILES, RW1])

        def row(ap):
            return ap.rearrange("(a n) -> a n", a=1).partition_broadcast(P)

        with ExitStack() as c:
            with ExitStack() as c2:
                x_sb = sb(c2, "x_sb", [P, TILES, HID])
                wqkv_raw, wr_raw = sb(c2, "wqkv0_raw", [P, KT, 512]), sb(c2, "wr0_raw", [P, KT, E0])
                wqkv = [sb(c2, f"wqkv0_{half}", [P, KT, 512], F32R) for half in ("hi", "lo")]
                wr = [sb(c2, f"wr0_{half}", [P, KT, E0], F32R) for half in ("hi", "lo")]
                rblk, bias_raw = sb(c2, "rblk", [P, 64]), sb(c2, "bias0_raw", [1, 512])
                bias = [sb(c2, f"bias0_{half}", [1, 512], F32R) for half in ("hi", "lo")]
                cos, sin = sb(c2, "cos", [P, POS_TILES, D]), sb(c2, "sin", [P, POS_TILES, D])
                with phase(nc) as start:
                    split_weights(nc, "w0", [(wqkv_raw[:], wqkv[0][:], wqkv[1][:]), (wr_raw[:], wr[0][:], wr[1][:]),
                                             (bias_raw[:], bias[0][:], bias[1][:])], [
                        (ident[:], a["ident"]), (wqkv_raw[:], a["wqkv0"]), (wr_raw[:], a["wr0"]), (rblk[:], a["rblk"]),
                        (bias_raw[:], a["bias0"].rearrange("(a n) -> a n", a=1)), (cos[:], a["cos"]), (sin[:], a["sin"])],
                                  shared=start)
                    standardise(nc, "ln0", mean_rstd, lambda ctx: tile_statistics(nc, ctx, "ln0", x_sb, mean_rstd),
                                lambda sp, i: sp.dma_start(x_sb[:, 4 * i:4 * i + 4, :],
                                                           x_v[4 * i:4 * i + 4].rearrange("t p n -> p t n")), start)
                first_attention(nc, x_sb, mean_rstd, XT_hi, XT_lo, logits[:, :, 0:E0], wr, wqkv, bias, cos, sin, rblk, ident,
                                o_dram)
            o_rows = o_dram.rearrange("b h s d -> (b h s d)").rearrange("(b t p n) -> b t p n", b=BATCH, p=P, n=HID)
            acc = sb(c, "acc0", [P, TILES, HID])
            with ExitStack() as c2:
                CT = sb(c2, "CT0", [PADDED, TOKENS], F32R)
                with phase(nc) as both:
                    route(nc, "r0", logits[:, :, 0:E0], E0, E0, TOP0, 1e-20, CT, ident, both)
                    project_out(nc, "po0", lambda s, i: o_rows[bass.ds(s, 1), i].rearrange("a p n -> p a n"), s0_dram, ident,
                                a["wo0"], a["bo0"], SHARE, both)
                experts(nc, "f0", a["ffn0"], NT0, G0, RAW0, E0, XT_hi, XT_lo, CT, acc)
            W3 = 3 * HID
            w_raw = sb(c, "wqkvr1_raw", [P, KT, W3 + RW1])
            wqk = [sb(c, f"wqk1_{half}", [P, KT, 2 * HID], F32R) for half in ("hi", "lo")]
            wvr = [sb(c, f"wvr1_{half}", [P, KT, HID + RW1], F32R) for half in ("hi", "lo")]
            b_raw, bias_qk, bias_v = sb(c, "b_raw", [P, QK_TILES]), sb(c, "bias_qk", [P, QK_TILES]), sb(c, "bias_v", [P, HID])
            with phase(nc) as middle:
                statistics = tile_statistics(nc, middle[0], "ln1", acc, mean_rstd)
                gate_and_add(nc, "g0", x_v, s0_dram, acc, x1_dram, statistics[0], middle)
                split_weights(nc, "w1", [(w_raw[:, :, 0:2 * HID], wqk[0][:], wqk[1][:]),
                                         (w_raw[:, :, 2 * HID:], wvr[0][:], wvr[1][:])],
                              [(w_raw[:], a["wqkvr1"]), (b_raw[:], a["bias_qk1"]), (bias_v[:], a["bias_v1"].partition_broadcast(P))],
                              scale=[(w_raw[:, :, 0:HID], w_raw[:, :, 0:HID], 0.25), (bias_qk[:, 0:KT], b_raw[:, 0:KT], 0.25),
                                     (bias_qk[:, KT:QK_TILES], b_raw[:, KT:QK_TILES], 1.0)], shared=middle)
                standardise(nc, "ln1", mean_rstd, lambda ctx: statistics, shared=middle)
            project_second(nc, acc, mean_rstd, XT_hi, XT_lo, logits, wqk, wvr, bias_qk, bias_v, ident, qk_dram, v_dram)
        with ExitStack() as c:
            ident_b, mask_qk = sb(c, "ident_b", [P, P], BF16), sb(c, "mask_qk", [P, 2 * P], BF16)
            masks(nc, ident_b, mask_qk)
            causal_attention(nc, qk_dram, v_dram, ident, mask_qk, ident_b, m_dram, ao_dram)
            ao_rows = ao_dram.rearrange("(b g) t p n -> b t p g n", g=GROUPS)
            acc = sb(c, "acc1", [P, TILES, HID])
            with ExitStack() as c2:
                CT = sb(c2, "CT1", [PADDED, TOKENS], F32R)
                with phase(nc) as both:
                    route(nc, "r1", logits[:, :, 0:E1 + 1], E1 + 1, E1, TOP1, 0.0, CT, ident, both)
                    project_out(nc, "po1", lambda s, i: ao_rows[bass.ds(s, 1), i].rearrange("a p g n -> p (a g) n"), s1_dram,
                                ident, a["wo1"], a["bo1"], 1.0, both)
                experts(nc, "f1", a["ffn1"], NT1, G1, RAW1, E1 + 1, XT_hi, XT_lo, CT, acc)
            gate_and_add(nc, "g1", x1_dram, s1_dram, acc, out_v)


def masks(nc, ident_b, mask_qk, shared=None):
    with phase(nc, shared) as (ctx, block):
        filled = new_semaphore(nc, ctx, "mk_filled")
        done = new_semaphore(nc, ctx, "mk_done")

        @block.gpsimd
        def _(pool):
            for m in (ident_b, mask_qk):
                pool.memset(m[:, :], 0.0).then_inc(filled, 1)
            pool.wait_ge(filled, 2)
            pool.affine_select(out=ident_b[:, :], in_=ident_b[:, :], compare_op=ALU.not_equal, fill=1.0, base=0,
                               pattern=[[-1, P]], channel_multiplier=1).then_inc(done, 1)
            diagonal = mask_qk[:, P:2 * P]
            pool.affine_select(out=diagonal, in_=diagonal, compare_op=ALU.is_ge, fill=NEG, base=0,
                               pattern=[[-1, P]], channel_multiplier=1).then_inc(done, 1)
            pool.wait_ge(done, 2)


def kernel(**inputs):
    import numpy as np
    import concourse.bacc as bacc
    from concourse.bass_utils import run_bass_kernel_spmd

    w = {k: np.asarray(v) for k, v in inputs.items()}

    def kmajor(m):
        return np.ascontiguousarray(m.reshape(KT, P, -1).transpose(1, 0, 2))

    def ffn(gate, up, down, nt, owner, n_experts):
        mid = gate.shape[1]
        pad = nt * P - mid
        gate, up = (np.concatenate([m, np.zeros((HID, pad), m.dtype)], 1) for m in (gate, up))
        down = np.concatenate([down, np.zeros((pad, HID), down.dtype)], 0)
        sel = np.zeros((P, nt * P), np.float32)
        sel[owner, np.arange(mid)] = 1.0
        sel[n_experts + owner, np.arange(mid)] = 1.0
        packed = np.zeros((nt, P, WTS), gate.dtype)
        gu = np.stack([gate, up]).reshape(2, KT, P, nt, P)
        packed[:, :, :2 * KT * P] = gu.transpose(3, 2, 0, 1, 4).reshape(nt, P, 2 * KT * P)
        packed[:, :, 2 * KT * P:WT] = down.reshape(nt, P, HID)
        packed[:, :, WT:] = sel.reshape(P, nt, P).transpose(1, 0, 2)
        return packed

    a = {"x": w["L0_attn_hidden_states"].reshape(TOKENS, HID), "ident": np.eye(P, dtype=np.float32)}
    a["wqkv0"] = kmajor(np.concatenate([w["L0_attn_Wq"], w["L0_attn_Wk"], w["L0_attn_Wv"]], 0).T)
    a["bias0"] = np.concatenate([w["L0_attn_bq"], w["L0_attn_bk"], w["L0_attn_bv"]])
    a["wr0"] = kmajor(w["L0_ffn_wg"].T)
    a["wo0"], a["bo0"] = kmajor(w["L0_attn_Wo"].T), w["L0_attn_bo"]
    a["wo1"], a["bo1"] = kmajor(w["L1_attn_Wo"].T), w["L1_attn_bo"]
    rblk = np.zeros((P, P // D, RF), np.float32)
    for h in range(P // D):
        rblk[h * D:(h + 1) * D, h, :] = w["L0_attn_rand_matrix"].T
    a["rblk"] = rblk.reshape(P, P // D * RF)
    inv_freq = (1.0 / 10000.0 ** (np.arange(0, D, 2, dtype=np.float32) / np.float32(D))).astype(np.float32)
    angle = (np.arange(SEQ, dtype=np.float32)[:, None] * inv_freq[None, :]).reshape(POS_TILES, P, RF).transpose(1, 0, 2)
    a["cos"] = np.concatenate([np.cos(angle), np.cos(angle)], -1).astype(np.float32)
    a["sin"] = np.concatenate([-np.sin(angle), np.sin(angle)], -1).astype(np.float32)
    w1, w2 = w["L0_ffn_w1"], w["L0_ffn_w2"]
    a["ffn0"] = ffn(w1[:, :, :MID].transpose(1, 0, 2).reshape(HID, E0 * MID), w1[:, :, MID:].transpose(1, 0, 2).reshape(HID, E0 * MID),
                    w2.reshape(E0 * MID, HID), NT0, np.repeat(np.arange(E0), MID), E0)
    gu, sgu = w["L1_ffn_expert_gate_up"], w["L1_ffn_shared_gate_up"]
    gate = np.concatenate([gu[:, :MID].reshape(E1 * MID, HID), sgu[:SHARED]], 0).T
    up = np.concatenate([gu[:, MID:].reshape(E1 * MID, HID), sgu[SHARED:]], 0).T
    down = np.concatenate([w["L1_ffn_expert_down"].transpose(0, 2, 1).reshape(E1 * MID, HID), w["L1_ffn_shared_down"].T], 0)
    owner = np.concatenate([np.repeat(np.arange(E1), MID), np.full(SHARED, E1)])
    a["ffn1"] = ffn(gate, up, down, NT1, owner, E1 + 1)
    a["wqkvr1"] = kmajor(np.concatenate([w["L1_attn_Wq"], w["L1_attn_Wk"], w["L1_attn_Wv"], w["L1_ffn_gate_w"],
                                         w["L1_ffn_shared_gate_vec"], np.zeros((1, HID), np.float32)], 0).T)
    a["bias_qk1"] = np.concatenate([w["L1_attn_bq"], w["L1_attn_bk"]]).reshape(QK_TILES, P).T
    a["bias_v1"] = w["L1_attn_bv"]
    a = {k: np.ascontiguousarray(v) for k, v in a.items()}

    nc = bacc.Bacc("TRN2", target_bir_lowering=False, num_devices=1)
    aps = {k: nc.dram_tensor(f"in_{k}", v.shape, mybir.dt.from_np(v.dtype), kind="ExternalInput").ap() for k, v in a.items()}
    out = nc.dram_tensor("out_0", (BATCH, SEQ, HID), F32, kind="ExternalOutput").ap()
    build(nc, aps, out)
    r = run_bass_kernel_spmd(nc, [{f"in_{k}": v for k, v in a.items()}], core_ids=[0])
    return r.results[0]["out_0"]
```
